# Optimizing a Trainium2 kernel written in Bass

```python
import numpy as np
import jax
import jax.numpy as jnp

def _softmax(x, axis=-1):
    return jax.nn.softmax(x, axis=axis)

def _gelu(x):
    return jax.nn.gelu(x, approximate=True)

def _silu(x):
    return jax.nn.silu(x)

def _sigmoid(x):
    return jax.nn.sigmoid(x)

def _layernorm(x, axis=-1, eps=1e-05):
    m = jnp.mean(x, axis=axis, keepdims=True)
    v = jnp.var(x, axis=axis, keepdims=True)
    return (x - m) / jnp.sqrt(v + eps)

def _scatter_add(tgt, idx, src, axis=0):
    return tgt.at[idx].add(src)

def _segment_sum(src, seg, n):
    return jax.ops.segment_sum(src, seg, n)
kernel_name = 'mk_adaln_ffn_d2_seqx_r8_230b3b'

def setup_inputs(seed: int=0):
    np.random.seed(seed)
    _w = jnp.asarray

    def _rec_inputs():
        import jax
        import jax.numpy as jnp
        _rk = jax.random.key(seed)
        x = -0.0003929 + 0.9999 * jax.random.normal(jax.random.fold_in(_rk, 1), (8, 256, 128), jnp.float32)
        _lenS = 256 - jax.random.randint(jax.random.fold_in(_rk, 7), (8,), 0, max(1, 256 // 4) + 1, jnp.int32)
        _lenS2 = 256 - jax.random.randint(jax.random.fold_in(_rk, 8), (8,), 0, max(1, 256 // 4) + 1, jnp.int32)
        itok_B_0_2 = jax.random.randint(jax.random.fold_in(_rk, 11), (8,), 0, 3, jnp.int32)
        itok_B_0_8 = jax.random.randint(jax.random.fold_in(_rk, 12), (8,), 0, 9, jnp.int32)
        return (x, itok_B_0_2, itok_B_0_8)
    x, itok_B_0_2, itok_B_0_8 = _rec_inputs()

    def _L0_cond_setup():
        import jax, jax.numpy as jnp
        import numpy as np
        NEG_INF = -1e+30
        key = jax.random.key(seed)
        k1, k2, k3, k4, k5 = jax.random.split(key, 5)
        B, S, D, A = (16, 128, 128, 32)
        hidden = jax.random.normal(k1, (B, S, D), dtype=jnp.float32)
        W1 = jax.random.normal(k2, (D, A), dtype=jnp.float32) / np.sqrt(D)
        b1 = jax.random.normal(k3, (A,), dtype=jnp.float32) * 0.01
        v = jax.random.normal(k4, (A,), dtype=jnp.float32) / np.sqrt(A)
        prompt_type_ids = jax.random.randint(k5, (B,), 0, 3, dtype=jnp.int32)
        return {'hidden': hidden, 'W1': W1, 'b1': b1, 'v': v, 'prompt_type_ids': prompt_type_ids}
    _L0_cond_all = _L0_cond_setup()
    _L0_cond_in = {k: v for k, v in _L0_cond_all.items() if k in ('W1', 'b1', 'v')}
    del _L0_cond_all

    def _L0_ffn_setup():
        import jax, jax.numpy as jnp
        import numpy as np
        B, L, D = (4, 128, 128)
        E, H = (8, 512)
        CAPACITY = 6
        key = jax.random.key(seed)
        ks = jax.random.split(key, 6)
        x = jax.random.normal(ks[0], (B, L, D), dtype=jnp.float32)
        gate_weight = jax.random.normal(ks[1], (E, D), dtype=jnp.float32) * 0.006
        w1 = jax.random.normal(ks[2], (E, H, D), dtype=jnp.float32) * 0.02
        b1 = jnp.zeros((E, H), dtype=jnp.float32)
        w2 = jax.random.normal(ks[3], (E, D, H), dtype=jnp.float32) * 0.02
        b2 = jnp.zeros((E, D), dtype=jnp.float32)
        return {'x': x, 'gate_weight': gate_weight, 'w1': w1, 'b1': b1, 'w2': w2, 'b2': b2}
    _L0_ffn_all = _L0_ffn_setup()
    _L0_ffn_in = {k: v for k, v in _L0_ffn_all.items() if k in ('gate_weight', 'w1', 'b1', 'w2', 'b2')}
    del _L0_ffn_all

    def _L1_cond_setup():
        import jax, jax.numpy as jnp
        import numpy as np
        LN_EPS = 1e-05
        key = jax.random.key(seed)
        ks = jax.random.split(key, 8)
        B, S, H, A, L = (32, 256, 128, 32, 10)
        return {'hidden_states': jax.random.normal(ks[0], (B, S, H), dtype=jnp.float32), 'language_ids': jax.random.randint(ks[1], (B,), 0, L, dtype=jnp.int64), 'W1': jax.random.normal(ks[2], (L, H, A), dtype=jnp.float32) * (1.0 / np.sqrt(H)), 'b1': jnp.zeros((L, A), dtype=jnp.float32), 'W2': jax.random.normal(ks[3], (L, A, H), dtype=jnp.float32) * (1.0 / np.sqrt(A)), 'b2': jnp.zeros((L, H), dtype=jnp.float32), 'gamma': jnp.ones((L, H), dtype=jnp.float32), 'beta': jnp.zeros((L, H), dtype=jnp.float32)}
    _L1_cond_all = _L1_cond_setup()
    _L1_cond_in = {k: v for k, v in _L1_cond_all.items() if k in ('W1', 'b1', 'W2', 'b2', 'gamma', 'beta')}
    del _L1_cond_all

    def _L1_ffn_setup():
        import jax, jax.numpy as jnp
        import numpy as np
        B, L, D, H, E, TOP_K = (4, 256, 128, 512, 8, 2)
        LN_EPS = 1e-05
        key = jax.random.key(seed)
        ks = jax.random.split(key, 8)
        x = jax.random.normal(ks[0], (B, L, D), dtype=jnp.float32)
        gate_w = jax.random.normal(ks[1], (D, E), dtype=jnp.float32) / np.sqrt(D)
        w1 = jax.random.normal(ks[2], (E, D, H), dtype=jnp.float32) / np.sqrt(D)
        b1 = jnp.zeros((E, H), dtype=jnp.float32)
        w2 = jax.random.normal(ks[3], (E, H, D), dtype=jnp.float32) / np.sqrt(H)
        b2 = jnp.zeros((E, D), dtype=jnp.float32)
        gamma = jnp.ones((D,), dtype=jnp.float32)
        beta = jnp.zeros((D,), dtype=jnp.float32)
        return {'x': x, 'gate_w': gate_w, 'w1': w1, 'b1': b1, 'w2': w2, 'b2': b2, 'gamma': gamma, 'beta': beta}
    _L1_ffn_all = _L1_ffn_setup()
    _L1_ffn_in = {k: v for k, v in _L1_ffn_all.items() if k in ('gate_w', 'w1', 'b1', 'w2', 'b2', 'gamma', 'beta')}
    del _L1_ffn_all
    return {'x': x, 'itok_B_0_2': itok_B_0_2, 'itok_B_0_8': itok_B_0_8, 'L0_cond_W1': _L0_cond_in['W1'], 'L0_cond_b1': _L0_cond_in['b1'], 'L0_cond_v': _L0_cond_in['v'], 'L0_ffn_gate_weight': _L0_ffn_in['gate_weight'], 'L0_ffn_w1': _L0_ffn_in['w1'], 'L0_ffn_b1': _L0_ffn_in['b1'], 'L0_ffn_w2': _L0_ffn_in['w2'], 'L0_ffn_b2': _L0_ffn_in['b2'], 'L1_cond_W1': _L1_cond_in['W1'], 'L1_cond_b1': _L1_cond_in['b1'], 'L1_cond_W2': _L1_cond_in['W2'], 'L1_cond_b2': _L1_cond_in['b2'], 'L1_cond_gamma': _L1_cond_in['gamma'], 'L1_cond_beta': _L1_cond_in['beta'], 'L1_ffn_gate_w': _L1_ffn_in['gate_w'], 'L1_ffn_w1': _L1_ffn_in['w1'], 'L1_ffn_b1': _L1_ffn_in['b1'], 'L1_ffn_w2': _L1_ffn_in['w2'], 'L1_ffn_b2': _L1_ffn_in['b2'], 'L1_ffn_gamma': _L1_ffn_in['gamma'], 'L1_ffn_beta': _L1_ffn_in['beta']}

def reference(x, itok_B_0_2, itok_B_0_8, L0_cond_W1, L0_cond_b1, L0_cond_v, L0_ffn_gate_weight, L0_ffn_w1, L0_ffn_b1, L0_ffn_w2, L0_ffn_b2, L1_cond_W1, L1_cond_b1, L1_cond_W2, L1_cond_b2, L1_cond_gamma, L1_cond_beta, L1_ffn_gate_w, L1_ffn_w1, L1_ffn_b1, L1_ffn_w2, L1_ffn_b2, L1_ffn_gamma, L1_ffn_beta):
    import jax
    import jax.numpy as jnp

    def _L0_cond_ref(hidden, W1, b1, v, prompt_type_ids):
        import jax, jax.numpy as jnp
        import numpy as np
        NEG_INF = -1e+30
        B, S, D = hidden.shape
        attn_in = jnp.tanh(jnp.einsum('bsd,da->bsa', hidden, W1) + b1)
        scores = jnp.einsum('bsa,a->bs', attn_in, v)
        idx = jnp.arange(S)
        j = idx[:, None]
        l = idx[None, :]
        prefix_m = l <= j
        postfix_m = l >= j
        cloze_m = l != j
        pt = prompt_type_ids[:, None, None]
        mask = jnp.where(pt == 0, prefix_m[None], jnp.where(pt == 1, postfix_m[None], cloze_m[None]))
        masked_scores = jnp.where(mask, scores[:, None, :], NEG_INF)
        p = jax.nn.softmax(masked_scores, axis=-1)
        cnt = jnp.sum(mask, axis=-1).astype(hidden.dtype)
        pooled = jnp.einsum('bjl,bld->bjd', p, hidden) / cnt[..., None]
        return pooled

    def _L0_ffn_ref(x, gate_weight, w1, b1, w2, b2):
        import jax, jax.numpy as jnp
        import numpy as np
        B, L, D = (4, 128, 128)
        E, H = (8, 512)
        CAPACITY = 6
        logits = jnp.einsum('bld,ed->ble', x, gate_weight)
        expert_k = B * L * CAPACITY
        kth_val = jnp.sort(logits.reshape(-1))[expert_k - 1]
        mask = (logits >= kth_val).astype(x.dtype)
        gates = logits * mask
        h = jax.nn.gelu(jnp.einsum('bld,ehd->bleh', x, w1) + b1, approximate=True)
        y = jnp.einsum('bleh,edh->blde', h, w2) + b2.T[None, None]
        out = jnp.einsum('blde,ble->bld', y, gates)
        return out

    def _L1_cond_ref(hidden_states, language_ids, W1, b1, W2, b2, gamma, beta):
        import jax, jax.numpy as jnp
        import numpy as np
        LN_EPS = 1e-05
        w1 = W1[language_ids]
        w2 = W2[language_ids]
        h = jnp.einsum('bsh,bha->bsa', hidden_states, w1) + b1[language_ids][:, None, :]
        h = jax.nn.relu(h)
        adapted = jnp.einsum('bsa,bah->bsh', h, w2) + b2[language_ids][:, None, :]
        x = hidden_states + adapted
        mean = jnp.mean(x, axis=-1, keepdims=True)
        var = jnp.mean(jnp.square(x - mean), axis=-1, keepdims=True)
        normed = (x - mean) * jax.lax.rsqrt(var + LN_EPS)
        return normed * gamma[language_ids][:, None, :] + beta[language_ids][:, None, :]

    def _L1_ffn_ref(x, gate_w, w1, b1, w2, b2, gamma, beta):
        import jax, jax.numpy as jnp
        import numpy as np
        B, L, D, H, E, TOP_K = (4, 256, 128, 512, 8, 2)
        LN_EPS = 1e-05
        residual = x
        mu = jnp.mean(x, axis=-1, keepdims=True)
        var = jnp.mean(jnp.square(x - mu), axis=-1, keepdims=True)
        xn = (x - mu) * jax.lax.rsqrt(var + LN_EPS) * gamma + beta
        probs = jax.nn.softmax(jnp.einsum('bld,de->ble', xn, gate_w), axis=-1)
        w, idx = jax.lax.top_k(probs, TOP_K)
        w = w / jnp.sum(w, axis=-1, keepdims=True)
        cw = jnp.sum(w[..., None] * jax.nn.one_hot(idx, E, dtype=x.dtype), axis=2)
        h = jax.nn.gelu(jnp.einsum('bld,edh->eblh', xn, w1) + b1[:, None, None, :], approximate=False)
        out_e = jnp.einsum('eblh,ehd->ebld', h, w2) + b2[:, None, None, :]
        output = jnp.einsum('ble,ebld->bld', cw, out_e)
        return output + residual
    x = x + _L0_ffn_ref(_L0_cond_ref(x, L0_cond_W1, L0_cond_b1, L0_cond_v, itok_B_0_2), L0_ffn_gate_weight, L0_ffn_w1, L0_ffn_b1, L0_ffn_w2, L0_ffn_b2)
    x = x + _L1_ffn_ref(_L1_cond_ref(x, itok_B_0_8, L1_cond_W1, L1_cond_b1, L1_cond_W2, L1_cond_b2, L1_cond_gamma, L1_cond_beta), L1_ffn_gate_w, L1_ffn_w1, L1_ffn_b1, L1_ffn_w2, L1_ffn_b2, L1_ffn_gamma, L1_ffn_beta)
    return x

_drawn_inputs = setup_inputs


def setup_inputs(seed=0):
    import zlib

    import numpy as np

    out = dict(_drawn_inputs(seed))
    spreads = {'L0_ffn_b1': (0.0, 0.8),
     'L0_ffn_b2': (0.0, 0.8),
     'L1_cond_b1': (0.0, 0.1),
     'L1_cond_b2': (0.0, 0.1),
     'L1_cond_gamma': (1.0, 0.2),
     'L1_cond_beta': (0.0, 0.1),
     'L1_ffn_b1': (0.0, 0.308),
     'L1_ffn_b2': (0.0, 0.1),
     'L1_ffn_gamma': (1.0, 0.2),
     'L1_ffn_beta': (0.0, 0.1)}
    factors = {'L0_cond_W1': 8.0,
     'L0_cond_b1': 162.233,
     'L0_cond_v': 8.0,
     'L0_ffn_gate_weight': 8.0,
     'L0_ffn_w1': 8.0,
     'L0_ffn_w2': 8.0}
    for name, (base, spread) in spreads.items():
        noise = np.random.default_rng([zlib.crc32(name.encode()), seed]).standard_normal(out[name].shape)
        drawn = base * np.exp(spread * noise) if base else spread * noise
        out[name] = jnp.asarray(drawn.astype(out[name].dtype))
    for name, factor in factors.items():
        out[name] = (out[name] * factor).astype(out[name].dtype)
    return out
```

```python
import numpy as np
import concourse.bass as bass
from concourse import mybir
from contextlib import ExitStack

F32 = mybir.dt.float32
F32R = mybir.dt.float32r
BF16 = mybir.dt.bfloat16
I32 = mybir.dt.int32
U32 = mybir.dt.uint32
ACT = mybir.ActivationFunctionType
ALU = mybir.AluOpType
AX = mybir.AxisListType

B, S, D, E, H, A = 8, 256, 128, 8, 512, 32
N = B * S
NT = N // 128
NG = 4
LANGS = 10
KTH = 4 * 128 * 6
BIG = 1.0e30
EPS = 1e-5

LAG = 3
NH = 5
NW = 4
NTMP = 3
NGS = 8
ND = 11


def step_order():
    out = []
    for e in range(6):
        out += [(0, e, g) for g in range(NG)]
    out += [(0, e, g) for g in range(NG) for e in (6, 7)]
    out += [(1, e, g) for g in range(NG) for e in (0, 1)]
    for e in range(2, 8):
        out += [(1, e, g) for g in range(NG)]
    return out


def build_adaln_ffn(nc, t, out):
    STEPS = step_order()
    NS = len(STEPS)
    NU = 4 * NS
    with ExitStack() as ctx:
        def sb(name, shape, dt=F32):
            return ctx.enter_context(nc.sbuf_tensor(name, shape, dt))

        def sem(name):
            return ctx.enter_context(nc.semaphore(name))

        scr = [nc.dram_tensor(f"gates{i}", [NT, E, 128], F32, kind="Internal").ap() for i in range(2)]

        acc = sb("acc", [128, N])
        first = sb("first", [128, max(ND * 512, N + NT * (D + 1) + 6 * S)])
        ysv = first[:, 0:ND * 512].rearrange("p (s n) -> p s n", n=512)
        attn = first[0:A, 0:N]
        xtm = first[:, N:N + NT * (D + 1)].rearrange("p (t d) -> p t d", t=NT)
        ET = first[:, N + NT * (D + 1):N + NT * (D + 1) + 6 * S].rearrange("p (k s) -> p k s", k=3)
        ident = sb("ident", [128, 128])
        identb = sb("identb", [128, 128], BF16)
        gTb = sb("gTb", [E, N])
        sel = gTb[:, 0:B * 128]
        onesb = sb("onesb", [128, 128], BF16)
        mg = sb("mg", [128, B * 257])
        maskt = mg[:, :].bitcast(BF16).rearrange("p (b n) -> p b n", b=B)
        gbc = mg[:, 0:B * 2 * D].rearrange("p (b n) -> p b n", b=B)
        w1c = sb("w1c", [D, A])
        b1c = sb("b1c", [A, 1])
        vc = sb("vc", [A, 1])
        vz = sb("vz", [A, 2 * B - 1])
        ty = sb("ty", [B, 1], I32)
        lid = sb("lid", [1, B], I32)
        tyr = sb("tyr", [1, B], I32)
        is_t = sb("is_t", [B, 4])
        rows = sb("rows", [B, S])
        pre = sb("pre", [B, S + 2])
        suf = sb("suf", [B, S + 2])
        cl = sb("cl", [B, S])
        mrow = sb("mrow", [B, 2, S])
        scol = sb("scol", [128, NT])
        rr = sb("rr", [128, 2, 2, 2])
        ptm = sb("ptm", [128, 2, 2 * D])
        pT = sb("pT", [128, 2, 2 * D])
        gw0 = sb("gw0", [D, E])
        gw1 = sb("gw1", [D, E])
        L32 = sb("L32", [128, NT * E])
        L2 = sb("L2", [128, NT * E])
        junk = sb("junk", [128, 3, NT * E], BF16)
        G0 = sb("G0", [128, NT * E])
        cnt3 = sb("cnt3", [128, 2, 4], BF16)
        bis = sb("bis", [128, 8])
        bisj = sb("bisj", [128, 4])
        inc_i = sb("inc_i", [128, 1], I32)
        cur_i = sb("cur_i", [128, 2], I32)
        cand = sb("cand", [128, 4], I32)
        bitc = sb("bitc", [128, 16 * 3], I32)
        gT0 = sb("gT0", [128, 128])
        b1f = [sb(f"b1f{i}", [128, 4 * E]) for i in range(2)]
        b2f = [sb(f"b2f{i}", [E, D]) for i in range(2)]
        xh = sb("xh", [128, 2, N // 2], F32R)
        xl = sb("xl", [128, 2, N // 2], F32R)
        xh1 = sb("xh1", [128, N], F32R)
        xl1 = sb("xl1", [128, N], F32R)
        wraw = sb("wraw", [128, 2, 1024])
        wh = sb("wh", [128, NW, 1024], F32R)
        wl = sb("wl", [128, NW, 1024], F32R)
        h32 = sb("h32", [128, NH, 512])
        hh = sb("hh", [128, NH, 512], F32R)
        hl = sb("hl", [128, NH, 512], F32R)
        Gs = sb("Gs", [128, NGS, 512])
        tmp = sb("tmp", [128, NTMP, 512])
        cw1 = sb("cw1", [D, B, A])
        cb1 = sb("cb1", [A, B])
        cw2 = sb("cw2", [A + 1, B, D])
        fgb = sb("fgb", [D, 2])
        hTs = sb("hTs", [A + 1, 512])
        st = sb("st", [128, 4, 6])
        mv = sb("mv", [128, 2, 4, 2])
        rs = sb("rs", [128, 2, 4])
        mhalf = sb("mhalf", [128, 4])
        ebase = sb("ebase", [128, 32])
        n1 = sb("n1", [128, 4 * D])
        x2 = sb("x2", [128, 4 * D])
        n2 = sb("n2", [128, 4 * D])
        xn32 = sb("xn32", [128, 512])
        lg = sb("lg", [128, 4, E])
        ex = sb("ex", [128, 4, E])
        pr = sb("pr", [128, 4, E])
        c4 = sb("c4", [128, 4, 4])
        mx8 = sb("mx8", [128, 4, 8])
        ix8 = sb("ix8", [128, 4, 8], U32)
        ixf = sb("ixf", [128, 4, 8])
        iota8 = sb("iota8", [128, E])
        oh = sb("oh", [128, 4, E])
        cw = sb("cw", [128, 4, E])
        cwT = sb("cwT", [32, 128])

        bank = [ctx.enter_context(nc.psum_tensor(f"bank{i}", [128, 512], F32)) for i in range(8)]

        ld = {}

        def load_sem(name):
            ld[name] = sem("ld_" + name)
            return ld[name]

        s_m1 = sem("s_m1")
        s_g = sem("s_g")
        s_hia = sem("s_hia")
        s_hid = sem("s_hid")
        s_lo = sem("s_lo")
        s_m2 = sem("s_m2")
        s_ysv = sem("s_ysv")
        s_tmp = sem("s_tmp")
        s_acc = sem("s_acc")
        s_w = sem("s_w")
        s_raw = [sem(f"s_raw{i}") for i in range(2)]
        s_G = [sem(f"s_G{i}") for i in range(NGS)]
        s_scr = sem("s_scr0")
        s_scr1 = [sem(f"s_scr1_{g}") for g in range(NG)]
        s_gtb = [sem(f"s_gtb{i}") for i in range(1 + NG)]
        s_out = sem("s_out")
        p_at = sem("p_at")
        p_th = sem("p_th")
        p_sc = sem("p_sc")
        p_v = sem("p_v")
        p_m = sem("p_m")
        p_col = sem("p_col")
        p_pm = sem("p_pm")
        p_ex = sem("p_ex")
        p_po = sem("p_po")
        p_no = sem("p_no")
        p_tr = sem("p_tr")
        p_ev = sem("p_ev")
        p_lg = sem("p_lg")
        p_x = sem("p_x")
        p_one = sem("p_one")
        b_cnt = sem("b_cnt")
        b_sum = sem("b_sum")
        b_upd = sem("b_upd")
        b_g = sem("b_g")
        b_gt = sem("b_gt")
        b_ev = sem("b_ev")
        b_b2 = sem("b_b2")
        m_h = sem("m_h")
        m_hs = sem("m_hs")
        m_xa = sem("m_xa")
        m_mv = sem("m_mv")
        m_rs = sem("m_rs")
        m_n1 = sem("m_n1")
        m_x2 = sem("m_x2")
        m_mv2 = sem("m_mv2")
        m_rs2 = sem("m_rs2")
        m_n2 = sem("m_n2")
        m_x2T = sem("m_x2T")
        m_nT = sem("m_nT")
        m_xn = sem("m_xn")
        m_sp = sem("m_sp")
        m_lg = sem("m_lg")
        m_d = sem("m_d")
        m_e = sem("m_e")
        m_cw = sem("m_cw")
        m_cT = sem("m_cT")
        m_cE = sem("m_cE")
        m_one = sem("m_one")

        chain = {"dve": [sem("c_dve"), 0], "pool": [sem("c_pool"), 0], "act": [sem("c_act"), 0]}

        def link(eng, who, ins):
            c = chain[who]
            c[1] += 1
            ins.then_inc(c[0], 1)
            eng.wait_ge(c[0], c[1])

        Q = {k: [] for k in ("pe", "act", "dve", "pool", "sp")}

        def at(q, pos, fn):
            Q[q].append((pos, len(Q[q]), fn))

        HIA = [u % 2 == 0 or u < 40 for u in range(NU)]
        nha = np.cumsum(HIA).tolist()
        nhd = np.cumsum([not x for x in HIA]).tolist()

        def expert(s):
            return STEPS[s][0] * 8 + STEPS[s][1]

        last_step = {expert(s): s for s in range(NS)}

        terms = []
        for s in range(NS):
            if s >= ND:
                terms.append((4 * s + 4 + LAG + 0.5, "y", s))
            else:
                terms.append((4 * ND + 6 + 2 * s + 0.7, "y", s))
        M0 = [110.0 + 8 * g for g in range(NG)]
        for g in range(NG):
            terms.append((4 * ND + 7 + 3 * g + 0.4, "b2", (0, g)))
            terms.append((M0[g] + 10.4, "x2", g))
            terms.append((M0[g] + 40 + 0.4, "b2", (1, g)))
        terms.sort(key=lambda x: x[0])
        where = {(k, v): i for i, (_, k, v) in enumerate(terms)}
        ys = [i for i, (_, k, _) in enumerate(terms) if k == "y"]
        gslot = {ti: j for j, ti in enumerate(ys)}
        group_terms = {g: 0 for g in range(NG)}

        def group_of(kind, v):
            return STEPS[v][2] if kind == "y" else (v if kind == "x2" else v[1])

        def layer_of(kind, v):
            return STEPS[v][0] if kind == "y" else (1 if kind == "x2" else v[0])

        done0 = {g: max(i for i, (_, k, v) in enumerate(terms) if group_of(k, v) == g and layer_of(k, v) == 0) + 1
                 for g in range(NG)}
        done1 = {g: max(i for i, (_, k, v) in enumerate(terms) if group_of(k, v) == g) + 1 for g in range(NG)}

        misc = []
        for r in range(17):
            misc.append((3.75 + 2 * r, ("bis", r), (b_upd, r + 1)))
        PG = 40.75
        misc.append((PG, ("gT0", 0), (b_ev, 1)))
        for g in range(NG):
            misc.append((4 * ND + 6 + 3 * g + 0.35, ("b2", (0, g)), (s_tmp, where[("b2", (0, g))] + 1)))
            misc.append((M0[g] + 0.75, ("h", g), (m_hs, 2 * g + 2)))
            misc.append((M0[g] + 2.75, ("xa", g), (m_n1, g + 1)))
            misc.append((M0[g] + 10.7, ("x2T", g), (s_tmp, where[("x2", g)] + 1)))
            misc.append((M0[g] + 10.8, ("nT", g), (m_xn, g + 1)))
            misc.append((M0[g] + 13.75, ("lg", g), (m_d, g + 1)))
            misc.append((M0[g] + 18.75, ("cT", g), (m_cE, g + 1)))
            misc.append((M0[g] + 40 + 0.35, ("b2", (1, g)), (s_tmp, where[("b2", (1, g))] + 1)))
        misc.sort(key=lambda x: x[0])
        mb = {key: (6 + i % 2, misc[i - 2][2] if i >= 2 else None) for i, (_, key, _) in enumerate(misc)}
        mpos = {key: pos for pos, key, _ in misc}

        def misc_bank(eng, key):
            i, free = mb[key]
            if free is not None:
                eng.wait_ge(free[0], free[1])
            return bank[i]

        def xparts(s):
            layer, e, g = STEPS[s]
            if layer == 0:
                return (xh[:, g // 2, (g % 2) * 512:(g % 2) * 512 + 512],
                        xl[:, g // 2, (g % 2) * 512:(g % 2) * 512 + 512])
            return xh1[:, g * 512:g * 512 + 512], xl1[:, g * 512:g * 512 + 512]

        def pe_m1(u):
            def fn(pe):
                s, c = u // 4, u % 4
                layer, e, g = STEPS[s]
                k = expert(s)
                if c == 0:
                    pe.wait_ge(s_w, k + 1)
                    if layer == 0:
                        pe.wait_ge(p_x, 2 * g + 2)
                    else:
                        pe.wait_ge(m_sp, g + 1)
                if u >= 4:
                    pe.wait_ge(s_g, u - 3)
                a, b_ = xparts(s)
                w_h = wh[:, k % NW, c * 128:c * 128 + 128]
                w_l = wl[:, k % NW, c * 128:c * 128 + 128]
                o = bank[u % 4][:, :]
                pe.matmul(o, w_h, a, start=True, stop=False)
                pe.matmul(o, w_h, b_, start=False, stop=False)
                pe.matmul(o, w_l, a, start=False, stop=True).then_inc(s_m1, 1)
            return fn

        def pe_m2(u):
            def fn(pe):
                s, c = u // 4, u % 4
                k = expert(s)
                o = bank[4 + s % 2][:, :]
                if c == 0 and s >= 2:
                    if s - 2 < ND:
                        pe.wait_ge(s_ysv, s - 1)
                    else:
                        pe.wait_ge(s_tmp, where[("y", s - 2)] + 1)
                pe.wait_ge(s_lo, u + 1)
                w_h = wh[:, k % NW, 512 + c * 128:640 + c * 128]
                w_l = wl[:, k % NW, 512 + c * 128:640 + c * 128]
                pe.matmul(o, w_h, hh[:, u % NH, :], start=(c == 0), stop=False)
                pe.matmul(o, w_l, hh[:, u % NH, :], start=False, stop=False)
                pe.matmul(o, w_h, hl[:, u % NH, :], start=False, stop=(c == 3)).then_inc(s_m2, 1)
            return fn

        def act_gelu(u):
            def fn(act):
                s, c = u // 4, u % 4
                layer, e, g = STEPS[s]
                act.wait_ge(s_m1, u + 1)
                if u >= NH:
                    act.wait_ge(s_lo, u - NH + 1)
                act.activation(h32[:, u % NH, :], bank[u % 4][:, :],
                               ACT.Gelu if layer else ACT.Gelu_apprx_tanh,
                               bias=b1f[layer][:, e * 4 + c:e * 4 + c + 1]).then_inc(s_g, 1)
            return fn

        def hi_part(q, u):
            def fn(eng):
                eng.wait_ge(s_g, u + 1)
                if u >= NH:
                    eng.wait_ge(s_m2, u - NH + 1)
                if q == "act":
                    eng.activation(hh[:, u % NH, :], h32[:, u % NH, :], ACT.Copy).then_inc(s_hia, 1)
                else:
                    eng.tensor_copy(hh[:, u % NH, :], h32[:, u % NH, :]).then_inc(s_hid, 1)
            return fn

        def lo_part(u):
            def fn(dve):
                if HIA[u]:
                    dve.wait_ge(s_hia, nha[u])
                else:
                    dve.wait_ge(s_hid, nhd[u])
                if u >= NH:
                    dve.wait_ge(s_m2, u - NH + 1)
                dve.tensor_tensor(hl[:, u % NH, :], h32[:, u % NH, :], hh[:, u % NH, :].bitcast(F32),
                                  ALU.subtract).then_inc(s_lo, 1)
            return fn

        for u in range(NU):
            at("pe", u, pe_m1(u))
            at("pe", u + LAG + 0.5, pe_m2(u))
            at("act", u, act_gelu(u))
            if HIA[u]:
                at("act", u + 1.2, hi_part("act", u))
            else:
                at("dve", u, hi_part("dve", u))
            at("dve", u + 1.1, lo_part(u))

        def keep(s):
            def fn(act):
                act.wait_ge(s_m2, 4 * s + 4)
                act.activation(ysv[:, s, :], bank[4 + s % 2][:, :], ACT.Copy).then_inc(s_ysv, 1)
            return fn

        for s in range(ND):
            at("act", 4 * s + 4 + LAG + 0.3, keep(s))

        def term(i, kind, v):
            def fn(dve):
                if i >= NTMP:
                    dve.wait_ge(s_acc, i - NTMP + 1)
                o = tmp[:, i % NTMP, :]
                if kind == "y":
                    j = gslot[i]
                    dve.wait_ge(s_G[j % NGS], 16 * (j // NGS + 1))
                    if v < ND:
                        dve.wait_ge(s_ysv, v + 1)
                        src = ysv[:, v, :]
                    else:
                        dve.wait_ge(s_m2, 4 * v + 4)
                        src = bank[4 + v % 2][:, :]
                    dve.tensor_tensor(o, src, Gs[:, j % NGS, :], ALU.mult).then_inc(s_tmp, 1)
                elif kind == "b2":
                    dve.wait_ge(b_b2, [("b2", x) for _, k, x in terms if k == "b2"].index(("b2", v)) + 1)
                    dve.tensor_copy(o, bank[mb[("b2", v)][0]][:, :]).then_inc(s_tmp, 1)
                else:
                    dve.wait_ge(m_x2T, v + 1)
                    dve.tensor_copy(o, bank[mb[("x2T", v)][0]][:, :]).then_inc(s_tmp, 1)
            return fn

        def add(i, kind, v):
            g = group_of(kind, v)

            def fn(pool):
                pool.wait_ge(s_tmp, i + 1)
                if i:
                    pool.wait_ge(s_acc, i)
                if kind == "x2":
                    pool.wait_ge(m_xa, v + 1)
                a = acc[:, g * 512:g * 512 + 512]
                pool.tensor_tensor(a, a, tmp[:, i % NTMP, :], ALU.add).then_inc(s_acc, 1)
            return fn

        for i, (pos, kind, v) in enumerate(terms):
            at("dve", pos, term(i, kind, v))
            at("pool", pos + 0.5, add(i, kind, v))

        def load_gates(j):
            ti = ys[j]
            s = terms[ti][2]
            layer, e, g = STEPS[s]

            def fn(sp):
                if layer == 0:
                    sp.wait_ge(s_scr, 16)
                else:
                    sp.wait_ge(s_scr1[g], 16)
                if j >= NGS:
                    sp.wait_ge(s_tmp, ys[j - NGS] + 1)
                src = scr[layer][4 * g:4 * g + 4, e:e + 1, :].rearrange("t e p -> e t p")
                sp.dma_start(Gs[:, j % NGS, :].rearrange("q (t p) -> q t p", t=4),
                             src.to_broadcast([128, 4, 128])).then_inc(s_G[j % NGS], 16)
            return fn

        for j, ti in enumerate(ys):
            s = terms[ti][2]
            pos = terms[ys[j - NGS]][0] + 1.5 if j >= NGS else PG + 2
            if STEPS[s][0] == 1:
                pos = max(pos, M0[STEPS[s][2]] + 20.5)
            at("sp", pos, load_gates(j))

        def load_w(k):
            def fn(sp):
                if k >= 2:
                    sp.wait_ge(s_w, k - 1)
                layer, e = k // 8, k % 8
                sp.dma_start(wraw[:, k % 2, 0:512], t[f"w1_{layer}"][:, e, :]).then_inc(s_raw[k % 2], 16)
                sp.dma_start(wraw[:, k % 2, 512:1024], t[f"w2_{layer}"][:, e, :]).then_inc(s_raw[k % 2], 16)
            return fn

        WP = 4

        def split_w(k, p):
            w = 1024 // WP
            sl = slice(p * w, p * w + w)

            def fn(pool):
                if p == 0:
                    pool.wait_ge(s_raw[k % 2], 32 * (k // 2 + 1))
                    if k >= NW:
                        pool.wait_ge(s_m2, 4 * last_step[k - NW] + 4)
                link(pool, "pool", pool.tensor_copy(wh[:, k % NW, sl], wraw[:, k % 2, sl]))
                last = pool.tensor_tensor(wl[:, k % NW, sl], wraw[:, k % 2, sl],
                                          wh[:, k % NW, sl].bitcast(F32), ALU.subtract)
                if p == WP - 1:
                    last.then_inc(s_w, 1)
                else:
                    link(pool, "pool", last)
            return fn

        for k in range(16):
            base = -50.0 + 2 * k if k < NW else 4 * last_step[k - NW] + 4 + LAG + 2
            for p in range(WP):
                at("pool", base + 1.3 * p if k >= NW else base + 0.1 * p, split_w(k, p))
            prev = -60 if k < 2 else (-50.0 + 2 * (k - 2) if k - 2 < NW else 4 * last_step[k - 2 - NW] + 4 + LAG + 2 + 5)
            at("sp", prev + 0.5, load_w(k))

        def sp_loads(sp):
            for g in range(NG):
                sp.dma_start(acc[:, g * 512:g * 512 + 512], t["xT"][:, g * 512:g * 512 + 512]).then_inc(load_sem(f"x{g}"), 16)
                if g == 0:
                    s0 = load_sem("c0")
                    sp.dma_start(w1c[:, :], t["w1c"]).then_inc(s0, 16)
                    sp.dma_start(b1c[:, :], t["b1c"]).then_inc(s0, 16)
                    sp.dma_start(vc[:, :], t["vc"]).then_inc(s0, 16)
            s0 = load_sem("ids")
            sp.dma_start(tyr[:, :], t["itype"].rearrange("(a n) -> a n", a=1)).then_inc(s0, 16)
            sp.dma_start(lid[:, :], t["ilang"].rearrange("(a n) -> a n", a=1)).then_inc(s0, 16)
            sp.dma_start(ty[:, :], t["itype"].rearrange("(n a) -> n a", a=1)).then_inc(load_sem("ty"), 16)
            sp.dma_start(sel[:, :], t["sel"]).then_inc(load_sem("sel"), 16)
            sp.dma_start(identb[:, :], t["identb"]).then_inc(load_sem("identb"), 16)
            sp.wait_ge(s0, 32)
            for b in range(B):
                r = sp.value_load(tyr[0:1, b:b + 1], min_val=0, max_val=2)
                sp.dma_start(maskt[:, b, :], t["maskt"][bass.ds(r, 1), :, :].rearrange("a p c -> p (a c)"))\
                    .then_inc(load_sem(f"mask{b}"), 16)
            sp.dma_start(xtm[:, :, 0:D], t["xtm"]).then_inc(load_sem("xtm"), 16)
            sp.dma_start(ident[:, :], t["ident"]).then_inc(load_sem("ident"), 16)
            sp.dma_start(gw0[:, :], t["gw0"]).then_inc(load_sem("gw0"), 16)
            sp.dma_start(b1f[0][:, :], t["b1_0"]).then_inc(load_sem("b1f0"), 16)
            sp.dma_start(bitc[:, :], t["bitc"]).then_inc(load_sem("bitc"), 16)

        at("sp", -100, sp_loads)

        def sp_later(sp):
            sp.dma_start(b2f[0][:, :], t["b2_0"]).then_inc(load_sem("b2f0"), 16)
            sp.dma_start(b2f[1][:, :], t["b2_1"]).then_inc(load_sem("b2f1"), 16)
            sp.dma_start(b1f[1][:, :], t["b1_1"]).then_inc(load_sem("b1f1"), 16)
            sp.dma_start(gw1[:, :], t["gw1"]).then_inc(load_sem("gw1"), 16)
            sp.dma_start(fgb[:, :], t["fgb"]).then_inc(load_sem("fgb"), 16)
            sp.dma_start(iota8[:, :], t["iota8"]).then_inc(load_sem("iota8"), 16)
            s0 = load_sem("lang")
            sp.wait_ge(p_no, B)
            for b in range(B):
                r = sp.value_load(lid[0:1, b:b + 1], min_val=0, max_val=LANGS - 1)
                sp.dma_start(cw1[:, b, :], t["cw1"][bass.ds(r, 1), :, :].rearrange("a p c -> p (a c)")).then_inc(s0, 16)
                sp.dma_start(cb1[:, b:b + 1], t["cb1"][bass.ds(r, 1), :].rearrange("a p -> p a")).then_inc(s0, 16)
                sp.dma_start(cw2[:, b, :], t["cw2"][bass.ds(r, 1), :, :].rearrange("a p c -> p (a c)")).then_inc(s0, 16)
                sp.dma_start(gbc[:, b, :], t["gbc"][bass.ds(r, 1), :].to_broadcast([128, 2 * D])).then_inc(s0, 16)

        at("sp", 2, sp_later)

        def pe_prologue(pe):
            pe.wait_ge(ld["c0"], 48)
            for g in range(NG):
                pe.wait_ge(ld[f"x{g}"], 16)
                pe.matmul(bank[g][0:A, :], w1c[:, :], acc[:, g * 512:g * 512 + 512], start=True, stop=True).then_inc(p_at, 1)
            pe.wait_ge(p_v, 1)
            for b in range(B):
                pe.wait_ge(p_th, b // 2 + 1)
                last = pe.matmul(bank[4][0:B, 0:S], vz[:, B - 1 - b:2 * B - 1 - b], attn[:, b * S:b * S + S],
                                 start=(b == 0), stop=(b == B - 1))
            last.then_inc(p_sc, 1)
            for i in range(NT):
                last = pe.matmul(bank[5][:, i:i + 1], attn[:, i * 128:i * 128 + 128], vc[:, :], start=True, stop=True)
            last.then_inc(p_sc, 1)

            def pm(b):
                if b == 0:
                    pe.wait_ge(p_m, 1)
                    pe.wait_ge(ld["sel"], 16)
                    pe.wait_ge(ld["identb"], 16)
                pe.wait_ge(ld[f"mask{b}"], 16)
                if b >= 2:
                    pe.wait_ge(p_ex, 2 * (b - 1))
                o = bank[b % 2][:, :]
                pe.matmul(o, sel[:, b * 128:b * 128 + 128], mrow[:, :, :].rearrange("b c s -> b (c s)"),
                          start=True, stop=False)
                pe.matmul(o, identb[:, :], maskt[:, b, 0:512], start=False, stop=True).then_inc(p_pm, 1)

            def pooled(b):
                if b == 0:
                    pe.wait_ge(ld["xtm"], 16)
                    pe.wait_ge(p_one, 1)
                pe.wait_ge(p_ex, 2 * b + 2)
                if b >= 2:
                    pe.wait_ge(p_no, b - 1)
                for j in range(2):
                    for l in range(2):
                        last = pe.matmul(bank[2 + b % 2][:, j * 256:j * 256 + D + 1],
                                         ET[:, b % 3, l * S + j * 128:l * S + j * 128 + 128],
                                         xtm[:, 2 * b + l, :], start=(l == 0), stop=(l == 1))
                last.then_inc(p_po, 1)

            def trans(b):
                if b == 0:
                    pe.wait_ge(ld["ident"], 16)
                    pe.wait_ge(p_m, 1)
                    pe.wait_ge(p_col, 1)
                pe.wait_ge(p_no, b + 1)
                if b >= 2:
                    pe.wait_ge(p_ev, b - 1)
                for j in range(2):
                    last = pe.transpose(bank[4 + b % 2][:, j * 128:j * 128 + 128],
                                        ptm[:, b % 2, j * 128:j * 128 + 128], ident[:, :])
                last.then_inc(p_tr, 1)

            def logit(b):
                if b == 0:
                    pe.wait_ge(ld["gw0"], 16)
                pe.wait_ge(p_ev, b + 1)
                for j in range(2):
                    i = 2 * b + j
                    last = pe.matmul(bank[7][:, i * E:i * E + E], pT[:, b % 2, j * 128:j * 128 + 128], gw0[:, :],
                                     start=True, stop=True)
                last.then_inc(p_lg, 1)

            for i in range(B + 4):
                if i < B:
                    pm(i)
                if 0 <= i - 1 < B:
                    pooled(i - 1)
                if 0 <= i - 2 < B:
                    trans(i - 2)
                if 0 <= i - 3 < B:
                    logit(i - 3)

        at("pe", -100, pe_prologue)

        def act_prologue(act):
            act.wait_ge(ld["c0"], 48)
            for g in range(NG):
                act.wait_ge(p_at, g + 1)
                act.activation(attn[:, g * 512:g * 512 + 512], bank[g][0:A, :], ACT.Tanh, bias=b1c[:, :]).then_inc(p_th, 1)
            act.wait_ge(p_col, 1)
            for i in range(B + 2):
                if i < B:
                    act.wait_ge(p_pm, i + 1)
                    if i >= 3:
                        act.wait_ge(p_po, i - 2)
                    for l in range(2):
                        act.activation(ET[:, i % 3, l * S:l * S + S], bank[i % 2][:, l * S:l * S + S], ACT.Exp,
                                       bias=scol[:, 2 * i + l:2 * i + l + 1], scale=-1.0).then_inc(p_ex, 1)
                b = i - 2
                if b >= 0:
                    act.wait_ge(p_tr, b + 1)
                    if b >= 2:
                        act.wait_ge(p_lg, b - 1)
                        act.wait_ge(p_x, b - 1)
                    act.activation(pT[:, b % 2, :], bank[4 + b % 2][:, 0:256], ACT.Copy).then_inc(p_ev, 1)
            act.wait_ge(ld["b1f0"], 16)

        at("act", -100, act_prologue)

        def dve_prologue(dve):
            def ln(ins):
                link(dve, "dve", ins)
            dve.memset(onesb[:, :], 1.0).then_inc(p_one, 1)
            ln(dve.memset(vz[:, :], 0.0))
            dve.memset(xtm[:, :, D:D + 1], 1.0).then_inc(p_one, 1)
            dve.wait_ge(ld["c0"], 48)
            dve.tensor_copy(vz[:, B - 1:B], vc[:, :]).then_inc(p_v, 1)
            dve.memset(pre[:, 0:1], -BIG)
            dve.memset(suf[:, S + 1:S + 2], -BIG)
            dve.wait_ge(ld["ty"], 16)
            dve.tensor_scalar(is_t[:, 0:1], ty[:, :], 0.0, None, ALU.is_equal)
            ln(dve.tensor_scalar(is_t[:, 1:2], ty[:, :], 1.0, None, ALU.is_equal))
            ln(dve.tensor_tensor(is_t[:, 3:4], is_t[:, 0:1], is_t[:, 1:2], ALU.add))
            ln(dve.tensor_scalar(is_t[:, 2:3], is_t[:, 3:4], -1.0, 1.0, ALU.mult, ALU.add))
            dve.wait_ge(p_sc, 1)
            ln(dve.tensor_copy(rows[:, :], bank[4][0:B, 0:S]))
            ln(dve.tensor_tensor_scan(pre[:, 1:S + 1], rows[:, :], rows[:, :], -BIG, ALU.max, ALU.max))
            ln(dve.tensor_tensor_scan(suf[:, S:0:-1], rows[:, ::-1], rows[:, ::-1], -BIG, ALU.max, ALU.max))
            dve.wait_ge(p_sc, 2)
            dve.tensor_copy(scol[:, :], bank[5][:, 0:NT]).then_inc(p_col, 1)
            ln(dve.tensor_tensor(cl[:, :], pre[:, 0:S], suf[:, 2:S + 2], ALU.max))
            ln(dve.tensor_scalar(cl[:, :], cl[:, :], is_t[:, 2:3], None, ALU.mult))
            ln(dve.scalar_tensor_tensor(cl[:, :], pre[:, 1:S + 1], is_t[:, 0:1], cl[:, :], ALU.mult, ALU.add))
            ln(dve.scalar_tensor_tensor(mrow[:, 0, :], suf[:, 1:S + 1], is_t[:, 1:2], cl[:, :], ALU.mult, ALU.add))
            dve.tensor_copy(mrow[:, 1, :], mrow[:, 0, :]).then_inc(p_m, 1)
            for b in range(B + 1):
                if b < B:
                    pb = bank[2 + b % 2]
                    dve.wait_ge(p_po, b + 1)
                    if b >= 2:
                        dve.wait_ge(p_tr, b - 1)
                    ln(dve.tensor_tensor(rr[:, b % 2, 0, :], pb[:, D:512:256], maskt[:, b, 512:514], ALU.mult))
                    ln(dve.reciprocal(rr[:, b % 2, 1, :], rr[:, b % 2, 0, :]))
                    for j in range(2):
                        last = dve.tensor_scalar(ptm[:, b % 2, j * 128:j * 128 + 128], pb[:, j * 256:j * 256 + D],
                                                 rr[:, b % 2, 1, j:j + 1], None, ALU.mult)
                    last.then_inc(p_no, 1)
                if b >= 1:
                    c = b - 1
                    dve.wait_ge(p_ev, c + 1)
                    o_h = xh[:, c // 4, (c % 4) * S:(c % 4) * S + S]
                    o_l = xl[:, c // 4, (c % 4) * S:(c % 4) * S + S]
                    ln(dve.tensor_copy(o_h, pT[:, c % 2, :]))
                    dve.tensor_tensor(o_l, pT[:, c % 2, :], o_h.bitcast(F32), ALU.subtract).then_inc(p_x, 1)
            dve.wait_ge(p_lg, B)
            ln(dve.tensor_copy(L32[:, :], bank[7][:, 0:128]))

        at("dve", -100, dve_prologue)

        NALL = N * E
        T_POS = NALL - KTH + 1

        def bis_count(r):
            def fn(dve):
                def ln(ins):
                    link(dve, "dve", ins)
                if r == 0:
                    dve.wait_ge(ld["bitc"], 16)
                    dve.tensor_scalar(junk[:, 0, :], L32[:, :], 0.0, None, ALU.is_ge, ALU.add, accum_out=cnt3[:, 0, 0:1])\
                        .then_inc(b_cnt, 1)
                    return
                dve.wait_ge(b_upd, r)
                for i in range(3 if r > 1 else 1):
                    last = dve.tensor_scalar(junk[:, i, :], L2[:, :], cand[:, i:i + 1].bitcast(F32), None, ALU.is_ge,
                                             ALU.add, accum_out=cnt3[:, r % 2, i:i + 1])
                last.then_inc(b_cnt, 1)
            return fn

        def bis_sum(r):
            def fn(pe):
                o = misc_bank(pe, ("bis", r))
                if r == 0:
                    pe.wait_ge(p_one, 1)
                pe.wait_ge(b_cnt, r + 1)
                n = 3 if r > 1 else 1
                pe.matmul(o[:, 0:n], onesb[:, :], cnt3[:, r % 2, 0:n], start=True, stop=True).then_inc(b_sum, 1)
            return fn

        def bis_update(r):
            def fn(dve):
                def ln(ins):
                    link(dve, "dve", ins)
                o = bank[mb[("bis", r)][0]]
                dve.wait_ge(b_sum, r + 1)
                if r == 0:
                    ln(dve.tensor_scalar(bis[:, 0:1], o[:, 0:1], float(T_POS), None, ALU.is_lt))
                    ln(dve.tensor_scalar(bis[:, 1:2], bis[:, 0:1], -2.0, 1.0, ALU.mult, ALU.add))
                    ln(dve.tensor_scalar(bis[:, 2:3], bis[:, 0:1], float(KTH - T_POS), float(T_POS), ALU.mult, ALU.add))
                    ln(dve.tensor_scalar(L2[:, :], L32[:, :], bis[:, 1:2], None, ALU.mult))
                    ln(dve.memset(cur_i[:, :], 0))
                    dve.tensor_copy(cand[:, 0:3], bitc[:, 0:3]).then_inc(b_upd, 1)
                    return
                n = 3 if r > 1 else 1
                shift = 30 if r == 1 else 30 - 2 * (r - 1)
                ln(dve.tensor_scalar(bisj[:, 0:n], o[:, 0:n], bis[:, 2:3], None, ALU.is_ge, ALU.add,
                                     accum_out=bis[:, 3:4]))
                ln(dve.tensor_scalar(inc_i[:, :], bis[:, 3:4], float(2 ** shift), None, ALU.mult))
                ln(dve.tensor_tensor(cur_i[:, r % 2:r % 2 + 1], cur_i[:, (r + 1) % 2:(r + 1) % 2 + 1], inc_i[:, :],
                                     ALU.bitwise_or))
                if r < 16:
                    dve.tensor_tensor(cand[:, 0:3], bitc[:, 3 * r:3 * r + 3],
                                      cur_i[:, r % 2:r % 2 + 1].to_broadcast([128, 3]), ALU.bitwise_or)\
                        .then_inc(b_upd, 1)
                else:
                    ln(dve.tensor_scalar(bis[:, 4:5], cur_i[:, 0:1].bitcast(F32), bis[:, 1:2], None, ALU.mult))
                    dve.scalar_tensor_tensor(G0[:, :], L32[:, :], bis[:, 4:5], L32[:, :], ALU.is_ge, ALU.mult)\
                        .then_inc(b_upd, 1)
            return fn

        for r in range(17):
            at("dve", 1.3 + 2 * r, bis_count(r))
            at("pe", mpos[("bis", r)], bis_sum(r))
            at("dve", 1.3 + 2 * r + 1.9, bis_update(r))

        def gates0_T(pe):
            o = misc_bank(pe, ("gT0", 0))
            pe.wait_ge(b_upd, 17)
            pe.transpose(o[:, 0:128], G0[:, :], ident[:, :]).then_inc(b_gt, 1)

        def gates0_ev(act):
            act.wait_ge(b_gt, 1)
            act.activation(gT0[:, :], bank[mb[("gT0", 0)][0]][:, 0:128], ACT.Copy).then_inc(b_ev, 1)

        def gates0_out(sp):
            sp.wait_ge(b_ev, 1)
            sp.dma_start(scr[0].rearrange("t e p -> (t e) p"), gT0[:, :]).then_inc(s_scr, 16)
            sp.wait_ge(s_scr, 16)
            sp.dma_start(gTb[:, :].rearrange("e (t p) -> e t p", p=128), scr[0].rearrange("t e p -> e t p"))\
                .then_inc(s_gtb[0], 16)

        at("pe", PG, gates0_T)
        at("act", PG, gates0_ev)
        at("sp", PG + 1, gates0_out)

        b2_order = [v for _, k, v in terms if k == "b2"]

        def b2_mm(v):
            layer, g = v

            def fn(pe):
                o = misc_bank(pe, ("b2", v))
                pe.wait_ge(ld[f"b2f{layer}"], 16)
                pe.wait_ge(s_gtb[0] if layer == 0 else s_gtb[1 + g], 16)
                pe.matmul(o[:, :], b2f[layer][:, :], gTb[:, g * 512:g * 512 + 512], start=True, stop=True)\
                    .then_inc(b_b2, 1)
            return fn

        for v in b2_order:
            at("pe", mpos[("b2", v)], b2_mm(v))

        def mid(g):
            m = M0[g]

            def pe_h(pe):
                o = misc_bank(pe, ("h", g))
                if g == 0:
                    pe.wait_ge(ld["lang"], 16 * 4 * B)
                pe.wait_ge(s_acc, done0[g])
                for i in range(2):
                    b = 2 * g + i
                    last = pe.matmul(o[0:A, i * S:i * S + S], cw1[:, b, :], acc[:, b * S:b * S + S], start=True, stop=True)
                last.then_inc(m_h, 1)

            def act_h(act):
                o = bank[mb[("h", g)][0]]
                act.wait_ge(m_h, g + 1)
                if g == 0:
                    act.wait_ge(ld["lang"], 16 * 4 * B)
                else:
                    act.wait_ge(m_xa, g)
                for i in range(2):
                    b = 2 * g + i
                    act.activation(hTs[0:A, i * S:i * S + S], o[0:A, i * S:i * S + S], ACT.Relu,
                                   bias=cb1[:, b:b + 1]).then_inc(m_hs, 1)

            def pe_xa(pe):
                o = misc_bank(pe, ("xa", g))
                pe.wait_ge(m_one, 1)
                pe.wait_ge(m_hs, 2 * g + 2)
                for i in range(4):
                    c = g * 512 + i * 128
                    pe.matmul(o[:, i * 128:i * 128 + 128], acc[:, c:c + 128], ident[:, :], start=True, stop=False)
                    last = pe.matmul(o[:, i * 128:i * 128 + 128], hTs[:, i * 128:i * 128 + 128],
                                     cw2[:, 2 * g + i // 2, :], start=False, stop=True)
                last.then_inc(m_xa, 1)

            def stats(dve, src, k, done):
                for i in range(4):
                    last = dve.bn_stats(st[:, i, :], src[:, i * 128:i * 128 + 128])
                link(dve, "dve", last)
                for i in range(4):
                    last = dve.bn_aggr(mv[:, k, i, :], st[:, i, :])
                last.then_inc(done, 1)

            def dve_stats(dve):
                dve.wait_ge(m_xa, g + 1)
                stats(dve, bank[mb[("xa", g)][0]], 0, m_mv)

            def rstd(k, ready, done):
                def fn(pool):
                    pool.wait_ge(ready, g + 1)
                    link(pool, "pool", pool.tensor_scalar(rs[:, k, :], mv[:, k, :, 1], EPS, None, ALU.add))
                    pool.tensor_tensor(rs[:, k, :], rs[:, k, :], mhalf[:, :], ALU.pow).then_inc(done, 1)
                return fn

            def dve_n1(dve):
                o = bank[mb[("xa", g)][0]]
                dve.wait_ge(m_rs, g + 1)
                if g:
                    dve.wait_ge(m_x2, g)
                for i in range(4):
                    last = dve.tensor_scalar(n1[:, i * 128:i * 128 + 128], o[:, i * 128:i * 128 + 128],
                                             mv[:, 0, i, 0:1], rs[:, 0, i:i + 1], ALU.subtract, ALU.mult)
                last.then_inc(m_n1, 1)

            def pool_x2(pool):
                pool.wait_ge(m_n1, g + 1)
                if g == 0:
                    pool.wait_ge(ld["lang"], 16 * 4 * B)
                else:
                    pool.wait_ge(m_x2T, g)
                    pool.wait_ge(m_n2, g)
                for i in range(2):
                    b = 2 * g + i
                    v3 = n1[:, i * S:i * S + S].rearrange("p (t d) -> p t d", t=2)
                    last = pool.tensor_tensor(v3, v3, gbc[:, b:b + 1, 0:D].to_broadcast([128, 2, D]), ALU.mult)
                link(pool, "pool", last)
                for i in range(2):
                    b = 2 * g + i
                    v3 = n1[:, i * S:i * S + S].rearrange("p (t d) -> p t d", t=2)
                    o3 = x2[:, i * S:i * S + S].rearrange("p (t d) -> p t d", t=2)
                    last = pool.tensor_tensor(o3, v3, gbc[:, b:b + 1, D:2 * D].to_broadcast([128, 2, D]), ALU.add)
                last.then_inc(m_x2, 1)

            def dve_stats2(dve):
                dve.wait_ge(m_x2, g + 1)
                stats(dve, x2, 1, m_mv2)

            def dve_n2(dve):
                dve.wait_ge(m_rs2, g + 1)
                if g:
                    dve.wait_ge(m_nT, g)
                for i in range(4):
                    last = dve.tensor_scalar(n2[:, i * 128:i * 128 + 128], x2[:, i * 128:i * 128 + 128],
                                             mv[:, 1, i, 0:1], rs[:, 1, i:i + 1], ALU.subtract, ALU.mult)
                last.then_inc(m_n2, 1)

            def pe_x2T(pe):
                o = misc_bank(pe, ("x2T", g))
                pe.wait_ge(m_x2, g + 1)
                for i in range(4):
                    last = pe.transpose(o[:, i * 128:i * 128 + 128], x2[:, i * 128:i * 128 + 128], ident[:, :])
                last.then_inc(m_x2T, 1)

            def pe_nT(pe):
                o = misc_bank(pe, ("nT", g))
                pe.wait_ge(m_n2, g + 1)
                for i in range(4):
                    last = pe.transpose(o[:, i * 128:i * 128 + 128], n2[:, i * 128:i * 128 + 128], ident[:, :])
                last.then_inc(m_nT, 1)

            def act_xn(act):
                o = bank[mb[("nT", g)][0]]
                if g == 0:
                    act.wait_ge(ld["fgb"], 16)
                else:
                    act.wait_ge(m_sp, g)
                    act.wait_ge(m_lg, g)
                act.wait_ge(m_nT, g + 1)
                act.activation(xn32[:, :], o[:, :], ACT.Identity, bias=fgb[:, 1:2], scale=fgb[:, 0:1]).then_inc(m_xn, 1)

            def pool_split(pool):
                pool.wait_ge(m_xn, g + 1)
                sl = slice(g * 512, g * 512 + 512)
                link(pool, "pool", pool.tensor_copy(xh1[:, sl], xn32[:, :]))
                pool.tensor_tensor(xl1[:, sl], xn32[:, :], xh1[:, sl].bitcast(F32), ALU.subtract).then_inc(m_sp, 1)

            def pe_lg(pe):
                o = misc_bank(pe, ("lg", g))
                if g == 0:
                    pe.wait_ge(ld["gw1"], 16)
                pe.wait_ge(m_xn, g + 1)
                for i in range(4):
                    last = pe.matmul(o[:, i * E:i * E + E], xn32[:, i * 128:i * 128 + 128], gw1[:, :], start=True, stop=True)
                last.then_inc(m_lg, 1)

            def dve_d(dve):
                o = bank[mb[("lg", g)][0]][:, 0:32].rearrange("p (t e) -> p t e", t=4)
                dve.wait_ge(m_lg, g + 1)
                link(dve, "dve", dve.tensor_reduce(c4[:, :, 0], o, AX.X, ALU.max))
                dve.tensor_tensor(lg[:, :, :], o, c4[:, :, 0:1].to_broadcast([128, 4, E]), ALU.subtract).then_inc(m_d, 1)

            def pool_exp(pool):
                pool.wait_ge(m_d, g + 1)
                pool.tensor_tensor(ex[:, :, :], ebase[:, :].rearrange("p (t e) -> p t e", t=4), lg[:, :, :], ALU.pow)\
                    .then_inc(m_e, 1)

            def dve_top(dve):
                def ln(ins):
                    link(dve, "dve", ins)
                dve.wait_ge(m_e, g + 1)
                if g == 0:
                    dve.wait_ge(ld["iota8"], 16)
                else:
                    dve.wait_ge(m_cT, g)
                ln(dve.tensor_reduce(c4[:, :, 0], ex[:, :, :], AX.X, ALU.add))
                ln(dve.reciprocal(c4[:, :, 1], c4[:, :, 0]))
                ln(dve.tensor_tensor(pr[:, :, :], ex[:, :, :], c4[:, :, 1:2].to_broadcast([128, 4, E]), ALU.mult))
                for i in range(4):
                    last = dve.max(mx8[:, i, :], pr[:, i, :])
                ln(last)
                for i in range(4):
                    last = dve.max_index(ix8[:, i, :], mx8[:, i, :], pr[:, i, :])
                ln(last)
                ln(dve.tensor_copy(ixf[:, :, :], ix8[:, :, :]))
                ln(dve.tensor_tensor(c4[:, :, 2], mx8[:, :, 0], mx8[:, :, 1], ALU.add))
                ln(dve.reciprocal(c4[:, :, 3], c4[:, :, 2]))
                ln(dve.tensor_tensor(mx8[:, :, 0:2], mx8[:, :, 0:2], c4[:, :, 3:4].to_broadcast([128, 4, 2]), ALU.mult))
                for i in range(4):
                    last = dve.tensor_scalar(oh[:, i, :], iota8[:, :], ixf[:, i, 1:2], mx8[:, i, 1:2], ALU.is_equal, ALU.mult)
                for i in range(4):
                    last = dve.tensor_scalar(cw[:, i, :], iota8[:, :], ixf[:, i, 0:1], mx8[:, i, 0:1], ALU.is_equal, ALU.mult)
                ln(last)
                dve.tensor_tensor(cw[:, :, :], cw[:, :, :], oh[:, :, :], ALU.add).then_inc(m_cw, 1)

            def pe_cT(pe):
                o = misc_bank(pe, ("cT", g))
                pe.wait_ge(m_cw, g + 1)
                pe.transpose(o[0:32, 0:128], cw[:, :, :].rearrange("p t e -> p (t e)"), ident[:, :]).then_inc(m_cT, 1)

            def act_cE(act):
                act.wait_ge(m_cT, g + 1)
                if g:
                    act.wait_ge(s_scr1[g - 1], 16)
                act.activation(cwT[:, :], bank[mb[("cT", g)][0]][0:32, 0:128], ACT.Copy).then_inc(m_cE, 1)

            def sp_gates(sp):
                sp.wait_ge(m_cE, g + 1)
                sp.dma_start(scr[1][4 * g:4 * g + 4, :, :].rearrange("t e p -> (t e) p"), cwT[:, :]).then_inc(s_scr1[g], 16)
                sp.wait_ge(s_scr1[g], 16)
                sp.wait_ge(b_b2, b2_order.index((0, g)) + 1)
                sp.dma_start(gTb[:, g * 512:g * 512 + 512].rearrange("e (t p) -> e t p", p=128),
                             scr[1][4 * g:4 * g + 4, :, :].rearrange("t e p -> e t p")).then_inc(s_gtb[1 + g], 16)

            at("pe", mpos[("h", g)], pe_h)
            at("act", m + 0.8, act_h)
            at("pe", mpos[("xa", g)], pe_xa)
            at("dve", m + 2.8, dve_stats)
            at("pool", m + 3.5, rstd(0, m_mv, m_rs))
            at("dve", m + 4.2, dve_n1)
            at("pool", m + 5.2, pool_x2)
            at("dve", m + 6.8, dve_stats2)
            at("pool", m + 7.5, rstd(1, m_mv2, m_rs2))
            at("dve", m + 8.3, dve_n2)
            at("pe", mpos[("x2T", g)], pe_x2T)
            at("pe", mpos[("nT", g)], pe_nT)
            at("act", m + 10.8, act_xn)
            at("pool", m + 12, pool_split)
            at("pe", mpos[("lg", g)], pe_lg)
            at("dve", m + 13.8, dve_d)
            at("pool", m + 14.8, pool_exp)
            at("dve", m + 15.8, dve_top)
            at("pe", mpos[("cT", g)], pe_cT)
            at("act", m + 18.8, act_cE)
            at("sp", m + 20, sp_gates)

        for g in range(NG):
            mid(g)

        def pool_consts(pool):
            pool.memset(hTs[A:A + 1, :], 1.0).then_inc(m_one, 1)
            pool.wait_ge(m_one, 1)
            pool.memset(mhalf[:, :], -0.5)
            link(pool, "pool", pool.memset(ebase[:, :], float(np.e)))

        at("pool", -99, pool_consts)

        def act_b1(act):
            act.wait_ge(ld["b1f1"], 16)

        at("act", 100, act_b1)

        def store(g):
            def fn(sp):
                sp.wait_ge(s_acc, done1[g])
                sp.dma_start(out[:, g * 512:g * 512 + 512], acc[:, g * 512:g * 512 + 512]).then_inc(s_out, 16)
            return fn

        for g in range(NG):
            at("sp", 1000 + g, store(g))

        def finish(sp):
            sp.wait_ge(s_out, 16 * NG)

        at("sp", 2000, finish)

        for q in Q.values():
            q.sort(key=lambda x: (x[0], x[1]))

        block = ctx.enter_context(nc.Block())

        @block.sync
        def _(eng):
            for _, _, fn in Q["sp"]:
                fn(eng)

        @block.tensor
        def _(eng):
            for _, _, fn in Q["pe"]:
                fn(eng)

        @block.scalar
        def _(eng):
            for _, _, fn in Q["act"]:
                fn(eng)

        @block.vector
        def _(eng):
            for _, _, fn in Q["dve"]:
                fn(eng)

        @block.gpsimd
        def _(eng):
            for _, _, fn in Q["pool"]:
                fn(eng)


def constants():
    def bf(v):
        return (np.ascontiguousarray(v, np.float32).view(np.uint32) >> 16).astype(np.uint16)

    l = np.arange(S)[:, None]
    j = np.arange(S)[None, :]
    allowed = np.stack([l <= j, l >= j, l != j])
    mask = np.where(allowed, 0.0, BIG).astype(np.float32)
    cnt = allowed.sum(axis=1).astype(np.float32)
    maskt = np.zeros((3, 128, 514), np.float32)
    for c in range(2):
        maskt[:, :, c * S:c * S + S] = mask[:, c * 128:c * 128 + 128, :]
        maskt[:, :, 2 * S + c] = cnt[:, c * 128:c * 128 + 128]
    sel = np.zeros((B, B, 128), np.float32)
    for b in range(B):
        sel[b, b, :] = 1.0
    bits = np.zeros((16, 3), np.int64)
    bits[0] = [1 << 30, 0, 0]
    for r in range(1, 16):
        bits[r] = [k << (30 - 2 * r) for k in (1, 2, 3)]
    return {
        "maskt": bf(maskt),
        "sel": sel.reshape(B, B * 128),
        "ident": np.eye(128, dtype=np.float32),
        "identb": bf(np.eye(128)),
        "bitc": np.broadcast_to(bits.reshape(1, 48).astype(np.int32), (128, 48)).copy(),
        "iota8": np.broadcast_to(np.arange(E, dtype=np.float32), (128, E)).copy(),
    }


def kernel(**inputs):
    import concourse.bacc as bacc
    from concourse.bass_utils import run_bass_kernel_spmd

    i = {k: np.asarray(v) for k, v in inputs.items()}
    c = np.ascontiguousarray
    x = i["x"].reshape(N, D)
    a = {
        "xT": c(x.T),
        "xtm": c(x.reshape(NT, 128, D).transpose(1, 0, 2)),
        "itype": i["itok_B_0_2"],
        "ilang": i["itok_B_0_8"],
        "w1c": i["L0_cond_W1"],
        "b1c": i["L0_cond_b1"].reshape(A, 1),
        "vc": i["L0_cond_v"].reshape(A, 1),
        "gw0": c(i["L0_ffn_gate_weight"].T),
        "w1_0": c(i["L0_ffn_w1"].transpose(2, 0, 1)),
        "b1_0": c(i["L0_ffn_b1"].reshape(E, 4, 128).transpose(2, 0, 1).reshape(128, 4 * E)),
        "w2_0": c(i["L0_ffn_w2"].transpose(2, 0, 1).reshape(4, 128, E, D).transpose(1, 2, 0, 3).reshape(128, E, 4 * D)),
        "b2_0": i["L0_ffn_b2"],
        "cw1": i["L1_cond_W1"],
        "cb1": i["L1_cond_b1"],
        "cw2": c(np.concatenate([i["L1_cond_W2"], i["L1_cond_b2"][:, None, :]], axis=1)),
        "gbc": c(np.concatenate([i["L1_cond_gamma"], i["L1_cond_beta"]], axis=1)),
        "gw1": i["L1_ffn_gate_w"],
        "w1_1": c(i["L1_ffn_w1"].transpose(1, 0, 2)),
        "b1_1": c(i["L1_ffn_b1"].reshape(E, 4, 128).transpose(2, 0, 1).reshape(128, 4 * E)),
        "w2_1": c(i["L1_ffn_w2"].reshape(E, 4, 128, D).transpose(2, 0, 1, 3).reshape(128, E, 4 * D)),
        "b2_1": i["L1_ffn_b2"],
        "fgb": c(np.stack([i["L1_ffn_gamma"], i["L1_ffn_beta"]], axis=1)),
    }
    a.update(constants())
    nc = bacc.Bacc("TRN2", target_bir_lowering=False, num_devices=1)
    arrays, t = {}, {}
    for name, v in a.items():
        v = c(v)
        arrays["in_" + name] = v
        t[name] = nc.dram_tensor("in_" + name, v.shape, mybir.dt.from_np(v.dtype), kind="ExternalInput").ap()
    for name in ("maskt", "identb"):
        t[name] = t[name].bitcast(BF16)
    out = nc.dram_tensor("out_T", [D, N], F32, kind="ExternalOutput").ap()
    build_adaln_ffn(nc, t, out)
    r = run_bass_kernel_spmd(nc, [arrays], core_ids=[0])
    return c(np.asarray(r.results[0]["out_T"]).T).reshape(B, S, D)
```

```python
import numpy as np
import concourse.bass as bass
from concourse import mybir
from contextlib import ExitStack

F32 = mybir.dt.float32
F32R = mybir.dt.float32r
BF16 = mybir.dt.bfloat16
F16 = mybir.dt.float16
I32 = mybir.dt.int32
U32 = mybir.dt.uint32
ACT = mybir.ActivationFunctionType
ALU = mybir.AluOpType
AX = mybir.AxisListType

B, S, D, E, H, A = 8, 256, 128, 8, 512, 32
N = B * S
NT = N // 128
NG = 4
LANGS = 10
KTH = 4 * 128 * 6
BIG = 1.0e30
EPS = 1e-5

GA = 3
TA = GA * 4
ZC = 7
TS = 256
NTL = GA * 512 * 2 // TS + E - 1
NZ = (E * GA * 512 + TS) // (128 * ZC)
CAP = GA * 512
WS, XS, HS = 64.0, 16.0, 8.0

RKO = 22.0
LAG = 3
NH = 4
NW = 4
NTMP = 3
NGS = 6
ND = 12
NX = 3


def step_order():
    out = []
    for e in range(6):
        out += [(0, e, g, e) for g in range(GA)]
    out += [(0, e, g, e) for g in range(GA) for e in (6, 7)]
    out += [(0, e, 3, k) for e, k in ((7, 7), (6, 6), (5, 5), (4, 4), (3, 8), (2, 9), (1, 10), (0, 11))]
    out += [(1, e, 3, None) for e in range(E)]
    return out


LOADS = [0, 1, 2, 3, 4, 5, 6, 7, 3, 2, 1, 0]
SLOT = [0, 1, 2, 3, 0, 1, 2, 3, 3, 2, 1, 0]
BEFORE = [None, None, None, None, 0, 1, 2, 3, 7, 6, 5, 4]


def build_adaln_ffn(nc, t, out):
    STEPS = step_order()
    NS0 = 32
    US = 4 * NS0
    UD = US + 2 * NTL
    UNITS = [("dense", s, c) for s in range(NS0) for c in range(4)]
    UNITS += [("tile", i, h) for i in range(NTL) for h in range(2)]
    UNITS += [("dense", s, c) for s in range(NS0, NS0 + E) for c in range(4)]
    NU = len(UNITS)

    def unit0(s):
        return 4 * s if s < NS0 else UD + 4 * (s - NS0)

    RES = [("dense", s) for s in range(NS0)] + [("tile", i) for i in range(NTL)] + [("dense", s) for s in range(NS0, NS0 + E)]
    res_of = {x: q for q, x in enumerate(RES)}

    def last_unit(q):
        kind, v = RES[q]
        return unit0(v) + 3 if kind == "dense" else US + 2 * v + 1
    with ExitStack() as ctx:
        def sb(name, shape, dt=F32):
            return ctx.enter_context(nc.sbuf_tensor(name, shape, dt))

        def sem(name):
            return ctx.enter_context(nc.semaphore(name))

        scr = [nc.dram_tensor(f"gates{i}", [NT, E, 128], F32, kind="Internal").ap() for i in range(2)]

        acc = sb("acc", [128, N])
        first = sb("first", [128, E * 1024])
        w16 = first[:, :].bitcast(F16)
        ysv = first[:, 0:ND * 512].rearrange("p (s n) -> p s n", n=512)
        attn = first[0:A, 0:N]
        xtm = first[:, N:N + NT * (D + 1)].rearrange("p (t d) -> p t d", t=NT)
        f1 = N + NT * (D + 1)
        ETa = first[:, f1:f1 + 8 * S].rearrange("p (k s) -> p k s", k=4)
        ident = sb("ident", [128, 128])
        identb = sb("identb", [128, 128], BF16)
        gTb = sb("gTb", [E, N])
        sel = gTb[:, 0:B * 128]
        onesb = sb("onesb", [128, 128], BF16)
        mg = sb("mg", [128, B * 257])
        maskt = mg[:, :].bitcast(BF16).rearrange("p (b n) -> p b n", b=B)
        gbc = mg[:, 0:B * 2 * D].rearrange("p (b n) -> p b n", b=B)
        w1c = sb("w1c", [D, A])
        b1c = sb("b1c", [A, 1])
        vc = sb("vc", [A, 1])
        vz = sb("vz", [A, 2 * B - 1])
        ty = sb("ty", [B, 1], I32)
        lid = sb("lid", [1, B], I32)
        tyr = sb("tyr", [1, B], I32)
        is_t = sb("is_t", [B, 4])
        f0 = N + NT * (D + 1) + 8 * S
        rows = first[0:B, f0:f0 + S]
        pre = first[0:B, f0 + S:f0 + 2 * S + 2]
        suf = first[0:B, f0 + 2 * S + 2:f0 + 3 * S + 4]
        cl = first[0:B, f0 + 3 * S + 4:f0 + 4 * S + 4]
        mrow = first[0:B, f0 + 4 * S + 4:f0 + 5 * S + 4]
        scol = sb("scol", [128, NT])
        rr = sb("rr", [128, 2, 2, 2])
        Gs = sb("Gs", [128, NGS, 512])
        ptm = Gs[:, 0, :].rearrange("p (k n) -> p k n", k=2)
        pT = Gs[:, 1, :].rearrange("p (k n) -> p k n", k=2)

        def ET(b):
            return ETa[:, b, :] if b < 4 else Gs[:, b - 2, :]

        gw0 = sb("gw0", [D, E])
        gw1 = sb("gw1", [D, E])
        L32 = sb("L32", [128, NT * E])
        L2 = sb("L2", [128, NT * E])
        junk = sb("junk", [128, 3, NT * E], BF16)
        G0 = sb("G0", [128, NT * E])
        cnt3 = sb("cnt3", [128, 2, 4], BF16)
        bis = sb("bis", [128, 8])
        bisj = sb("bisj", [128, 4])
        inc_i = sb("inc_i", [128, 1], I32)
        cur_i = sb("cur_i", [128, 2], I32)
        cand = sb("cand", [128, 4], I32)
        bitc = sb("bitc", [128, 16 * 3], I32)
        gT0 = sb("gT0", [128, 128])
        b1f = [sb(f"b1f{i}", [128, 4 * E]) for i in range(2)]
        b2f = [sb(f"b2f{i}", [E, D]) for i in range(2)]
        xh = sb("xh", [128, 2, N // 2], F32R)
        xl = sb("xl", [128, 2, N // 2], F32R)
        selr = xh[0:B, 1, :]
        mh = xl[0:B, 1, 0:2 * S].rearrange("b (c s) -> b c s", c=2)
        ml = xl[0:B, 1, 2 * S:4 * S].rearrange("b (c s) -> b c s", c=2)
        xbh = sb("xbh", [128, 512], F16)
        xbl = sb("xbl", [128, 512], F16)
        h16 = sb("h16", [128, NH, 512], F16)
        l16 = sb("l16", [128, NH, 512], F16)
        scx = nc.dram_tensor("sorted_in", [E * CAP + TS, D], F32, kind="Internal").ap()
        scy = nc.dram_tensor("sorted_out", [NTL * TS, D], F32, kind="Internal").ap()
        n2A = sb("n2A", [128, TA, D])
        OH = sb("OH", [128, 2, TA, E])
        OB = sb("OB", [128, TA, E], BF16)
        wA = sb("wA", [128, TA, 2])
        triu = sb("triu", [128, 128], BF16)
        cumb = sb("cumb", [128, TA + 1, E], BF16)
        oh2 = sb("oh2", [128, 2, 4, E])
        rk4 = sb("rk4", [128, 4, E])
        region = sb("region", [128, E])
        zer = sb("zer", [128, ZC * D])
        e8 = sb("e8", [128, 4, E])
        ci = sb("ci", [128, E], I32)
        pk = sb("pk", [128, 2, TA])
        idx = sb("idx", [128, 2, TA], U32)
        pk2 = sb("pk2", [128, 2, TA])
        idx2 = sb("idx2", [128, 2, TA], U32)
        it256 = sb("it256", [128, NTL])
        cmp_ = sb("cmp_", [128, NTL, E])
        cmp2 = sb("cmp2", [128, NTL, E])
        tef = sb("tef", [128, 2, NTL])
        tei = sb("tei", [128, 3, NTL], I32)
        wraw = sb("wraw", [128, 2, 1024])
        wr = wraw[:, :, :].rearrange("p a n -> p (a n)")
        xr = wr[:, 0:NX * 256].rearrange("p (k z d) -> p k z d", k=NX, z=2)
        xt32 = wr[:, NX * 256:NX * 256 + 512].rearrange("p (k n) -> p k n", k=2)
        xth = sb("xth", [128, NX, TS], F16)
        xtl = sb("xtl", [128, NX, TS], F16)
        fgs = sb("fgs", [D, 2])
        yo = sb("yo", [128, 2, 2 * D])
        mo1 = sb("mo1", [128, 2, D])
        mo = sb("mo", [128, 2, D])
        wh = sb("wh", [128, NW, 1024], F32R)
        wl = sb("wl", [128, NW, 1024], F32R)
        yg = wh[:, 0:3, :].bitcast(F32).rearrange("p a (k d) -> p (a k) d", d=D)
        h32 = sb("h32", [128, NH, 512])
        hh = sb("hh", [128, NH, 512], F32R)
        hl = sb("hl", [128, NH, 512], F32R)
        tmp = sb("tmp", [128, NTMP, 512])
        cw1 = sb("cw1", [D, B, A])
        cb1 = sb("cb1", [A, B])
        cw2 = sb("cw2", [A + 1, B, D])
        fgb = sb("fgb", [D, 2])
        hTs = sb("hTs", [A + 1, 512])
        st = sb("st", [128, 4, 6])
        mv = sb("mv", [128, 2, 4, 2])
        rs = sb("rs", [128, 2, 4])
        mhalf = sb("mhalf", [128, 4])
        n1 = sb("n1", [128, 4 * D])
        x2 = sb("x2", [128, 4 * D])
        xn32 = sb("xn32", [128, 512])
        lg = sb("lg", [128, 4, E])
        ex = sb("ex", [128, 4, E])
        pr = sb("pr", [128, 4, E])
        wk = sb("wk", [128, 4, 2])
        c4 = sb("c4", [128, 4, 5])
        mx8 = sb("mx8", [128, 4, 8])
        ix8 = sb("ix8", [128, 4, 8], U32)
        ixf = sb("ixf", [128, 4, 8])
        iota8 = sb("iota8", [128, 4, E])
        oh = sb("oh", [128, 2, 4, E])
        cw = sb("cw", [128, 4, E])
        cwT = sb("cwT", [32, 128])

        bank = [ctx.enter_context(nc.psum_tensor(f"bank{i}", [128, 512], F32)) for i in range(8)]

        ld = {}

        def load_sem(name):
            ld[name] = sem("ld_" + name)
            return ld[name]

        s_m1 = sem("s_m1")
        s_g = sem("s_g")
        s_hia = sem("s_hia")
        s_hid = sem("s_hid")
        s_lo = sem("s_lo")
        s_m2 = sem("s_m2")
        s_ysv = sem("s_ysv")
        s_tmp = sem("s_tmp")
        s_acc = sem("s_acc")
        s_w = sem("s_w")
        s_wd = [sem(f"s_wd{i}") for i in range(NW)]
        s_w16h = sem("s_w16h")
        s_w16 = sem("s_w16")
        t_rk = sem("t_rk")
        t_ix = sem("t_ix")
        t_pl = sem("t_pl")
        t_te = sem("t_te")
        t_z = sem("t_z")
        t_zm = sem("t_zm")
        t_sc = sem("t_sc")
        t_xr = [sem(f"t_xr{i}") for i in range(NX)]
        t_tr = sem("t_tr")
        t_x32 = sem("t_x32")
        t_xh = sem("t_xh")
        t_xl = sem("t_xl")
        t_fg = sem("t_fg")
        t_yo = sem("t_yo")
        t_ys = [sem(f"t_ys{i}") for i in range(2)]
        t_yg = [sem(f"t_yg{i}") for i in range(TA)]
        t_mo1 = sem("t_mo1")
        t_mo = sem("t_mo")
        t_moe = sem("t_moe")
        s_raw = [sem(f"s_raw{i}") for i in range(2)]
        s_G = [sem(f"s_G{i}") for i in range(NGS)]
        s_scr = sem("s_scr0")
        s_scr1 = [sem(f"s_scr1_{g}") for g in range(NG)]
        s_gtb = [sem(f"s_gtb{i}") for i in range(1 + NG)]
        s_out = sem("s_out")
        p_at = sem("p_at")
        p_th = sem("p_th")
        p_sc = sem("p_sc")
        p_v = sem("p_v")
        p_m = sem("p_m")
        p_col = sem("p_col")
        p_pm = sem("p_pm")
        p_ex = sem("p_ex")
        p_po = sem("p_po")
        p_no = sem("p_no")
        p_tr = sem("p_tr")
        p_ev = sem("p_ev")
        p_lg = sem("p_lg")
        p_x = sem("p_x")
        p_row = sem("p_row")
        p_lc = sem("p_lc")
        p_one = sem("p_one")
        b_cnt = sem("b_cnt")
        b_sum = sem("b_sum")
        b_upd = sem("b_upd")
        b_g = sem("b_g")
        b_gt = sem("b_gt")
        b_ev = sem("b_ev")
        b_b2 = sem("b_b2")
        m_h = sem("m_h")
        m_hs = sem("m_hs")
        m_xa = sem("m_xa")
        m_mv = sem("m_mv")
        m_rs = sem("m_rs")
        m_n1 = sem("m_n1")
        m_x2 = sem("m_x2")
        m_mv2 = sem("m_mv2")
        m_rs2 = sem("m_rs2")
        m_n2 = sem("m_n2")
        m_x2T = sem("m_x2T")
        m_nT = sem("m_nT")
        m_xn = sem("m_xn")
        m_sp = sem("m_sp")
        m_lg = sem("m_lg")
        m_d = sem("m_d")
        m_e = sem("m_e")
        m_cw = sem("m_cw")
        m_cT = sem("m_cT")
        m_cE = sem("m_cE")
        m_one = sem("m_one")

        chain = {"dve": [sem("c_dve"), 0], "pool": [sem("c_pool"), 0], "act": [sem("c_act"), 0]}

        def link(eng, who, ins):
            c = chain[who]
            c[1] += 1
            ins.then_inc(c[0], 1)
            eng.wait_ge(c[0], c[1])

        Q = {k: [] for k in ("pe", "act", "dve", "pool", "sp")}

        def at(q, pos, fn):
            Q[q].append((pos, len(Q[q]), fn))

        def spread(q, who, pos, step, parts):
            reached = {}
            for n, part in enumerate(parts):
                def fn(eng, n=n, part=part):
                    if n:
                        eng.wait_ge(chain[who][0], reached["n"])
                    ins = part(eng)
                    if n < len(parts) - 1:
                        chain[who][1] += 1
                        reached["n"] = chain[who][1]
                        ins.then_inc(chain[who][0], 1)
                at(q, pos + step * n, fn)

        HIA = [u % 2 == 0 or u < 40 for u in range(NU)]
        nha = np.cumsum(HIA).tolist()
        nhd = np.cumsum([not x for x in HIA]).tolist()

        last_use = {}
        for s_, (layer_, _, _, k_) in enumerate(STEPS):
            if layer_ == 0:
                last_use[k_] = s_

        terms = []
        for s in range(NS0 + E):
            if s >= ND:
                terms.append((unit0(s) + 4 + LAG + 0.5, "y", s))
            else:
                terms.append((4 * ND + 6 + 2 * s + 0.7, "y", s))
        M0 = [4.0 * max(s for s in range(NS0) if STEPS[s][2] == g) + 10 for g in range(NG)]
        MO = UD + 4.0
        WP = [MO + 5.5 + 1.7 * i for i in range(TA)]
        for g in range(NG):
            terms.append((4 * ND + 7 + 3 * g + 0.4, "b2", (0, g)))
            terms.append((M0[g] + 13.4, "x2", g))
        terms.append((UD + 8.4, "b2", (1, 3)))
        for g in range(GA):
            terms.append((WP[4 * g + 3] + 3.2, "moe", g))
        terms.sort(key=lambda x: x[0])
        where = {(k, v): i for i, (_, k, v) in enumerate(terms)}
        ys = [i for i, (_, k, _) in enumerate(terms) if k == "y"]
        gslot = {ti: j for j, ti in enumerate(ys)}
        group_terms = {g: 0 for g in range(NG)}

        def group_of(kind, v):
            return STEPS[v][2] if kind == "y" else (v if kind in ("x2", "moe") else v[1])

        def layer_of(kind, v):
            return STEPS[v][0] if kind == "y" else (1 if kind in ("x2", "moe") else v[0])

        done0 = {g: max(i for i, (_, k, v) in enumerate(terms) if group_of(k, v) == g and layer_of(k, v) == 0) + 1
                 for g in range(NG)}
        done1 = {g: max(i for i, (_, k, v) in enumerate(terms) if group_of(k, v) == g) + 1 for g in range(NG)}

        misc = []
        PB = [-20.0, -19.0] + [0.55 + 1.5 * (b - 2) for b in range(2, B)]
        PD = [0.1, 1.6, 1.7, 1.8, 3.2, 3.3]
        for b in range(B):
            misc.append((PB[b], ("po", b), (p_no, b + 1)))
            misc.append((PB[b] + PD[1], ("pt", b), (p_ev, b + 1)))
            misc.append((PB[b] + PD[4], ("pl", b), (p_lc, b + 1)))
        B0 = PB[B - 1] + PD[5] + 0.3
        for r in range(17):
            misc.append((B0 + 2.45 + 2 * r, ("bis", r), (b_upd, r + 1)))
        PG = B0 + 39.45
        misc.append((PG, ("gT0", 0), (b_ev, 1)))
        for g in range(NG):
            misc.append((4 * ND + 6 + 3 * g + 0.35, ("b2", (0, g)), (s_tmp, where[("b2", (0, g))] + 1)))
            misc.append((M0[g] + 0.75, ("h", g), (m_hs, 2 * g + 2)))
            misc.append((M0[g] + 2.75, ("xa", g), (m_n1, g + 1)))
            misc.append((M0[g] + 13.0, ("x2T", g), (s_tmp, where[("x2", g)] + 1)))
            misc.append((M0[g] + 15.1, ("nT", g), (m_xn, g + 1)))
            misc.append((M0[g] + 17.0, ("lg", g), (m_d, g + 1)))
            misc.append((M0[g] + 22.5, ("cT", g), (m_cE, g + 1)))
        RK = [M0[g] + RKO for g in range(GA)]
        for g in range(GA):
            misc.append((RK[g] + 0.75, ("rk", g), (t_te, 1) if g == GA - 1 else (t_ix, g + 1)))

        def tpos(i):
            return max(US - 0.4 + 0.05 * i, US + 2 * i - 5 + 0.6)

        for i in range(NTL):
            misc.append((tpos(i), ("t", i), (t_x32, i + 1)))
        misc.append((UD + 8.35, ("b2", (1, 3)), (s_tmp, where[("b2", (1, 3))] + 1)))
        for g in range(GA):
            misc.append((WP[4 * g] + 3.0, ("moe", g), (s_tmp, where[("moe", g)] + 1)))
        misc.sort(key=lambda x: x[0])
        HOLD = {"xa": 4.5, "moe": 7.5, "bis": 1.8, "rk": 2.0}
        mb, held = {}, [(-1e9, None), (-1e9 + 1, None)]
        for pos, key, free in misc:
            i = 0 if held[0][0] <= held[1][0] else 1
            mb[key] = (6 + i, held[i][1])
            held[i] = (pos + HOLD.get(key[0], 0.8), free)
        mpos = {key: pos for pos, key, _ in misc}

        def misc_bank(eng, key):
            i, free = mb[key]
            if free is not None:
                eng.wait_ge(free[0], free[1])
            return bank[i]

        regs = {}

        def tile_expert(eng, name, i):
            if (name, "ready") not in regs:
                eng.wait_ge(t_te, 1)
                regs[(name, "ready")] = True
            if (name, i) not in regs:
                k, unit = (1, 4) if name == "act" else (0, 2048)
                regs[(name, i)] = eng.value_load(tei[0:1, k, i:i + 1], min_val=0, max_val=(E - 1) * unit)
            return regs[(name, i)]

        def expert_weights(r, off):
            return w16[:, off:off + (E - 1) * 2048 + 128][:, bass.ds(r, 128)]

        def pe_m1(u):
            kind, v, c = UNITS[u]
            o = bank[u % 4]

            def fn(pe):
                if kind == "tile":
                    if v == 0 and c == 0:
                        pe.wait_ge(s_w16, E)
                    r = tile_expert(pe, "pe", v)
                    if c == 0:
                        pe.wait_ge(t_xl, v + 1)
                    pe.wait_ge(s_g, u - 3)
                    a, b_ = xth[:, v % NX, :], xtl[:, v % NX, :]
                    for k in range(2):
                        off = (2 * c + k) * 128
                        w_h, w_l = expert_weights(r, off), expert_weights(r, 1024 + off)
                        oo = o[:, k * TS:k * TS + TS]
                        pe.matmul(oo, w_h, a, start=True, stop=False)
                        pe.matmul(oo, w_h, b_, start=False, stop=False)
                        last = pe.matmul(oo, w_l, a, start=False, stop=True)
                    last.then_inc(s_m1, 1)
                    return
                layer, e, g, k = STEPS[v]
                if layer == 0:
                    if c == 0:
                        pe.wait_ge(s_w, k + 1)
                        pe.wait_ge(p_x, 2 * g + 2)
                    a = xh[:, g // 2, (g % 2) * 512:(g % 2) * 512 + 512]
                    b_ = xl[:, g // 2, (g % 2) * 512:(g % 2) * 512 + 512]
                    w_h = wh[:, SLOT[k], c * 128:c * 128 + 128]
                    w_l = wl[:, SLOT[k], c * 128:c * 128 + 128]
                else:
                    pe.wait_ge(m_sp, 1)
                    a, b_ = xbh[:, :], xbl[:, :]
                    w_h = w16[:, e * 2048 + c * 128:e * 2048 + c * 128 + 128]
                    w_l = w16[:, e * 2048 + 1024 + c * 128:e * 2048 + 1024 + c * 128 + 128]
                if u >= 4:
                    pe.wait_ge(s_g, u - 3)
                pe.matmul(o[:, :], w_h, a, start=True, stop=False)
                pe.matmul(o[:, :], w_h, b_, start=False, stop=False)
                pe.matmul(o[:, :], w_l, a, start=False, stop=True).then_inc(s_m1, 1)
            return fn

        def result_read(eng, q):
            kind, v = RES[q]
            if kind == "tile":
                eng.wait_ge(t_yo, v + 1)
            elif v < ND:
                eng.wait_ge(s_ysv, v + 1)
            else:
                eng.wait_ge(s_tmp, where[("y", v)] + 1)

        def pe_m2(u):
            kind, v, c = UNITS[u]
            q = res_of[(kind, v)]
            o = bank[4 + q % 2]

            def fn(pe):
                if c == 0 and q >= 2:
                    result_read(pe, q - 2)
                pe.wait_ge(s_lo, u + 1)
                if kind == "tile":
                    r = tile_expert(pe, "pe", v)
                    for k in range(2):
                        off = 512 + (2 * c + k) * 128
                        w_h, w_l = expert_weights(r, off), expert_weights(r, 1024 + off)
                        for z in range(2):
                            sl = slice(k * TS + z * 128, k * TS + z * 128 + 128)
                            oo = o[:, z * 128:z * 128 + 128]
                            a, b_ = h16[:, u % NH, sl], l16[:, u % NH, sl]
                            pe.matmul(oo, a, w_h, start=(c == 0 and k == 0 and z == 0), stop=False, skip_group_check=True)
                            pe.matmul(oo, a, w_l, start=False, stop=False, skip_group_check=True)
                            last = pe.matmul(oo, b_, w_h, start=False, stop=(c == 1 and k == 1), skip_group_check=True)
                    last.then_inc(s_m2, 1)
                    return
                layer, e, g, k = STEPS[v]
                if layer == 0:
                    w_h = wh[:, SLOT[k], 512 + c * 128:640 + c * 128]
                    w_l = wl[:, SLOT[k], 512 + c * 128:640 + c * 128]
                    a, b_ = hh[:, u % NH, :], hl[:, u % NH, :]
                else:
                    w_h = w16[:, e * 2048 + 512 + c * 128:e * 2048 + 640 + c * 128]
                    w_l = w16[:, e * 2048 + 1536 + c * 128:e * 2048 + 1664 + c * 128]
                    a, b_ = h16[:, u % NH, :], l16[:, u % NH, :]
                pe.matmul(o[:, :], w_h, a, start=(c == 0), stop=False)
                pe.matmul(o[:, :], w_l, a, start=False, stop=False)
                pe.matmul(o[:, :], w_h, b_, start=False, stop=(c == 3)).then_inc(s_m2, 1)
            return fn

        def act_gelu(u):
            kind, v, c = UNITS[u]

            def fn(act):
                if kind == "tile":
                    r = tile_expert(act, "act", v)
                act.wait_ge(s_m1, u + 1)
                if u >= NH:
                    act.wait_ge(s_lo, u - NH + 1)
                if kind == "tile":
                    for k in range(2):
                        last = act.activation(h32[:, u % NH, k * TS:k * TS + TS], bank[u % 4][:, k * TS:k * TS + TS],
                                              ACT.Gelu, bias=b1f[1][:, 2 * c + k:2 * c + k + 4 * (E - 1) + 1][:, bass.ds(r, 1)],
                                              scale=1.0 / (WS * XS))
                    last.then_inc(s_g, 1)
                    return
                layer, e, g, _ = STEPS[v]
                act.activation(h32[:, u % NH, :], bank[u % 4][:, :],
                               ACT.Gelu if layer else ACT.Gelu_apprx_tanh,
                               bias=b1f[layer][:, e * 4 + c:e * 4 + c + 1],
                               scale=1.0 / (WS * XS) if layer else 1.0).then_inc(s_g, 1)
            return fn

        def hi_part(q, u):
            def fn(eng):
                eng.wait_ge(s_g, u + 1)
                if u >= NH:
                    eng.wait_ge(s_m2, u - NH + 1)
                dst = hh[:, u % NH, :] if u < US else h16[:, u % NH, :]
                if q == "act":
                    eng.activation(dst, h32[:, u % NH, :], ACT.Copy, scale=1.0 if u < US else HS).then_inc(s_hia, 1)
                elif u < US:
                    eng.tensor_copy(dst, h32[:, u % NH, :]).then_inc(s_hid, 1)
                else:
                    eng.tensor_scalar(dst, h32[:, u % NH, :], HS, None, ALU.mult).then_inc(s_hid, 1)
            return fn

        def lo_part(u):
            def fn(dve):
                if HIA[u]:
                    dve.wait_ge(s_hia, nha[u])
                else:
                    dve.wait_ge(s_hid, nhd[u])
                if u >= NH:
                    dve.wait_ge(s_m2, u - NH + 1)
                if u < US:
                    dve.tensor_tensor(hl[:, u % NH, :], h32[:, u % NH, :], hh[:, u % NH, :].bitcast(F32),
                                      ALU.subtract).then_inc(s_lo, 1)
                else:
                    dve.scalar_tensor_tensor(l16[:, u % NH, :], h32[:, u % NH, :], HS, h16[:, u % NH, :],
                                             ALU.mult, ALU.subtract).then_inc(s_lo, 1)
            return fn

        for u in range(NU):
            at("pe", u, pe_m1(u))
            at("pe", u + LAG + 0.5, pe_m2(u))
            at("act", u, act_gelu(u))
            if HIA[u]:
                at("act", u + 1.2, hi_part("act", u))
            else:
                at("dve", u, hi_part("dve", u))
            at("dve", u + 1.1, lo_part(u))

        def keep(s):
            def fn(act):
                act.wait_ge(s_m2, 4 * s + 4)
                act.activation(ysv[:, s, :], bank[4 + s % 2][:, :], ACT.Copy).then_inc(s_ysv, 1)
            return fn

        for s in range(ND):
            at("act", 4 * s + 4 + LAG + 0.3, keep(s))

        def term(i, kind, v):
            def fn(dve):
                if i >= NTMP:
                    dve.wait_ge(s_acc, i - NTMP + 1)
                o = tmp[:, i % NTMP, :]
                if kind == "y":
                    j = gslot[i]
                    dve.wait_ge(s_G[j % NGS], 16 * (j // NGS + 1))
                    if v < ND:
                        dve.wait_ge(s_ysv, v + 1)
                        src = ysv[:, v, :]
                    else:
                        q = res_of[("dense", v)]
                        dve.wait_ge(s_m2, last_unit(q) + 1)
                        src = bank[4 + q % 2][:, :]
                    if STEPS[v][0] == 0:
                        dve.tensor_tensor(o, src, Gs[:, j % NGS, :], ALU.mult).then_inc(s_tmp, 1)
                    else:
                        dve.scalar_tensor_tensor(o, src, 1.0 / (WS * HS), Gs[:, j % NGS, :], ALU.mult, ALU.mult)\
                            .then_inc(s_tmp, 1)
                elif kind == "b2":
                    dve.wait_ge(b_b2, [("b2", x) for _, k, x in terms if k == "b2"].index(("b2", v)) + 1)
                    dve.tensor_copy(o, bank[mb[("b2", v)][0]][:, :]).then_inc(s_tmp, 1)
                elif kind == "moe":
                    dve.wait_ge(t_moe, 4 * v + 4)
                    dve.tensor_copy(o, bank[mb[("moe", v)][0]][:, :]).then_inc(s_tmp, 1)
                else:
                    dve.wait_ge(m_x2T, v + 1)
                    dve.tensor_copy(o, bank[mb[("x2T", v)][0]][:, :]).then_inc(s_tmp, 1)
            return fn

        def add(i, kind, v):
            g = group_of(kind, v)

            def fn(pool):
                pool.wait_ge(s_tmp, i + 1)
                if i:
                    pool.wait_ge(s_acc, i)
                if kind == "x2":
                    pool.wait_ge(m_xa, v + 1)
                a = acc[:, g * 512:g * 512 + 512]
                pool.tensor_tensor(a, a, tmp[:, i % NTMP, :], ALU.add).then_inc(s_acc, 1)
            return fn

        for i, (pos, kind, v) in enumerate(terms):
            at("dve", pos, term(i, kind, v))
            at("pool", pos + 0.5, add(i, kind, v))

        def load_gates(j):
            ti = ys[j]
            s = terms[ti][2]
            layer, e, g, _ = STEPS[s]

            def fn(sp):
                if layer == 0:
                    sp.wait_ge(s_scr, 16)
                else:
                    sp.wait_ge(s_scr1[g], 16)
                if j >= NGS:
                    sp.wait_ge(s_tmp, ys[j - NGS] + 1)
                src = scr[layer][4 * g:4 * g + 4, e:e + 1, :].rearrange("t e p -> e t p")
                sp.dma_start(Gs[:, j % NGS, :].rearrange("q (t p) -> q t p", t=4),
                             src.to_broadcast([128, 4, 128])).then_inc(s_G[j % NGS], 16)
            return fn

        for j, ti in enumerate(ys):
            s = terms[ti][2]
            pos = terms[ys[j - NGS]][0] + 1.5 if j >= NGS else PG + 2
            if STEPS[s][0] == 1:
                pos = max(pos, M0[STEPS[s][2]] + 26.5)
            at("sp", pos, load_gates(j))

        ORDER16 = [5, 6, 7, 0, 1, 2, 3, 4]
        NL = len(LOADS)

        def w_free(k):
            return -50.0 + 2 * k if k < NW else 4.0 * last_use[BEFORE[k]] + 4 + LAG + 1.5

        P16 = 4 * ND + 6 + 2 * ND + 2.0

        def w_pos(k):
            if k < NL:
                return w_free(k)
            return P16 + 4.5 * (k - NL)

        def raw_read(eng, k):
            if k < NL:
                eng.wait_ge(s_w, k + 1)
            else:
                eng.wait_ge(s_w16, k - NL + 1)

        seq = sorted(range(NL + E), key=w_pos)
        assert [k for k in seq if k < NL] == list(range(NL))
        turn = {k: n for n, k in enumerate(seq)}

        def load_w(k):
            n = turn[k]

            def fn(sp):
                if n >= 2:
                    raw_read(sp, seq[n - 2])
                if k < NL:
                    src = t["w_0"][:, LOADS[k], :]
                else:
                    src = t["w_1"][:, ORDER16[k - NL], :]
                sp.dma_start(wraw[:, n % 2, :], src).then_inc(s_raw[n % 2], 16)
            return fn

        def round_w(k):
            def fn(pool):
                if k >= NW:
                    pool.wait_ge(s_m2, 4 * last_use[BEFORE[k]] + 4)
                pool.dma_start(wh[:, SLOT[k], :], t["w_0"][:, LOADS[k], :]).then_inc(s_wd[SLOT[k]], 16)
            return fn

        def split_w(k):
            n = turn[k]

            def fn(pool):
                pool.wait_ge(s_raw[n % 2], 16 * (n // 2 + 1))
                pool.wait_ge(s_wd[SLOT[k]], 16 * (1 + SLOT[:k].count(SLOT[k])))
                if k >= NW:
                    pool.wait_ge(s_m2, 4 * last_use[BEFORE[k]] + 4)
                for p in range(2):
                    sl = slice(p * 512, p * 512 + 512)
                    last = pool.tensor_tensor(wl[:, SLOT[k], sl], wraw[:, n % 2, sl],
                                              wh[:, SLOT[k], sl].bitcast(F32), ALU.subtract)
                last.then_inc(s_w, 1)
            return fn

        last_kept = max(where[("y", s)] for s in range(ND))

        def w16_high(k):
            n, e = turn[k], ORDER16[k - NL]

            def fn(act):
                act.wait_ge(s_raw[n % 2], 16 * (n // 2 + 1))
                act.wait_ge(s_tmp, last_kept + 1)
                act.activation(w16[:, e * 2048:e * 2048 + 1024], wraw[:, n % 2, :], ACT.Copy, scale=WS).then_inc(s_w16h, 1)
            return fn

        def w16_low(k):
            n, e = turn[k], ORDER16[k - NL]

            def fn(dve):
                dve.wait_ge(s_w16h, k - NL + 1)
                dve.scalar_tensor_tensor(w16[:, e * 2048 + 1024:e * 2048 + 2048], wraw[:, n % 2, :], WS,
                                         w16[:, e * 2048:e * 2048 + 1024], ALU.mult, ALU.subtract).then_inc(s_w16, 1)
            return fn

        for k in range(NL + E):
            if k < NL:
                at("pool", w_free(k), round_w(k))
                at("pool", w_free(k) + (2.5 if k >= NW else 0.1), split_w(k))
            else:
                at("act", w_pos(k) + 2, w16_high(k))
                at("dve", w_pos(k) + 2.4, w16_low(k))
            n = turn[k]
            at("sp", -60.0 + n if n < 2 else w_pos(seq[n - 2]) + 2.9, load_w(k))

        def sp_loads(sp):
            for g in range(NG):
                sp.dma_start(acc[:, g * 512:g * 512 + 512], t["xT"][:, g * 512:g * 512 + 512]).then_inc(load_sem(f"x{g}"), 16)
                if g == 0:
                    s0 = load_sem("c0")
                    sp.dma_start(w1c[:, :], t["w1c"]).then_inc(s0, 16)
                    sp.dma_start(b1c[:, :], t["b1c"]).then_inc(s0, 16)
                    sp.dma_start(vc[:, :], t["vc"]).then_inc(s0, 16)
            s0 = load_sem("ids")
            sp.dma_start(tyr[:, :], t["itype"].rearrange("(a n) -> a n", a=1)).then_inc(s0, 16)
            sp.dma_start(lid[:, :], t["ilang"].rearrange("(a n) -> a n", a=1)).then_inc(s0, 16)
            sp.dma_start(ty[:, :], t["itype"].rearrange("(n a) -> n a", a=1)).then_inc(load_sem("ty"), 16)
            sp.dma_start(sel[:, :], t["sel"]).then_inc(load_sem("sel"), 16)
            sp.dma_start(identb[:, :], t["identb"]).then_inc(load_sem("identb"), 16)
            sp.wait_ge(s0, 32)
            for b in range(B):
                r = sp.value_load(tyr[0:1, b:b + 1], min_val=0, max_val=2)
                sp.dma_start(maskt[:, b, :], t["maskt"][bass.ds(r, 1), :, :].rearrange("a p c -> p (a c)"))\
                    .then_inc(load_sem(f"mask{b}"), 16)
            sp.dma_start(xtm[:, :, 0:D], t["xtm"]).then_inc(load_sem("xtm"), 16)
            sp.dma_start(ident[:, :], t["ident"]).then_inc(load_sem("ident"), 16)
            sp.dma_start(gw0[:, :], t["gw0"]).then_inc(load_sem("gw0"), 16)
            sp.dma_start(b1f[0][:, :], t["b1_0"]).then_inc(load_sem("b1f0"), 16)
            sp.dma_start(bitc[:, :], t["bitc"]).then_inc(load_sem("bitc"), 16)

        at("sp", -100, sp_loads)

        def sp_later(sp):
            sp.dma_start(b2f[0][:, :], t["b2_0"]).then_inc(load_sem("b2f0"), 16)
            sp.dma_start(b2f[1][:, :], t["b2_1"]).then_inc(load_sem("b2f1"), 16)
            sp.dma_start(b1f[1][:, :], t["b1_1"]).then_inc(load_sem("b1f1"), 16)
            sp.dma_start(gw1[:, :], t["gw1"]).then_inc(load_sem("gw1"), 16)
            sp.dma_start(fgb[:, :], t["fgb"]).then_inc(load_sem("fgb"), 16)
            sp.dma_start(iota8[:, :, :], t["iota8"]).then_inc(load_sem("iota8"), 16)
            s0 = load_sem("sort")
            sp.dma_start(triu[:, :], t["triu"]).then_inc(s0, 16)
            sp.dma_start(it256[:, :], t["it256"]).then_inc(s0, 16)
            sp.dma_start(region[:, :], t["region"]).then_inc(s0, 16)
            sp.wait_ge(t_zm, 1)
            zr = scx.rearrange("(n p c) d -> n p (c d)", p=128, c=ZC)
            for i in range(NZ):
                sp.dma_start(zr[i, :, :], zer[:, :]).then_inc(t_z, 16)
            s0 = load_sem("lang")
            sp.wait_ge(p_no, B)
            for b in range(B):
                r = sp.value_load(lid[0:1, b:b + 1], min_val=0, max_val=LANGS - 1)
                sp.dma_start(cw1[:, b, :], t["cw1"][bass.ds(r, 1), :, :].rearrange("a p c -> p (a c)")).then_inc(s0, 16)
                sp.dma_start(cb1[:, b:b + 1], t["cb1"][bass.ds(r, 1), :].rearrange("a p -> p a")).then_inc(s0, 16)
                sp.dma_start(cw2[:, b, :], t["cw2"][bass.ds(r, 1), :, :].rearrange("a p c -> p (a c)")).then_inc(s0, 16)
                sp.dma_start(gbc[:, b, :], t["gbc"][bass.ds(r, 1), :].to_broadcast([128, 2 * D])).then_inc(s0, 16)

        at("sp", 14, sp_later)

        def pe_prologue(pe):
            pe.wait_ge(ld["c0"], 48)
            for g in range(NG):
                pe.wait_ge(ld[f"x{g}"], 16)
                pe.matmul(bank[g][0:A, :], w1c[:, :], acc[:, g * 512:g * 512 + 512], start=True, stop=True).then_inc(p_at, 1)
            pe.wait_ge(p_v, 1)
            for b in range(B):
                pe.wait_ge(p_th, b // 2 + 1)
                last = pe.matmul(bank[4][0:B, 0:S], vz[:, B - 1 - b:2 * B - 1 - b], attn[:, b * S:b * S + S],
                                 start=(b == 0), stop=(b == B - 1))
            last.then_inc(p_sc, 1)
            pe.wait_ge(ld["ident"], 16)
            pe.wait_ge(p_row, 1)
            for l in range(2):
                last = pe.transpose(bank[5][:, l * B:l * B + B], rows[:, l * 128:l * 128 + 128], ident[0:B, 0:B])
            last.then_inc(p_sc, 1)
            pe.wait_ge(p_m, 1)
            pe.wait_ge(ld["identb"], 16)
            for b in range(B):
                pe.wait_ge(ld[f"mask{b}"], 16)
                if b >= 4:
                    pe.wait_ge(p_ex, 2 * (b - 3))
                o = bank[b % 4][:, :]
                sl = selr[:, b * 128:b * 128 + 128]
                pe.matmul(o, sl, mh[:, :, :].rearrange("b c s -> b (c s)"), start=True, stop=False)
                pe.matmul(o, sl, ml[:, :, :].rearrange("b c s -> b (c s)"), start=False, stop=False)
                pe.matmul(o, identb[:, :], maskt[:, b, 0:512], start=False, stop=True).then_inc(p_pm, 1)

        def pooled(b):
            def fn(pe):
                o = misc_bank(pe, ("po", b))
                if b == 0:
                    pe.wait_ge(ld["xtm"], 16)
                    pe.wait_ge(p_one, 2)
                pe.wait_ge(p_ex, 2 * b + 2)
                for j in range(2):
                    for l in range(2):
                        last = pe.matmul(o[:, j * 256:j * 256 + D + 1], ET(b)[:, l * S + j * 128:l * S + j * 128 + 128],
                                         xtm[:, 2 * b + l, :], start=(l == 0), stop=(l == 1))
                last.then_inc(p_po, 1)
            return fn

        def trans(b):
            def fn(pe):
                o = misc_bank(pe, ("pt", b))
                pe.wait_ge(p_no, b + 1)
                for j in range(2):
                    last = pe.transpose(o[:, j * 128:j * 128 + 128], ptm[:, b % 2, j * 128:j * 128 + 128], ident[:, :])
                last.then_inc(p_tr, 1)
            return fn

        def logit(b):
            def fn(pe):
                o = misc_bank(pe, ("pl", b))
                if b == 0:
                    pe.wait_ge(ld["gw0"], 16)
                pe.wait_ge(p_ev, b + 1)
                for j in range(2):
                    last = pe.matmul(o[:, j * E:j * E + E], pT[:, b % 2, j * 128:j * 128 + 128], gw0[:, :],
                                     start=True, stop=True)
                last.then_inc(p_lg, 1)
            return fn

        def evac(b):
            def fn(act):
                act.wait_ge(p_tr, b + 1)
                if b >= 2:
                    act.wait_ge(p_lg, b - 1)
                    act.wait_ge(p_x, b - 1)
                act.activation(pT[:, b % 2, :], bank[mb[("pt", b)][0]][:, 0:256], ACT.Copy).then_inc(p_ev, 1)
            return fn

        def norm(b):
            def fn(dve):
                def ln(ins):
                    link(dve, "dve", ins)
                pb = bank[mb[("po", b)][0]]
                dve.wait_ge(p_po, b + 1)
                if b >= 2:
                    dve.wait_ge(p_tr, b - 1)
                ln(dve.tensor_tensor(rr[:, b % 2, 0, :], pb[:, D:512:256], maskt[:, b, 512:514], ALU.mult))
                ln(dve.reciprocal(rr[:, b % 2, 1, :], rr[:, b % 2, 0, :]))
                for j in range(2):
                    last = dve.tensor_scalar(ptm[:, b % 2, j * 128:j * 128 + 128], pb[:, j * 256:j * 256 + D],
                                             rr[:, b % 2, 1, j:j + 1], None, ALU.mult)
                last.then_inc(p_no, 1)
            return fn

        def xsplit(b):
            def fn(dve):
                dve.wait_ge(p_ev, b + 1)
                o_h = xh[:, b // 4, (b % 4) * S:(b % 4) * S + S]
                o_l = xl[:, b // 4, (b % 4) * S:(b % 4) * S + S]
                link(dve, "dve", dve.tensor_copy(o_h, pT[:, b % 2, :]))
                dve.tensor_tensor(o_l, pT[:, b % 2, :], o_h.bitcast(F32), ALU.subtract).then_inc(p_x, 1)
            return fn

        def logcopy(b):
            def fn(dve):
                dve.wait_ge(p_lg, b + 1)
                dve.tensor_copy(L32[:, 2 * b * E:2 * b * E + 2 * E], bank[mb[("pl", b)][0]][:, 0:2 * E]).then_inc(p_lc, 1)
            return fn

        at("pe", -100, pe_prologue)
        for b in range(B):
            p = PB[b]
            at("pe", mpos[("po", b)], pooled(b))
            at("dve", p + PD[0], norm(b))
            at("pe", mpos[("pt", b)], trans(b))
            at("act", p + PD[2], evac(b))
            at("dve", p + PD[3], xsplit(b))
            at("pe", mpos[("pl", b)], logit(b))
            at("dve", p + PD[5], logcopy(b))

        def act_prologue(act):
            act.wait_ge(ld["c0"], 48)
            for g in range(NG):
                act.wait_ge(p_at, g + 1)
                act.activation(attn[:, g * 512:g * 512 + 512], bank[g][0:A, :], ACT.Tanh, bias=b1c[:, :]).then_inc(p_th, 1)
            act.wait_ge(p_col, 1)
            for i in range(B):
                act.wait_ge(p_pm, i + 1)
                for l in range(2):
                    act.activation(ET(i)[:, l * S:l * S + S], bank[i % 4][:, l * S:l * S + S], ACT.Exp,
                                   bias=scol[:, l * B + i:l * B + i + 1], scale=-1.0).then_inc(p_ex, 1)
            act.wait_ge(ld["b1f0"], 16)

        at("act", -100, act_prologue)

        def dve_prologue(dve):
            def ln(ins):
                link(dve, "dve", ins)
            dve.memset(onesb[:, :], 1.0).then_inc(p_one, 1)
            ln(dve.memset(vz[:, :], 0.0))
            dve.memset(xtm[:, :, D:D + 1], 1.0).then_inc(p_one, 1)
            dve.wait_ge(ld["c0"], 48)
            dve.tensor_copy(vz[:, B - 1:B], vc[:, :]).then_inc(p_v, 1)
            dve.memset(pre[:, 0:1], -BIG)
            dve.memset(suf[:, S + 1:S + 2], -BIG)
            dve.wait_ge(ld["ty"], 16)
            dve.tensor_scalar(is_t[:, 0:1], ty[:, :], 0.0, None, ALU.is_equal)
            ln(dve.tensor_scalar(is_t[:, 1:2], ty[:, :], 1.0, None, ALU.is_equal))
            ln(dve.tensor_tensor(is_t[:, 3:4], is_t[:, 0:1], is_t[:, 1:2], ALU.add))
            ln(dve.tensor_scalar(is_t[:, 2:3], is_t[:, 3:4], -1.0, 1.0, ALU.mult, ALU.add))
            dve.wait_ge(p_sc, 1)
            dve.tensor_copy(rows, bank[4][0:B, 0:S]).then_inc(p_row, 1)
            dve.wait_ge(p_row, 1)
            ln(dve.tensor_tensor_scan(pre[:, 1:S + 1], rows[:, :], rows[:, :], -BIG, ALU.max, ALU.max))
            ln(dve.tensor_tensor_scan(suf[:, S:0:-1], rows[:, ::-1], rows[:, ::-1], -BIG, ALU.max, ALU.max))
            dve.wait_ge(p_sc, 2)
            dve.tensor_copy(scol[:, :], bank[5][:, 0:NT]).then_inc(p_col, 1)
            ln(dve.tensor_tensor(cl[:, :], pre[:, 0:S], suf[:, 2:S + 2], ALU.max))
            ln(dve.tensor_scalar(cl[:, :], cl[:, :], is_t[:, 2:3], None, ALU.mult))
            ln(dve.scalar_tensor_tensor(cl[:, :], pre[:, 1:S + 1], is_t[:, 0:1], cl[:, :], ALU.mult, ALU.add))
            ln(dve.scalar_tensor_tensor(mrow, suf[:, 1:S + 1], is_t[:, 1:2], cl[:, :], ALU.mult, ALU.add))
            dve.wait_ge(ld["sel"], 16)
            mr2 = mrow.unsqueeze(1).to_broadcast([B, 2, S])
            dve.tensor_copy(selr[:, :], sel)
            ln(dve.tensor_copy(mh[:, :, :], mr2))
            dve.tensor_tensor(ml[:, :, :], mr2, mh[:, :, :].bitcast(F32), ALU.subtract).then_inc(p_m, 1)

        at("dve", -100, dve_prologue)

        NALL = N * E
        T_POS = NALL - KTH + 1

        def bis_count(r):
            def fn(dve):
                def ln(ins):
                    link(dve, "dve", ins)
                if r == 0:
                    dve.wait_ge(ld["bitc"], 16)
                    dve.wait_ge(p_lc, B)
                    dve.tensor_scalar(junk[:, 0, :], L32[:, :], 0.0, None, ALU.is_ge, ALU.add, accum_out=cnt3[:, 0, 0:1])\
                        .then_inc(b_cnt, 1)
                    return
                dve.wait_ge(b_upd, r)
                for i in range(3 if r > 1 else 1):
                    last = dve.tensor_scalar(junk[:, i, :], L2[:, :], cand[:, i:i + 1].bitcast(F32), None, ALU.is_ge,
                                             ALU.add, accum_out=cnt3[:, r % 2, i:i + 1])
                last.then_inc(b_cnt, 1)
            return fn

        def bis_sum(r):
            def fn(pe):
                o = misc_bank(pe, ("bis", r))
                if r == 0:
                    pe.wait_ge(p_one, 1)
                pe.wait_ge(b_cnt, r + 1)
                n = 3 if r > 1 else 1
                pe.matmul(o[:, 0:n], onesb[:, :], cnt3[:, r % 2, 0:n], start=True, stop=True).then_inc(b_sum, 1)
            return fn

        def bis_update(r):
            def fn(dve):
                def ln(ins):
                    link(dve, "dve", ins)
                o = bank[mb[("bis", r)][0]]
                dve.wait_ge(b_sum, r + 1)
                if r == 0:
                    ln(dve.tensor_scalar(bis[:, 0:1], o[:, 0:1], float(T_POS), None, ALU.is_lt))
                    ln(dve.tensor_scalar(bis[:, 1:2], bis[:, 0:1], -2.0, 1.0, ALU.mult, ALU.add))
                    ln(dve.tensor_scalar(bis[:, 2:3], bis[:, 0:1], float(KTH - T_POS), float(T_POS), ALU.mult, ALU.add))
                    ln(dve.tensor_scalar(L2[:, :], L32[:, :], bis[:, 1:2], None, ALU.mult))
                    ln(dve.memset(cur_i[:, :], 0))
                    dve.tensor_copy(cand[:, 0:3], bitc[:, 0:3]).then_inc(b_upd, 1)
                    return
                n = 3 if r > 1 else 1
                shift = 30 if r == 1 else 30 - 2 * (r - 1)
                ln(dve.tensor_scalar(bisj[:, 0:n], o[:, 0:n], bis[:, 2:3], None, ALU.is_ge, ALU.add,
                                     accum_out=bis[:, 3:4]))
                ln(dve.tensor_scalar(inc_i[:, :], bis[:, 3:4], float(2 ** shift), None, ALU.mult))
                ln(dve.tensor_tensor(cur_i[:, r % 2:r % 2 + 1], cur_i[:, (r + 1) % 2:(r + 1) % 2 + 1], inc_i[:, :],
                                     ALU.bitwise_or))
                if r < 16:
                    dve.tensor_tensor(cand[:, 0:3], bitc[:, 3 * r:3 * r + 3],
                                      cur_i[:, r % 2:r % 2 + 1].to_broadcast([128, 3]), ALU.bitwise_or)\
                        .then_inc(b_upd, 1)
                else:
                    ln(dve.tensor_scalar(bis[:, 4:5], cur_i[:, 0:1].bitcast(F32), bis[:, 1:2], None, ALU.mult))
                    dve.scalar_tensor_tensor(G0[:, :], L32[:, :], bis[:, 4:5], L32[:, :], ALU.is_ge, ALU.mult)\
                        .then_inc(b_upd, 1)
            return fn

        for r in range(17):
            at("dve", B0 + 2 * r, bis_count(r))
            at("pe", mpos[("bis", r)], bis_sum(r))
            at("dve", B0 + 2 * r + 1.9, bis_update(r))

        def gates0_T(pe):
            o = misc_bank(pe, ("gT0", 0))
            pe.wait_ge(b_upd, 17)
            pe.transpose(o[:, 0:128], G0[:, :], ident[:, :]).then_inc(b_gt, 1)

        def gates0_ev(act):
            act.wait_ge(b_gt, 1)
            act.activation(gT0[:, :], bank[mb[("gT0", 0)][0]][:, 0:128], ACT.Copy).then_inc(b_ev, 1)

        def gates0_out(sp):
            sp.wait_ge(b_ev, 1)
            sp.dma_start(scr[0].rearrange("t e p -> (t e) p"), gT0[:, :]).then_inc(s_scr, 16)
            sp.wait_ge(s_scr, 16)
            sp.dma_start(gTb[:, :].rearrange("e (t p) -> e t p", p=128), scr[0].rearrange("t e p -> e t p"))\
                .then_inc(s_gtb[0], 16)

        at("pe", PG, gates0_T)
        at("act", PG, gates0_ev)
        at("sp", PG + 1, gates0_out)

        b2_order = [v for _, k, v in terms if k == "b2"]

        def b2_mm(v):
            layer, g = v

            def fn(pe):
                o = misc_bank(pe, ("b2", v))
                pe.wait_ge(ld[f"b2f{layer}"], 16)
                pe.wait_ge(s_gtb[0] if layer == 0 else s_gtb[1 + g], 16)
                pe.matmul(o[:, :], b2f[layer][:, :], gTb[:, g * 512:g * 512 + 512], start=True, stop=True)\
                    .then_inc(b_b2, 1)
            return fn

        for v in b2_order:
            at("pe", mpos[("b2", v)], b2_mm(v))

        def mid(g):
            m = M0[g]

            def pe_h(pe):
                o = misc_bank(pe, ("h", g))
                if g == 0:
                    pe.wait_ge(ld["lang"], 16 * 4 * B)
                pe.wait_ge(s_acc, done0[g])
                for i in range(2):
                    b = 2 * g + i
                    last = pe.matmul(o[0:A, i * S:i * S + S], cw1[:, b, :], acc[:, b * S:b * S + S], start=True, stop=True)
                last.then_inc(m_h, 1)

            def act_h(act):
                o = bank[mb[("h", g)][0]]
                act.wait_ge(m_h, g + 1)
                if g == 0:
                    act.wait_ge(ld["lang"], 16 * 4 * B)
                else:
                    act.wait_ge(m_xa, g)
                for i in range(2):
                    b = 2 * g + i
                    act.activation(hTs[0:A, i * S:i * S + S], o[0:A, i * S:i * S + S], ACT.Relu,
                                   bias=cb1[:, b:b + 1]).then_inc(m_hs, 1)

            def pe_xa(pe):
                o = misc_bank(pe, ("xa", g))
                pe.wait_ge(m_one, 1)
                pe.wait_ge(m_hs, 2 * g + 2)
                for i in range(4):
                    c = g * 512 + i * 128
                    pe.matmul(o[:, i * 128:i * 128 + 128], acc[:, c:c + 128], ident[:, :], start=True, stop=False)
                    last = pe.matmul(o[:, i * 128:i * 128 + 128], hTs[:, i * 128:i * 128 + 128],
                                     cw2[:, 2 * g + i // 2, :], start=False, stop=True)
                last.then_inc(m_xa, 1)

            def stats(src, k, done, ready):
                def each(dve):
                    ready(dve)
                    for i in range(4):
                        last = dve.bn_stats(st[:, i, :], src[:, i * 128:i * 128 + 128])
                    return last

                def join(dve):
                    for i in range(4):
                        last = dve.bn_aggr(mv[:, k, i, :], st[:, i, :])
                    last.then_inc(done, 1)
                return [each, join]

            def ready1(dve):
                dve.wait_ge(m_xa, g + 1)
                if g:
                    dve.wait_ge(m_mv2, g)
                    dve.wait_ge(m_n1, g)

            def rstd(k, ready, done):
                def fn(pool):
                    pool.wait_ge(ready, g + 1)
                    link(pool, "pool", pool.tensor_scalar(rs[:, k, :], mv[:, k, :, 1], EPS, None, ALU.add))
                    pool.tensor_tensor(rs[:, k, :], rs[:, k, :], mhalf[:, :], ALU.pow).then_inc(done, 1)
                return fn

            def dve_n1(dve):
                o = bank[mb[("xa", g)][0]]
                dve.wait_ge(m_rs, g + 1)
                if g:
                    dve.wait_ge(m_x2, g)
                for i in range(4):
                    last = dve.tensor_scalar(n1[:, i * 128:i * 128 + 128], o[:, i * 128:i * 128 + 128],
                                             mv[:, 0, i, 0:1], rs[:, 0, i:i + 1], ALU.subtract, ALU.mult)
                last.then_inc(m_n1, 1)

            def pool_x2(pool):
                pool.wait_ge(m_n1, g + 1)
                if g == 0:
                    pool.wait_ge(ld["lang"], 16 * 4 * B)
                else:
                    pool.wait_ge(m_x2T, g)
                    pool.wait_ge(m_n2, g)
                for i in range(2):
                    b = 2 * g + i
                    v3 = n1[:, i * S:i * S + S].rearrange("p (t d) -> p t d", t=2)
                    last = pool.tensor_tensor(v3, v3, gbc[:, b:b + 1, 0:D].to_broadcast([128, 2, D]), ALU.mult)
                link(pool, "pool", last)
                for i in range(2):
                    b = 2 * g + i
                    v3 = n1[:, i * S:i * S + S].rearrange("p (t d) -> p t d", t=2)
                    o3 = x2[:, i * S:i * S + S].rearrange("p (t d) -> p t d", t=2)
                    last = pool.tensor_tensor(o3, v3, gbc[:, b:b + 1, D:2 * D].to_broadcast([128, 2, D]), ALU.add)
                last.then_inc(m_x2, 1)

            def ready2(dve):
                dve.wait_ge(m_x2, g + 1)
                dve.wait_ge(m_mv, g + 1)
                if g:
                    dve.wait_ge(m_n2, g)

            n2 = n2A[:, 4 * (g % GA):4 * (g % GA) + 4, :].rearrange("p t d -> p (t d)")

            def dve_n2(dve):
                dve.wait_ge(m_rs2, g + 1)
                if g == GA:
                    dve.wait_ge(t_sc, 16 * 2 * TA)
                for i in range(4):
                    last = dve.tensor_scalar(n2[:, i * 128:i * 128 + 128], x2[:, i * 128:i * 128 + 128],
                                             mv[:, 1, i, 0:1], rs[:, 1, i:i + 1], ALU.subtract, ALU.mult)
                last.then_inc(m_n2, 1)

            def pe_x2T(pe):
                o = misc_bank(pe, ("x2T", g))
                pe.wait_ge(m_x2, g + 1)
                for i in range(4):
                    last = pe.transpose(o[:, i * 128:i * 128 + 128], x2[:, i * 128:i * 128 + 128], ident[:, :])
                last.then_inc(m_x2T, 1)

            def pe_nT(pe):
                o = misc_bank(pe, ("nT", g))
                pe.wait_ge(m_n2, g + 1)
                for i in range(4):
                    last = pe.transpose(o[:, i * 128:i * 128 + 128], n2[:, i * 128:i * 128 + 128], ident[:, :])
                last.then_inc(m_nT, 1)

            def act_xn(act):
                o = bank[mb[("nT", g)][0]]
                if g == 0:
                    act.wait_ge(ld["fgb"], 16)
                else:
                    act.wait_ge(m_lg, g)
                act.wait_ge(m_nT, g + 1)
                act.activation(xn32[:, :], o[:, :], ACT.Identity, bias=fgb[:, 1:2], scale=fgb[:, 0:1]).then_inc(m_xn, 1)

            def dve_split(dve):
                dve.wait_ge(m_xn, g + 1)
                link(dve, "dve", dve.tensor_scalar(xbh[:, :], xn32[:, :], XS, None, ALU.mult))
                dve.scalar_tensor_tensor(xbl[:, :], xn32[:, :], XS, xbh[:, :], ALU.mult, ALU.subtract).then_inc(m_sp, 1)

            def pe_lg(pe):
                o = misc_bank(pe, ("lg", g))
                if g == 0:
                    pe.wait_ge(ld["gw1"], 16)
                pe.wait_ge(m_xn, g + 1)
                for i in range(4):
                    last = pe.matmul(o[:, i * E:i * E + E], xn32[:, i * 128:i * 128 + 128], gw1[:, :], start=True, stop=True)
                last.then_inc(m_lg, 1)

            def dve_d(dve):
                o = bank[mb[("lg", g)][0]][:, 0:32].rearrange("p (t e) -> p t e", t=4)
                dve.wait_ge(m_lg, g + 1)
                link(dve, "dve", dve.tensor_reduce(c4[:, :, 0], o, AX.X, ALU.max))
                dve.tensor_tensor(lg[:, :, :], o, c4[:, :, 0:1].to_broadcast([128, 4, E]), ALU.subtract).then_inc(m_d, 1)

            def act_exp(act):
                act.wait_ge(m_d, g + 1)
                act.activation(ex[:, :, :], lg[:, :, :], ACT.Exp).then_inc(m_e, 1)

            def top():
                sl = slice(4 * g, 4 * g + 4)
                parts = []

                def part(fn):
                    parts.append(fn)

                @part
                def _(dve):
                    dve.wait_ge(m_e, g + 1)
                    if g == 0:
                        dve.wait_ge(ld["iota8"], 16)
                    else:
                        dve.wait_ge(m_cT, g)
                    return dve.tensor_reduce(c4[:, :, 1], ex[:, :, :], AX.X, ALU.add)

                @part
                def _(dve):
                    return dve.reciprocal(c4[:, :, 2], c4[:, :, 1])

                @part
                def _(dve):
                    return dve.tensor_tensor(pr[:, :, :], ex[:, :, :], c4[:, :, 2:3].to_broadcast([128, 4, E]), ALU.mult)

                @part
                def _(dve):
                    for i in range(4):
                        last = dve.max(mx8[:, i, :], pr[:, i, :])
                    return last

                @part
                def _(dve):
                    for i in range(4):
                        dve.max_index(ix8[:, i, :], mx8[:, i, :], pr[:, i, :])
                    return dve.tensor_tensor(c4[:, :, 3], mx8[:, :, 0], mx8[:, :, 1], ALU.add)

                @part
                def _(dve):
                    dve.tensor_copy(ixf[:, :, :], ix8[:, :, :])
                    return dve.reciprocal(c4[:, :, 4], c4[:, :, 3])

                @part
                def _(dve):
                    for k in range(2):
                        dve.tensor_tensor(oh[:, k, :, :], iota8[:, :, :], ixf[:, :, k:k + 1].to_broadcast([128, 4, E]),
                                          ALU.is_equal)
                    return dve.tensor_tensor(wk[:, :, :], mx8[:, :, 0:2], c4[:, :, 4:5].to_broadcast([128, 4, 2]), ALU.mult)

                if g < GA:
                    @part
                    def _(dve):
                        dve.tensor_copy(OH[:, :, sl, :].rearrange("p k t e -> p k (t e)"),
                                        oh[:, :, :, :].rearrange("p k t e -> p k (t e)"))
                        dve.tensor_copy(wA[:, sl, :], wk[:, :, :])
                        if g == 0:
                            dve.memset(cumb[:, 0, :], 0.0)
                        return dve.tensor_tensor(OB[:, sl, :], oh[:, 0, :, :], oh[:, 1, :, :], ALU.add)

                    for i in range(4 * g, 4 * g + 4):
                        @part
                        def _(dve, i=i):
                            return dve.tensor_tensor(cumb[:, i + 1, :], cumb[:, i, :], OB[:, i, :], ALU.add)

                @part
                def _(dve):
                    for k in range(2):
                        last = dve.tensor_tensor(oh[:, k, :, :], oh[:, k, :, :], wk[:, :, k:k + 1].to_broadcast([128, 4, E]),
                                                 ALU.mult)
                    return last

                @part
                def _(dve):
                    dve.tensor_tensor(cw[:, :, :], oh[:, 0, :, :], oh[:, 1, :, :], ALU.add).then_inc(m_cw, 1)
                return parts

            def pe_cT(pe):
                o = misc_bank(pe, ("cT", g))
                pe.wait_ge(m_cw, g + 1)
                pe.transpose(o[0:32, 0:128], cw[:, :, :].rearrange("p t e -> p (t e)"), ident[:, :]).then_inc(m_cT, 1)

            def act_cE(act):
                act.wait_ge(m_cT, g + 1)
                if g:
                    act.wait_ge(s_scr1[g - 1], 16)
                act.activation(cwT[:, :], bank[mb[("cT", g)][0]][0:32, 0:128], ACT.Copy).then_inc(m_cE, 1)

            def sp_gates(sp):
                sp.wait_ge(m_cE, g + 1)
                sp.dma_start(scr[1][4 * g:4 * g + 4, :, :].rearrange("t e p -> (t e) p"), cwT[:, :]).then_inc(s_scr1[g], 16)

            def sp_gtb(sp):
                sp.wait_ge(s_scr1[g], 16)
                sp.wait_ge(b_b2, b2_order.index((0, g)) + 1)
                sp.dma_start(gTb[:, g * 512:g * 512 + 512].rearrange("e (t p) -> e t p", p=128),
                             scr[1][4 * g:4 * g + 4, :, :].rearrange("t e p -> e t p")).then_inc(s_gtb[1 + g], 16)

            at("pe", mpos[("h", g)], pe_h)
            at("act", m + 0.8, act_h)
            at("pe", mpos[("xa", g)], pe_xa)
            spread("dve", "dve", m + 2.8, 0.15, stats(bank[mb[("xa", g)][0]], 0, m_mv, ready1))
            at("pool", m + 4.5, rstd(0, m_mv, m_rs))
            at("dve", m + 6.0, dve_n1)
            at("pool", m + 6.5, pool_x2)
            spread("dve", "dve", m + 9.8, 0.15, stats(x2, 1, m_mv2, ready2))
            at("pool", m + 11.0, rstd(1, m_mv2, m_rs2))
            at("dve", m + 12.6, dve_n2)
            at("pe", mpos[("x2T", g)], pe_x2T)
            at("pe", mpos[("nT", g)], pe_nT)
            at("act", m + 15.2, act_xn)
            if g == GA:
                at("dve", m + 16.5, dve_split)
            at("pe", mpos[("lg", g)], pe_lg)
            at("dve", m + 17.1, dve_d)
            at("act", m + 18.5, act_exp)
            spread("dve", "dve", m + 19.5, 0.15, top())
            at("pe", mpos[("cT", g)], pe_cT)
            at("act", m + 22.6, act_cE)
            at("sp", m + 23, sp_gates)
            at("sp", m + 26, sp_gtb)

        for g in range(NG):
            mid(g)

        def pe_rank(g):
            def fn(pe):
                o = misc_bank(pe, ("rk", g))
                pe.wait_ge(m_cw, g + 1)
                pe.wait_ge(ld["sort"], 48)
                sl = slice(4 * g, 4 * g + 4)
                pe.matmul(o[:, 0:4 * E], triu[:, :], OB[:, sl, :].rearrange("p t e -> p (t e)"), start=True, stop=False)
                last = pe.matmul(o[:, 0:4 * E], onesb[:, :], cumb[:, sl, :].rearrange("p t e -> p (t e)"),
                                 start=False, stop=True)
                if g == GA - 1:
                    last = pe.matmul(o[:, 4 * E:5 * E], onesb[:, :], cumb[:, TA, :], start=True, stop=True)
                last.then_inc(t_rk, 1)
            return fn

        def rank(g):
            sl = slice(4 * g, 4 * g + 4)

            def add_region(dve):
                dve.wait_ge(t_rk, g + 1)
                if g == 0:
                    dve.wait_ge(ld["sort"], 48)
                o = bank[mb[("rk", g)][0]]
                return dve.tensor_tensor(rk4[:, :, :], o[:, 0:4 * E].rearrange("p (t e) -> p t e", e=E),
                                         region[:, :].unsqueeze(1).to_broadcast([128, 4, E]), ALU.add)

            def chosen(dve):
                for k in range(2):
                    last = dve.tensor_tensor(oh2[:, k, :, :], OH[:, k, sl, :], rk4[:, :, :], ALU.mult)
                return last

            def total(dve):
                return dve.tensor_reduce(pk[:, :, sl], oh2[:, :, :, :], AX.X, ALU.add)

            def whole(dve):
                dve.tensor_copy(idx[:, :, sl], pk[:, :, sl]).then_inc(t_ix, 1)
            return [add_region, chosen, total, whole]

        tile_parts = []

        def tiles(fn):
            tile_parts.append(fn)

        @tiles
        def _(dve):
            dve.wait_ge(t_zm, 1)
            dve.wait_ge(t_rk, GA)
            return dve.tensor_scalar(ci[:, :], bank[mb[("rk", GA - 1)][0]][:, 4 * E:5 * E], float(TS - 1), None, ALU.add)

        @tiles
        def _(dve):
            return dve.tensor_scalar(ci[:, :], ci[:, :], -TS, None, ALU.bitwise_and)

        @tiles
        def _(dve):
            return dve.tensor_copy(e8[:, 0, :], ci[:, :])

        @tiles
        def _(dve):
            dve.tensor_scalar(e8[:, 2, :], e8[:, 0, :], -1.0, float(CAP), ALU.mult, ALU.add)
            return dve.tensor_tensor_scan(e8[:, 1, :], e8[:, 0, :], zer[:, 0:E], 0.0, ALU.add, ALU.add)

        @tiles
        def _(dve):
            return dve.tensor_tensor(cmp_[:, :, :], e8[:, 1:2, :].to_broadcast([128, NTL, E]),
                                     it256[:, :].unsqueeze(2).to_broadcast([128, NTL, E]), ALU.is_le)

        @tiles
        def _(dve):
            dve.tensor_reduce(tef[:, 0, :], cmp_[:, :, :], AX.X, ALU.add)
            return dve.tensor_tensor(cmp2[:, :, :], cmp_[:, :, :], e8[:, 2:3, :].to_broadcast([128, NTL, E]), ALU.mult)

        @tiles
        def _(dve):
            return dve.tensor_reduce(tef[:, 1, :], cmp2[:, :, :], AX.X, ALU.add)

        @tiles
        def _(dve):
            dve.tensor_scalar(tei[:, 0, :], tef[:, 0, :], float(E - 1), 2048.0, ALU.min, ALU.mult)
            dve.tensor_scalar(tei[:, 1, :], tef[:, 0, :], float(E - 1), 4.0, ALU.min, ALU.mult)
            return dve.tensor_tensor(tef[:, 1, :], tef[:, 1, :], it256[:, :], ALU.add)

        @tiles
        def _(dve):
            dve.tensor_scalar(tei[:, 2, :], tef[:, 1, :], float(E * CAP), None, ALU.min).then_inc(t_te, 1)

        place_parts = []

        def places(fn):
            place_parts.append(fn)

        @places
        def _(dve):
            dve.wait_ge(t_te, 1)
            return dve.tensor_tensor(e8[:, 3, :], e8[:, 1, :], e8[:, 0, :], ALU.subtract)

        @places
        def _(dve):
            return dve.tensor_tensor(e8[:, 3, :], e8[:, 3, :], region[:, :], ALU.subtract)

        @places
        def _(dve):
            for k in range(2):
                last = dve.tensor_tensor(OH[:, k, :, :], OH[:, k, :, :], e8[:, 3:4, :].to_broadcast([128, TA, E]), ALU.mult)
            return last

        @places
        def _(dve):
            return dve.tensor_reduce(pk2[:, :, :], OH[:, :, :, :], AX.X, ALU.add)

        @places
        def _(dve):
            return dve.tensor_tensor(pk2[:, :, :], pk2[:, :, :], pk[:, :, :], ALU.add)

        @places
        def _(dve):
            dve.tensor_copy(idx2[:, :, :], pk2[:, :, :]).then_inc(t_pl, 1)

        def pool_scatter(g):
            def fn(pool):
                pool.wait_ge(t_ix, g + 1)
                pool.wait_ge(m_n2, g + 1)
                if g == 0:
                    pool.wait_ge(t_z, 16 * NZ)
                for i in range(4 * g, 4 * g + 4):
                    for k in range(2):
                        pool.indirect_dma_start(scx, bass.IndirectOffsetOnAxis(idx[:, k, i:i + 1], 0), n2A[:, i, :], None)\
                            .then_inc(t_sc, 16)
            return fn

        for g in range(GA):
            at("pe", mpos[("rk", g)], pe_rank(g))
            spread("dve", "dve", RK[g] + 1.2, 0.15, rank(g))
            at("pool", RK[g] + 2, pool_scatter(g))
        spread("dve", "dve", RK[GA - 1] + 1.75, 0.15, tile_parts)
        spread("dve", "dve", US + 12.3, 0.4, place_parts)

        def dve_fgs(dve):
            dve.wait_ge(ld["fgb"], 16)
            dve.tensor_scalar(fgs[:, :], fgb[:, :], XS, None, ALU.mult).then_inc(t_fg, 1)

        at("dve", 60.2, dve_fgs)

        def tile(i):
            p = tpos(i)

            def sp_in(sp):
                if i == 0:
                    sp.wait_ge(t_sc, 16 * 2 * TA)
                    sp.wait_ge(t_te, 1)
                    sp.wait_ge(s_w16, E)
                if i >= NX:
                    sp.wait_ge(t_tr, i - NX + 1)
                r = sp.value_load(tei[0:1, 2, i:i + 1], min_val=0, max_val=E * CAP)
                sp.dma_start(xr[:, i % NX, :, :], scx[bass.ds(r, TS), :].rearrange("(z p) d -> p z d", p=128))\
                    .then_inc(t_xr[i % NX], 16)

            def pe_t(pe):
                o = misc_bank(pe, ("t", i))
                pe.wait_ge(t_xr[i % NX], 16 * (i // NX + 1))
                for z in range(2):
                    last = pe.transpose(o[:, z * 128:z * 128 + 128], xr[:, i % NX, z, :], ident[:, :])
                last.then_inc(t_tr, 1)

            def act_x(act):
                if i == 0:
                    act.wait_ge(t_fg, 1)
                if i >= 2:
                    act.wait_ge(t_xl, i - 1)
                act.wait_ge(t_tr, i + 1)
                act.activation(xt32[:, i % 2, :], bank[mb[("t", i)][0]][:, 0:TS], ACT.Identity,
                               bias=fgs[:, 1:2], scale=fgs[:, 0:1]).then_inc(t_x32, 1)

            def dve_x(dve):
                dve.wait_ge(t_x32, i + 1)
                if i >= NX:
                    dve.wait_ge(s_m1, US + 2 * (i - NX) + 2)
                dve.tensor_copy(xth[:, i % NX, :], xt32[:, i % 2, :]).then_inc(t_xh, 1)

            def pool_x(pool):
                pool.wait_ge(t_xh, i + 1)
                pool.tensor_tensor(xtl[:, i % NX, :], xt32[:, i % 2, :], xth[:, i % NX, :], ALU.subtract).then_inc(t_xl, 1)

            def dve_y(dve):
                if i >= 2:
                    dve.wait_ge(t_ys[i % 2], 16 * (i // 2))
                dve.wait_ge(s_m2, US + 2 * i + 2)
                dve.tensor_scalar(yo[:, i % 2, :], bank[4 + res_of[("tile", i)] % 2][:, 0:2 * D], 1.0 / (WS * HS), None,
                                  ALU.mult).then_inc(t_yo, 1)

            def sp_out(sp):
                sp.wait_ge(t_yo, i + 1)
                sp.dma_start(scy[i * TS:i * TS + TS, :].rearrange("(z p) d -> p z d", p=128),
                             yo[:, i % 2, :].rearrange("p (z d) -> p z d", z=2)).then_inc(t_ys[i % 2], 16)

            at("sp", p - 1 if i < NX else tpos(i - NX) + 0.5, sp_in)
            at("pe", mpos[("t", i)], pe_t)
            at("act", p + 0.1, act_x)
            at("dve", p + 0.2, dve_x)
            at("pool", p + 0.3, pool_x)
            at("dve", US + 2 * i + 1 + LAG + 1.6, dve_y)
            at("sp", US + 2 * i + 1 + LAG + 1.7, sp_out)

        for i in range(NTL):
            tile(i)

        def gather(i, k):
            n = 2 * i + k

            def fn(pool):
                if n == 0:
                    for z in range(2):
                        pool.wait_ge(t_ys[z], 16 * ((NTL + 1 - z) // 2))
                    pool.wait_ge(t_pl, 1)
                    pool.wait_ge(s_m2, US)
                pool.indirect_dma_start(yg[:, n, :], None, scy, bass.IndirectOffsetOnAxis(idx2[:, k, i:i + 1], 0))\
                    .then_inc(t_yg[i], 16)
            return fn

        def weigh(i):
            def fn(dve):
                n = 2 * i
                if i >= 2:
                    dve.wait_ge(t_moe, i - 1)
                dve.wait_ge(t_yg[i], 32)
                dve.tensor_scalar(mo1[:, i % 2, :], yg[:, n, :], wA[:, i, 0:1], None, ALU.mult).then_inc(t_mo1, 1)
                dve.wait_ge(t_mo1, i + 1)
                n += 1
                dve.scalar_tensor_tensor(mo[:, i % 2, :], yg[:, n, :], wA[:, i, 1:2], mo1[:, i % 2, :],
                                         ALU.mult, ALU.add).then_inc(t_mo, 1)
            return fn

        def moe(i):
            g = i // 4

            def fn(pe):
                if i % 4 == 0:
                    o = misc_bank(pe, ("moe", g))
                    pe.wait_ge(s_gtb[1 + g], 16)
                    pe.wait_ge(ld["b2f1"], 16)
                else:
                    o = bank[mb[("moe", g)][0]]
                o = o[:, (i % 4) * 128:(i % 4) * 128 + 128]
                pe.wait_ge(t_mo, i + 1)
                pe.matmul(o, b2f[1][:, :], gTb[:, i * 128:i * 128 + 128], start=True, stop=False)
                pe.matmul(o, mo[:, i % 2, :], ident[:, :], start=False, stop=True).then_inc(t_moe, 1)
            return fn

        for i in range(TA):
            at("pool", MO + 1.6 * i, gather(i, 0))
            at("pool", MO + 1.6 * i + 0.8, gather(i, 1))
            at("dve", WP[i], weigh(i))
            at("pe", WP[i] + 3.0, moe(i))

        def pool_consts(pool):
            pool.memset(zer[:, :], 0.0).then_inc(t_zm, 1)
            pool.wait_ge(t_zm, 1)
            pool.memset(hTs[A:A + 1, :], 1.0).then_inc(m_one, 1)
            pool.wait_ge(m_one, 1)
            link(pool, "pool", pool.memset(mhalf[:, :], -0.5))

        at("pool", -99, pool_consts)

        def act_b1(act):
            act.wait_ge(ld["b1f1"], 16)

        at("act", 100, act_b1)

        def store(g):
            def fn(sp):
                sp.wait_ge(s_acc, done1[g])
                sp.dma_start(out[:, g * 512:g * 512 + 512], acc[:, g * 512:g * 512 + 512]).then_inc(s_out, 16)
            return fn

        for g in range(NG):
            at("sp", 1000 + g, store(g))

        def finish(sp):
            sp.wait_ge(s_out, 16 * NG)

        at("sp", 2000, finish)

        for q in Q.values():
            q.sort(key=lambda x: (x[0], x[1]))

        block = ctx.enter_context(nc.Block())

        @block.sync
        def _(eng):
            for _, _, fn in Q["sp"]:
                fn(eng)

        @block.tensor
        def _(eng):
            for _, _, fn in Q["pe"]:
                fn(eng)

        @block.scalar
        def _(eng):
            for _, _, fn in Q["act"]:
                fn(eng)

        @block.vector
        def _(eng):
            for _, _, fn in Q["dve"]:
                fn(eng)

        @block.gpsimd
        def _(eng):
            for _, _, fn in Q["pool"]:
                fn(eng)


def constants():
    def bf(v):
        return (np.ascontiguousarray(v, np.float32).view(np.uint32) >> 16).astype(np.uint16)

    l = np.arange(S)[:, None]
    j = np.arange(S)[None, :]
    allowed = np.stack([l <= j, l >= j, l != j])
    mask = np.where(allowed, 0.0, BIG).astype(np.float32)
    cnt = allowed.sum(axis=1).astype(np.float32)
    maskt = np.zeros((3, 128, 514), np.float32)
    for c in range(2):
        maskt[:, :, c * S:c * S + S] = mask[:, c * 128:c * 128 + 128, :]
        maskt[:, :, 2 * S + c] = cnt[:, c * 128:c * 128 + 128]
    sel = np.zeros((B, B, 128), np.float32)
    for b in range(B):
        sel[b, b, :] = 1.0
    bits = np.zeros((16, 3), np.int64)
    bits[0] = [1 << 30, 0, 0]
    for r in range(1, 16):
        bits[r] = [k << (30 - 2 * r) for k in (1, 2, 3)]
    return {
        "maskt": bf(maskt),
        "sel": sel.reshape(B, B * 128),
        "ident": np.eye(128, dtype=np.float32),
        "identb": bf(np.eye(128)),
        "bitc": np.broadcast_to(bits.reshape(1, 48).astype(np.int32), (128, 48)).copy(),
        "iota8": np.broadcast_to(np.arange(E, dtype=np.float32), (128, 4, E)).copy(),
        "triu": bf(np.triu(np.ones((128, 128)), 1)),
        "region": np.broadcast_to(CAP * np.arange(E, dtype=np.float32), (128, E)).copy(),
        "it256": np.broadcast_to(TS * np.arange(NTL, dtype=np.float32), (128, NTL)).copy(),
    }


def kernel(**inputs):
    import concourse.bacc as bacc
    from concourse.bass_utils import run_bass_kernel_spmd

    i = {k: np.asarray(v) for k, v in inputs.items()}
    c = np.ascontiguousarray
    x = i["x"].reshape(N, D)
    a = {
        "xT": c(x.T),
        "xtm": c(x.reshape(NT, 128, D).transpose(1, 0, 2)),
        "itype": i["itok_B_0_2"],
        "ilang": i["itok_B_0_8"],
        "w1c": i["L0_cond_W1"],
        "b1c": i["L0_cond_b1"].reshape(A, 1),
        "vc": i["L0_cond_v"].reshape(A, 1),
        "gw0": c(i["L0_ffn_gate_weight"].T),
        "b1_0": c(i["L0_ffn_b1"].reshape(E, 4, 128).transpose(2, 0, 1).reshape(128, 4 * E)),
        "w_0": c(np.concatenate([i["L0_ffn_w1"].transpose(2, 0, 1),
                                 i["L0_ffn_w2"].transpose(2, 0, 1).reshape(4, 128, E, D).transpose(1, 2, 0, 3)
                                 .reshape(128, E, 4 * D)], axis=2)),
        "b2_0": i["L0_ffn_b2"],
        "cw1": i["L1_cond_W1"],
        "cb1": i["L1_cond_b1"],
        "cw2": c(np.concatenate([i["L1_cond_W2"], i["L1_cond_b2"][:, None, :]], axis=1)),
        "gbc": c(np.concatenate([i["L1_cond_gamma"], i["L1_cond_beta"]], axis=1)),
        "gw1": i["L1_ffn_gate_w"],
        "b1_1": c(i["L1_ffn_b1"].reshape(E, 4, 128).transpose(2, 0, 1).reshape(128, 4 * E)),
        "w_1": c(np.concatenate([i["L1_ffn_w1"].transpose(1, 0, 2),
                                 i["L1_ffn_w2"].reshape(E, 4, 128, D).transpose(2, 0, 1, 3)
                                 .reshape(128, E, 4 * D)], axis=2)),
        "b2_1": i["L1_ffn_b2"],
        "fgb": c(np.stack([i["L1_ffn_gamma"], i["L1_ffn_beta"]], axis=1)),
    }
    a.update(constants())
    nc = bacc.Bacc("TRN2", target_bir_lowering=False, num_devices=1)
    arrays, t = {}, {}
    for name, v in a.items():
        v = c(v)
        arrays["in_" + name] = v
        t[name] = nc.dram_tensor("in_" + name, v.shape, mybir.dt.from_np(v.dtype), kind="ExternalInput").ap()
    for name in ("maskt", "identb", "triu"):
        t[name] = t[name].bitcast(BF16)
    out = nc.dram_tensor("out_T", [D, N], F32, kind="ExternalOutput").ap()
    build_adaln_ffn(nc, t, out)
    r = run_bass_kernel_spmd(nc, [arrays], core_ids=[0])
    return c(np.asarray(r.results[0]["out_T"]).T).reshape(B, S, D)
```

```python
import numpy as np
import concourse.bass as bass
from concourse import mybir
from contextlib import ExitStack

F32 = mybir.dt.float32
F32R = mybir.dt.float32r
BF16 = mybir.dt.bfloat16
F16 = mybir.dt.float16
I32 = mybir.dt.int32
U32 = mybir.dt.uint32
ACT = mybir.ActivationFunctionType
ALU = mybir.AluOpType
AX = mybir.AxisListType

B, S, D, E, H, A = 8, 256, 128, 8, 512, 32
N = B * S
NT = N // 128
NG = 4
LANGS = 10
KTH = 4 * 128 * 6
BIG = 1.0e30
EPS = 1e-5

GA = 3
TA = GA * 4
ZC = 7
TS = 256
NTL = GA * 512 * 2 // TS + E - 1
NZ = (E * GA * 512 + TS) // (128 * ZC)
CAP = GA * 512
WS, XS, HS = 64.0, 16.0, 8.0

AT = {
    "h": 0.75,
    "act_h": 1.1,
    "xa": 2.75,
    "stats": 2.8,
    "rstd": 4.0,
    "n1": 5.5,
    "x2": 7.5,
    "stats2": 8.5,
    "rstd2": 10.2,
    "n2": 13.3,
    "x2T": 13.0,
    "x2a": 13.9,
    "nT": 15.4,
    "xn": 15.8,
    "lg": 18.5,
    "d": 17.9,
    "exp": 18.2,
    "top": 18.4,
    "cT": 24.5,
    "rank": 21.7,
    "copied": 0.3,
    "rank0": 24.5,
    "x2d": 0.7,
    "rankd": 0.9,
    "scatter": 2.9,
    "kept0": 7.2,
    "term": 0.5,
    "lo": 1.4,
    "hia": 0.7,
    "m2": 1.2,
    "splitd": 3.5,
    "split": 1.9,
    "add": 1.5,
    "chains": -2.35,
    "batch": 1.5,
    "pt": 2.0,
    "pl": 4.0,
    "bis": 2.95,
    "upd": 0.9,
    "tile": 0.3,
    "tdve": 0.2,
    "yo": 1.3,
    "w16l": 3.4,
    "w16h": 1.7,
    "raw": 2.6,
    "weigh": 6.5,
    "moe": 2.2,
}
LAG = 3
NH = 4
NW = 4
NTMP = 3
NGS = 6
ND = 12
NX = 3


HURRY = {
    "stats": 2.8,
    "rstd": 3.3,
    "n1": 4.3,
    "stats2": 5.9,
    "rstd2": 5.7,
    "n2": 8.0,
    "x2T": 7.4,
    "x2a": 7.8,
    "nT": 9.6,
    "xn": 9.8,
    "lg": 12.4,
    "d": 12.0,
    "exp": 12.5,
    "top": 13.6,
    "rank": 16.0,
    "scatter": 2.0,
}


def step_order():
    out = []
    for p in range(2):
        out += [(0, e, g, e) for g in range(GA) for e in (2 * p, 2 * p + 1)]
    out += [(0, e, g, e) for g in range(GA) for e in range(4, 8)]
    out += [(0, e, 3, e) for e in range(4, 8)]
    out += [(0, e, 3, 8 + e) for e in range(4)]
    out += [(1, e, 3, None) for e in range(E)]
    return out


LOADS = [0, 1, 2, 3, 4, 5, 6, 7, 0, 1, 2, 3]
SLOT = [k % 4 for k in range(12)]
BEFORE = [None, None, None, None, 0, 1, 2, 3, 4, 5, 6, 7]
KEPT = 1.8
NWP = 8
W16 = 3.7
WARM = [52, 50]
SHARE = [1.0, 0.92, 1.0, 0.75, 0.8400000000000001]


def build_adaln_ffn(nc, t, out):
    STEPS = step_order()
    NS0 = 32
    US = 4 * NS0
    UD = US + 2 * NTL
    UNITS = [("dense", s, c) for s in range(NS0) for c in range(4)]
    UNITS += [("tile", i, h) for i in range(NTL) for h in range(2)]
    UNITS += [("dense", s, c) for s in range(NS0, NS0 + E) for c in range(4)]
    NU = len(UNITS)

    def unit0(s):
        return 4 * s if s < NS0 else UD + 4 * (s - NS0)

    RES = [("dense", s) for s in range(NS0)] + [("tile", i) for i in range(NTL)] + [("dense", s) for s in range(NS0, NS0 + E)]
    res_of = {x: q for q, x in enumerate(RES)}

    def last_unit(q):
        kind, v = RES[q]
        return unit0(v) + 3 if kind == "dense" else US + 2 * v + 1
    with ExitStack() as ctx:
        def sb(name, shape, dt=F32):
            return ctx.enter_context(nc.sbuf_tensor(name, shape, dt))

        def sem(name):
            return ctx.enter_context(nc.semaphore(name))

        scr = [nc.dram_tensor(f"gates{i}", [NT, E, 128], F32, kind="Internal").ap() for i in range(2)]

        acc = sb("acc", [128, N])
        first = sb("first", [128, E * 1024])
        w16 = first[:, :].bitcast(F16)
        ysv = first[:, 0:ND * 512].rearrange("p (s n) -> p s n", n=512)
        attn = first[0:A, 0:N]
        xtm = first[:, N:N + NT * (D + 1)].rearrange("p (t d) -> p t d", t=NT)
        f1 = N + NT * (D + 1)
        ETa = first[:, f1:f1 + 8 * S].rearrange("p (k s) -> p k s", k=4)
        ident = sb("ident", [128, 128])
        identb = sb("identb", [128, 128], BF16)
        gTb = sb("gTb", [E, N])
        sel = gTb[:, 0:B * 128]
        onesb = sb("onesb", [128, 128], BF16)
        mg = sb("mg", [128, B * 257])
        maskt = mg[:, :].bitcast(BF16).rearrange("p (b n) -> p b n", b=B)
        gbc = mg[:, 0:B * 2 * D].rearrange("p (b n) -> p b n", b=B)
        w1c = sb("w1c", [D, A])
        b1c = sb("b1c", [A, 1])
        vc = sb("vc", [A, 1])
        vz = sb("vz", [A, 2 * B - 1])
        ty = sb("ty", [B, 1], I32)
        lid = sb("lid", [1, B], I32)
        tyr = sb("tyr", [1, B], I32)
        is_t = sb("is_t", [B, 4])
        f0 = N + NT * (D + 1) + 8 * S
        rows = first[0:B, f0:f0 + S]
        pre = first[0:B, f0 + S:f0 + 2 * S + 2]
        suf = first[0:B, f0 + 2 * S + 2:f0 + 3 * S + 4]
        cl = first[0:B, f0 + 3 * S + 4:f0 + 4 * S + 4]
        mrow = first[0:B, f0 + 4 * S + 4:f0 + 5 * S + 4]
        scol = sb("scol", [128, NT])
        rr = sb("rr", [128, 2, 2, 2])
        Gs = sb("Gs", [128, NGS, 512])
        ptm = Gs[:, 0, :].rearrange("p (k n) -> p k n", k=2)
        pT = Gs[:, 1, :].rearrange("p (k n) -> p k n", k=2)

        def ET(b):
            return ETa[:, b, :] if b < 4 else Gs[:, b - 2, :]

        gw0 = sb("gw0", [D, E])
        gw1 = sb("gw1", [D, E])
        L32 = sb("L32", [128, NT * E])
        L2 = sb("L2", [128, NT * E])
        junk = sb("junk", [128, 3, NT * E], BF16)
        G0 = sb("G0", [128, NT * E])
        cnt3 = sb("cnt3", [128, 2, 4], BF16)
        bis = sb("bis", [128, 8])
        bisj = sb("bisj", [128, 4])
        inc_i = sb("inc_i", [128, 1], I32)
        cur_i = sb("cur_i", [128, 2], I32)
        cand = sb("cand", [128, 4], I32)
        bitc = sb("bitc", [128, 16 * 3], I32)
        gT0 = sb("gT0", [128, 128])
        b1f = [sb(f"b1f{i}", [128, 4 * E]) for i in range(2)]
        b2f = [sb(f"b2f{i}", [E, D]) for i in range(2)]
        xh = sb("xh", [128, 2, N // 2], F32R)
        xl = sb("xl", [128, 2, N // 2], F32R)
        selr = xh[0:B, 1, :]
        mh = xl[0:B, 1, 0:2 * S].rearrange("b (c s) -> b c s", c=2)
        ml = xl[0:B, 1, 2 * S:4 * S].rearrange("b (c s) -> b c s", c=2)
        xbh = sb("xbh", [128, 512], F16)
        xbl = sb("xbl", [128, 512], F16)
        h16 = sb("h16", [128, NH, 512], F16)
        l16 = sb("l16", [128, NH, 512], F16)
        scx = nc.dram_tensor("sorted_in", [E * CAP + TS, D], F32, kind="Internal").ap()
        scy = nc.dram_tensor("sorted_out", [NTL * TS, D], F32, kind="Internal").ap()
        n2A = sb("n2A", [128, TA, D])
        OH = sb("OH", [128, 2, TA, E])
        OB = sb("OB", [128, TA, E], BF16)
        wA = sb("wA", [128, TA, 2])
        triu = sb("triu", [128, 128], BF16)
        cumb = sb("cumb", [128, TA + 1, E], BF16)
        oh2 = sb("oh2", [128, 2, 4, E])
        rk4 = sb("rk4", [128, 4, E])
        region = sb("region", [128, E])
        zer = sb("zer", [128, ZC * D])
        e8 = sb("e8", [128, 4, E])
        ci = sb("ci", [128, E], I32)
        pk = sb("pk", [128, 2, TA])
        idx = sb("idx", [128, 2, TA], U32)
        pk2 = sb("pk2", [128, 2, TA])
        idx2 = sb("idx2", [128, 2, TA], U32)
        it256 = sb("it256", [128, NTL])
        cmp_ = sb("cmp_", [128, NTL, E])
        cmp2 = sb("cmp2", [128, NTL, E])
        tef = sb("tef", [128, 2, NTL])
        tei = sb("tei", [128, 3, NTL], I32)
        wraw = sb("wraw", [128, 2, 1024])
        wr = wraw[:, :, :].rearrange("p a n -> p (a n)")
        xr = wr[:, 0:NX * 256].rearrange("p (k z d) -> p k z d", k=NX, z=2)
        xt32 = wr[:, NX * 256:NX * 256 + 512].rearrange("p (k n) -> p k n", k=2)
        xth = sb("xth", [128, NX, TS], F16)
        xtl = sb("xtl", [128, NX, TS], F16)
        fgs = sb("fgs", [D, 2])
        yo = sb("yo", [128, 2, 2 * D])
        mo1 = sb("mo1", [128, 2, D])
        mo = sb("mo", [128, 2, D])
        wh = sb("wh", [128, NW, 1024], F32R)
        wl = sb("wl", [128, NW, 1024], F32R)
        yg = wh[:, 0:3, :].bitcast(F32).rearrange("p a (k d) -> p (a k) d", d=D)
        h32 = sb("h32", [128, NH, 512])
        hh = sb("hh", [128, NH, 512], F32R)
        hl = sb("hl", [128, NH, 512], F32R)
        tmp = sb("tmp", [128, NTMP, 512])
        cw1 = sb("cw1", [D, B, A])
        cb1 = sb("cb1", [A, B])
        cw2 = sb("cw2", [A + 1, B, D])
        fgb = sb("fgb", [D, 2])
        hTs = sb("hTs", [A + 1, 512])
        st = sb("st", [128, 4, 6])
        mv = sb("mv", [128, 2, 4, 2])
        rs = sb("rs", [128, 2, 4])
        mhalf = sb("mhalf", [128, 4])
        n1 = sb("n1", [128, 4 * D])
        x2 = sb("x2", [128, 4 * D])
        xn32 = sb("xn32", [128, 512])
        lg = sb("lg", [128, 4, E])
        ex = sb("ex", [128, 4, E])
        pr = sb("pr", [128, 4, E])
        wk = sb("wk", [128, 4, 2])
        c4 = sb("c4", [128, 4, 5])
        mx8 = sb("mx8", [128, 4, 8])
        ix8 = sb("ix8", [128, 4, 8], U32)
        ixf = sb("ixf", [128, 4, 8])
        iota8 = sb("iota8", [128, 4, E])
        oh = sb("oh", [128, 2, 4, E])
        cw = sb("cw", [128, 4, E])
        cwT = sb("cwT", [32, 128])

        bank = [ctx.enter_context(nc.psum_tensor(f"bank{i}", [128, 512], F32)) for i in range(8)]

        ld = {}

        def load_sem(name):
            ld[name] = sem("ld_" + name)
            return ld[name]

        s_m1 = sem("s_m1")
        s_g = sem("s_g")
        s_hia = sem("s_hia")
        s_hid = sem("s_hid")
        s_lo = sem("s_lo")
        s_m2 = sem("s_m2")
        s_ysv = sem("s_ysv")
        s_tmp = sem("s_tmp")
        s_tma = sem("s_tma")
        s_acc = sem("s_acc")
        s_w = sem("s_w")
        s_wv = sem("s_wv")
        s_wd = [sem(f"s_wd{i}") for i in range(NW)]
        s_w16h = sem("s_w16h")
        s_w16 = sem("s_w16")
        t_rk = sem("t_rk")
        t_ix = sem("t_ix")
        t_pl = sem("t_pl")
        t_te = sem("t_te")
        t_z = sem("t_z")
        t_zm = sem("t_zm")
        t_sc = sem("t_sc")
        t_xr = [sem(f"t_xr{i}") for i in range(NX)]
        t_tr = sem("t_tr")
        t_x32 = sem("t_x32")
        t_xh = sem("t_xh")
        t_xl = sem("t_xl")
        t_fg = sem("t_fg")
        t_yo = sem("t_yo")
        t_ys = [sem(f"t_ys{i}") for i in range(2)]
        t_yg = [sem(f"t_yg{i}") for i in range(TA)]
        t_mo1 = sem("t_mo1")
        t_mo = sem("t_mo")
        t_moe = sem("t_moe")
        s_raw = [sem(f"s_raw{i}") for i in range(2)]
        s_G = [sem(f"s_G{i}") for i in range(NGS)]
        s_scr = sem("s_scr0")
        s_scr1 = [sem(f"s_scr1_{g}") for g in range(NG)]
        s_gtb = [sem(f"s_gtb{i}") for i in range(1 + NG)]
        s_out = sem("s_out")
        p_at = sem("p_at")
        p_th = sem("p_th")
        p_sc = sem("p_sc")
        p_v = sem("p_v")
        p_m = sem("p_m")
        p_col = sem("p_col")
        p_pm = sem("p_pm")
        p_ex = sem("p_ex")
        p_po = sem("p_po")
        p_no = sem("p_no")
        p_tr = sem("p_tr")
        p_ev = sem("p_ev")
        p_lg = sem("p_lg")
        p_x = sem("p_x")
        p_row = sem("p_row")
        p_lc = sem("p_lc")
        p_one = sem("p_one")
        b_cnt = sem("b_cnt")
        b_sum = sem("b_sum")
        b_upd = sem("b_upd")
        b_g = sem("b_g")
        b_gt = sem("b_gt")
        b_ev = sem("b_ev")
        b_b2 = sem("b_b2")
        m_h = sem("m_h")
        m_hs = sem("m_hs")
        m_xa = sem("m_xa")
        m_mv = sem("m_mv")
        m_rs = sem("m_rs")
        m_n1 = sem("m_n1")
        m_x2 = sem("m_x2")
        m_mv2 = sem("m_mv2")
        m_rs2 = sem("m_rs2")
        m_n2 = sem("m_n2")
        m_x2T = sem("m_x2T")
        m_nT = sem("m_nT")
        m_xn = sem("m_xn")
        m_sp = sem("m_sp")
        m_lg = sem("m_lg")
        m_d = sem("m_d")
        m_e = sem("m_e")
        m_cw = sem("m_cw")
        m_cT = sem("m_cT")
        m_cE = sem("m_cE")
        m_one = sem("m_one")

        chain = {"dve": [sem("c_dve"), 0], "pool": [sem("c_pool"), 0], "act": [sem("c_act"), 0]}

        def link(eng, who, ins):
            c = chain[who]
            c[1] += 1
            ins.then_inc(c[0], 1)
            eng.wait_ge(c[0], c[1])

        Q = {k: [] for k in ("pe", "act", "dve", "pool", "sp")}

        def at(q, pos, fn):
            Q[q].append((pos, len(Q[q]), fn))

        def spread(q, who, pos, step, parts):
            reached = {}
            for n, part in enumerate(parts):
                def fn(eng, n=n, part=part):
                    if n:
                        eng.wait_ge(chain[who][0], reached["n"])
                    ins = part(eng)
                    if n < len(parts) - 1:
                        chain[who][1] += 1
                        reached["n"] = chain[who][1]
                        ins.then_inc(chain[who][0], 1)
                at(q, pos + step * n, fn)

        def share(u):
            return SHARE[0 if u < 40 else 1 if u < 64 else 2 if u < US else 3 if u < UD else 4]

        HIA = [int((u + 1) * share(u)) > int(u * share(u)) for u in range(NU)]
        nha = np.cumsum(HIA).tolist()
        nhd = np.cumsum([not x for x in HIA]).tolist()

        last_use = {}
        for s_, (layer_, _, _, k_) in enumerate(STEPS):
            if layer_ == 0:
                last_use[k_] = s_

        def after(name, g):
            return HURRY.get(name, AT[name]) if g == GA - 1 else AT[name]

        terms = []
        kept = sorted(range(ND), key=lambda s: (STEPS[s][2], s))
        for s in range(NS0 + E):
            if s >= ND:
                terms.append((unit0(s) + 4 + LAG + AT["term"], "y", s))
            else:
                terms.append((4 * ND + AT["kept0"] + KEPT * kept.index(s), "y", s))
        M0 = [4.0 * max(s for s in range(NS0) if STEPS[s][2] == g) + 10 for g in range(NG)]
        MO = UD + 4.0
        WP = [MO + AT["weigh"] + 1.7 * i for i in range(TA)]
        for g in range(NG):
            terms.append((4 * ND + 7 + 5 * g + 0.4, "b2", (0, g)))
            terms.append((M0[g] + after("x2a", g), "x2", g))
        terms.append((UD + 8.4, "b2", (1, 3)))
        for g in range(GA):
            terms.append((WP[4 * g + 3] + AT["moe"] + 0.2, "moe", g))
        terms.sort(key=lambda x: x[0])
        where = {(k, v): i for i, (_, k, v) in enumerate(terms)}
        ys = [i for i, (_, k, _) in enumerate(terms) if k == "y"]

        def in_tmp(i):
            gated = terms[i][1] == "y"
            return (s_tmp if gated else s_tma), sum((k == "y") == gated for _, k, _ in terms[:i + 1])

        gslot = {ti: j for j, ti in enumerate(ys)}

        def group_of(kind, v):
            return STEPS[v][2] if kind == "y" else (v if kind in ("x2", "moe") else v[1])

        def layer_of(kind, v):
            return STEPS[v][0] if kind == "y" else (1 if kind in ("x2", "moe") else v[0])

        done0 = {g: max(i for i, (_, k, v) in enumerate(terms) if group_of(k, v) == g and layer_of(k, v) == 0) + 1
                 for g in range(NG)}
        done1 = {g: max(i for i, (_, k, v) in enumerate(terms) if group_of(k, v) == g) + 1 for g in range(NG)}

        misc = []
        PB = [-34.5, -32.8] + [AT["chains"] + AT["batch"] * (b - 2) for b in range(2, B)]
        PD = [0.1, AT["pt"], AT["pt"] + 0.1, AT["pt"] + 0.2, AT["pl"], AT["pl"] + 0.1]
        for b in range(B):
            misc.append((PB[b], ("po", b), (p_no, b + 1)))
            misc.append((PB[b] + (PD[1] if b > 1 else 2.0), ("pt", b), (p_ev, b + 1)))
            misc.append((PB[b] + (PD[4] if b > 1 else 4.0), ("pl", b), (p_lc, b + 1)))
        B0 = PB[B - 1] + PD[5] + 0.3
        for r in range(17):
            misc.append((B0 + AT["bis"] + 2 * r, ("bis", r), (b_upd, r + 1)))
        PG = B0 + 39.45
        misc.append((PG, ("gT0", 0), (b_ev, 1)))
        for g in range(NG):
            misc.append((4 * ND + 6 + 5 * g + 0.35, ("b2", (0, g)), in_tmp(where[("b2", (0, g))])))
            misc.append((M0[g] + after("h", g), ("h", g), (m_hs, 2 * g + 2)))
            misc.append((M0[g] + after("xa", g), ("xa", g), (m_n1, g + 1)))
            misc.append((M0[g] + after("x2T", g), ("x2T", g), in_tmp(where[("x2", g)])))
            misc.append((M0[g] + after("nT", g), ("nT", g), (m_xn, g + 1)))
            misc.append((M0[g] + after("lg", g), ("lg", g), (m_d, g + 1)))
            misc.append((M0[g] + after("cT", g), ("cT", g), (m_cE, g + 1)))
        RK = [M0[g] + (after("rank", g) if g == GA - 1 else AT["rank0"]) for g in range(GA)]
        for g in range(GA):
            misc.append((RK[g] + 0.75, ("rk", g), (t_te, 1) if g == GA - 1 else (t_ix, g + 1)))

        def tpos(i):
            return max(US - 0.4 + 0.05 * i, US + 2 * i - 5 + AT["tile"])

        for i in range(NTL):
            misc.append((tpos(i), ("t", i), (t_x32, i + 1)))
        misc.append((UD + 8.35, ("b2", (1, 3)), in_tmp(where[("b2", (1, 3))])))
        for g in range(GA):
            misc.append((WP[4 * g] + AT["moe"], ("moe", g), in_tmp(where[("moe", g)])))
        misc.sort(key=lambda x: x[0])
        HOLD = {"xa": 4.5, "moe": 7.5, "bis": 1.8, "rk": 2.0}
        mb, held = {}, [(-1e9, None), (-1e9 + 1, None)]
        for pos, key, free in misc:
            i = 0 if held[0][0] <= held[1][0] else 1
            mb[key] = (6 + i, held[i][1])
            held[i] = (pos + HOLD.get(key[0], 0.8), free)
        mpos = {key: pos for pos, key, _ in misc}

        def misc_bank(eng, key):
            i, free = mb[key]
            if free is not None:
                eng.wait_ge(free[0], free[1])
            return bank[i]

        def weights_split(k):
            return (s_w, k + 1) if k < NWP else (s_wv, k + 1 - NWP)

        regs = {}

        def tile_expert(eng, name, i):
            if (name, "ready") not in regs:
                eng.wait_ge(t_te, 1)
                regs[(name, "ready")] = True
            if (name, i) not in regs:
                k, unit = (1, 4) if name == "act" else (0, 2048)
                regs[(name, i)] = eng.value_load(tei[0:1, k, i:i + 1], min_val=0, max_val=(E - 1) * unit)
            return regs[(name, i)]

        def expert_weights(r, off):
            return w16[:, off:off + (E - 1) * 2048 + 128][:, bass.ds(r, 128)]

        def pe_m1(u):
            kind, v, c = UNITS[u]
            o = bank[u % 4]

            def fn(pe):
                if kind == "tile":
                    if v == 0 and c == 0:
                        pe.wait_ge(s_w16, E)
                    r = tile_expert(pe, "pe", v)
                    if c == 0:
                        pe.wait_ge(t_xl, v + 1)
                    pe.wait_ge(s_g, u - 3)
                    a, b_ = xth[:, v % NX, :], xtl[:, v % NX, :]
                    for k in range(2):
                        off = (2 * c + k) * 128
                        w_h, w_l = expert_weights(r, off), expert_weights(r, 1024 + off)
                        oo = o[:, k * TS:k * TS + TS]
                        pe.matmul(oo, w_h, a, start=True, stop=False)
                        pe.matmul(oo, w_h, b_, start=False, stop=False)
                        last = pe.matmul(oo, w_l, a, start=False, stop=True)
                    last.then_inc(s_m1, 1)
                    return
                layer, e, g, k = STEPS[v]
                if layer == 0:
                    if c == 0:
                        pe.wait_ge(*weights_split(k))
                        pe.wait_ge(p_x, 2 * g + 2)
                    a = xh[:, g // 2, (g % 2) * 512:(g % 2) * 512 + 512]
                    b_ = xl[:, g // 2, (g % 2) * 512:(g % 2) * 512 + 512]
                    w_h = wh[:, SLOT[k], c * 128:c * 128 + 128]
                    w_l = wl[:, SLOT[k], c * 128:c * 128 + 128]
                else:
                    pe.wait_ge(m_sp, 1)
                    a, b_ = xbh[:, :], xbl[:, :]
                    w_h = w16[:, e * 2048 + c * 128:e * 2048 + c * 128 + 128]
                    w_l = w16[:, e * 2048 + 1024 + c * 128:e * 2048 + 1024 + c * 128 + 128]
                if u >= 4:
                    pe.wait_ge(s_g, u - 3)
                else:
                    pe.wait_ge(p_ex, 2 * u + 2)
                pe.matmul(o[:, :], w_h, a, start=True, stop=False)
                pe.matmul(o[:, :], w_h, b_, start=False, stop=False)
                pe.matmul(o[:, :], w_l, a, start=False, stop=True).then_inc(s_m1, 1)
            return fn

        def result_read(eng, q):
            kind, v = RES[q]
            if kind == "tile":
                eng.wait_ge(t_yo, v + 1)
            elif v < ND:
                eng.wait_ge(s_ysv, v + 1)
            else:
                eng.wait_ge(*in_tmp(where[("y", v)]))

        def pe_m2(u):
            kind, v, c = UNITS[u]
            q = res_of[(kind, v)]
            o = bank[4 + q % 2]

            def fn(pe):
                if c == 0 and q >= 2:
                    result_read(pe, q - 2)
                elif c == 0:
                    pe.wait_ge(p_ex, 2 * B - 2 + 2 * q)
                pe.wait_ge(s_lo, u + 1)
                if kind == "tile":
                    r = tile_expert(pe, "pe", v)
                    for k in range(2):
                        off = 512 + (2 * c + k) * 128
                        w_h, w_l = expert_weights(r, off), expert_weights(r, 1024 + off)
                        for z in range(2):
                            sl = slice(k * TS + z * 128, k * TS + z * 128 + 128)
                            oo = o[:, z * 128:z * 128 + 128]
                            a, b_ = h16[:, u % NH, sl], l16[:, u % NH, sl]
                            pe.matmul(oo, a, w_h, start=(c == 0 and k == 0 and z == 0), stop=False, skip_group_check=True)
                            pe.matmul(oo, a, w_l, start=False, stop=False, skip_group_check=True)
                            last = pe.matmul(oo, b_, w_h, start=False, stop=(c == 1 and k == 1), skip_group_check=True)
                    last.then_inc(s_m2, 1)
                    return
                layer, e, g, k = STEPS[v]
                if layer == 0:
                    w_h = wh[:, SLOT[k], 512 + c * 128:640 + c * 128]
                    w_l = wl[:, SLOT[k], 512 + c * 128:640 + c * 128]
                    a, b_ = hh[:, u % NH, :], hl[:, u % NH, :]
                else:
                    w_h = w16[:, e * 2048 + 512 + c * 128:e * 2048 + 640 + c * 128]
                    w_l = w16[:, e * 2048 + 1536 + c * 128:e * 2048 + 1664 + c * 128]
                    a, b_ = h16[:, u % NH, :], l16[:, u % NH, :]
                pe.matmul(o[:, :], w_h, a, start=(c == 0), stop=False)
                pe.matmul(o[:, :], w_l, a, start=False, stop=False)
                pe.matmul(o[:, :], w_h, b_, start=False, stop=(c == 3)).then_inc(s_m2, 1)
            return fn

        def act_gelu(u):
            kind, v, c = UNITS[u]

            def fn(act):
                if kind == "tile":
                    r = tile_expert(act, "act", v)
                act.wait_ge(s_m1, u + 1)
                if u >= NH:
                    act.wait_ge(s_lo, u - NH + 1)
                if kind == "tile":
                    for k in range(2):
                        last = act.activation(h32[:, u % NH, k * TS:k * TS + TS], bank[u % 4][:, k * TS:k * TS + TS],
                                              ACT.Gelu, bias=b1f[1][:, 2 * c + k:2 * c + k + 4 * (E - 1) + 1][:, bass.ds(r, 1)],
                                              scale=1.0 / (WS * XS))
                    last.then_inc(s_g, 1)
                    return
                layer, e, g, _ = STEPS[v]
                act.activation(h32[:, u % NH, :], bank[u % 4][:, :],
                               ACT.Gelu if layer else ACT.Gelu_apprx_tanh,
                               bias=b1f[layer][:, e * 4 + c:e * 4 + c + 1],
                               scale=1.0 / (WS * XS) if layer else 1.0).then_inc(s_g, 1)
            return fn

        def hi_part(q, u):
            def fn(eng):
                eng.wait_ge(s_g, u + 1)
                if u >= NH:
                    eng.wait_ge(s_m2, u - NH + 1)
                dst = hh[:, u % NH, :] if u < US else h16[:, u % NH, :]
                if q == "act":
                    eng.activation(dst, h32[:, u % NH, :], ACT.Copy, scale=1.0 if u < US else HS).then_inc(s_hia, 1)
                elif u < US:
                    eng.tensor_copy(dst, h32[:, u % NH, :]).then_inc(s_hid, 1)
                else:
                    eng.tensor_scalar(dst, h32[:, u % NH, :], HS, None, ALU.mult).then_inc(s_hid, 1)
            return fn

        def lo_part(u):
            def fn(dve):
                if HIA[u]:
                    dve.wait_ge(s_hia, nha[u])
                else:
                    dve.wait_ge(s_hid, nhd[u])
                if u >= NH:
                    dve.wait_ge(s_m2, u - NH + 1)
                if u < US:
                    dve.tensor_tensor(hl[:, u % NH, :], h32[:, u % NH, :], hh[:, u % NH, :].bitcast(F32),
                                      ALU.subtract).then_inc(s_lo, 1)
                else:
                    dve.scalar_tensor_tensor(l16[:, u % NH, :], h32[:, u % NH, :], HS, h16[:, u % NH, :],
                                             ALU.mult, ALU.subtract).then_inc(s_lo, 1)
            return fn

        for u in range(NU):
            at("pe", u, pe_m1(u))
            at("pe", u + LAG + AT["m2"], pe_m2(u))
            at("act", u, act_gelu(u))
            if HIA[u]:
                at("act", u + AT["hia"], hi_part("act", u))
            else:
                at("dve", u, hi_part("dve", u))
            at("dve", u + AT["lo"], lo_part(u))

        def keep(s):
            def fn(act):
                act.wait_ge(s_m2, 4 * s + 4)
                act.activation(ysv[:, s, :], bank[4 + s % 2][:, :], ACT.Copy).then_inc(s_ysv, 1)
            return fn

        for s in range(ND):
            at("act", 4 * s + 4 + LAG + 0.3, keep(s))

        def gated(i, v):
            def fn(dve):
                if i >= NTMP:
                    dve.wait_ge(s_acc, i - NTMP + 1)
                o = tmp[:, i % NTMP, :]
                j = gslot[i]
                dve.wait_ge(s_G[j % NGS], 16 * (j // NGS + 1))
                if v < ND:
                    dve.wait_ge(s_ysv, v + 1)
                    src = ysv[:, v, :]
                else:
                    q = res_of[("dense", v)]
                    dve.wait_ge(s_m2, last_unit(q) + 1)
                    src = bank[4 + q % 2][:, :]
                if STEPS[v][0] == 0:
                    dve.tensor_tensor(o, src, Gs[:, j % NGS, :], ALU.mult).then_inc(s_tmp, 1)
                else:
                    dve.scalar_tensor_tensor(o, src, 1.0 / (WS * HS), Gs[:, j % NGS, :], ALU.mult, ALU.mult)\
                        .then_inc(s_tmp, 1)
            return fn

        def copied(i, kind, v):
            def fn(act):
                if i >= NTMP:
                    act.wait_ge(s_acc, i - NTMP + 1)
                if kind == "b2":
                    act.wait_ge(b_b2, [("b2", x) for _, k, x in terms if k == "b2"].index(("b2", v)) + 1)
                    src = bank[mb[("b2", v)][0]]
                elif kind == "moe":
                    act.wait_ge(t_moe, 4 * v + 4)
                    src = bank[mb[("moe", v)][0]]
                else:
                    act.wait_ge(m_x2T, v + 1)
                    src = bank[mb[("x2T", v)][0]]
                act.activation(tmp[:, i % NTMP, :], src[:, :], ACT.Copy).then_inc(s_tma, 1)
            return fn

        def add(i, kind, v):
            g = group_of(kind, v)

            def fn(pool):
                pool.wait_ge(*in_tmp(i))
                if i:
                    pool.wait_ge(s_acc, i)
                if kind == "x2":
                    pool.wait_ge(m_xa, v + 1)
                a = acc[:, g * 512:g * 512 + 512]
                pool.tensor_tensor(a, a, tmp[:, i % NTMP, :], ALU.add).then_inc(s_acc, 1)
            return fn

        for i, (pos, kind, v) in enumerate(terms):
            if kind == "y":
                at("dve", pos, gated(i, v))
            else:
                at("act", pos + AT["copied"], copied(i, kind, v))
            at("pool", pos + AT["add"], add(i, kind, v))

        def load_gates(j):
            ti = ys[j]
            s = terms[ti][2]
            layer, e, g, _ = STEPS[s]

            def fn(sp):
                if layer == 0:
                    sp.wait_ge(s_scr, 16)
                else:
                    sp.wait_ge(s_scr1[g], 16)
                if j >= NGS:
                    sp.wait_ge(*in_tmp(ys[j - NGS]))
                src = scr[layer][4 * g:4 * g + 4, e:e + 1, :].rearrange("t e p -> e t p")
                sp.dma_start(Gs[:, j % NGS, :].rearrange("q (t p) -> q t p", t=4),
                             src.to_broadcast([128, 4, 128])).then_inc(s_G[j % NGS], 16)
            return fn

        for j, ti in enumerate(ys):
            s = terms[ti][2]
            pos = terms[ys[j - NGS]][0] + 1.5 if j >= NGS else PG + 2
            if STEPS[s][0] == 1:
                pos = max(pos, M0[STEPS[s][2]] + after("cT", STEPS[s][2]) + 3.5)
            at("sp", pos, load_gates(j))

        ORDER16 = [5, 6, 7, 0, 1, 2, 3, 4]
        NL = len(LOADS)

        def w_free(k):
            return -50.0 + 2 * k if k < NW else 4.0 * last_use[BEFORE[k]] + 4 + LAG + 1.5

        P16 = 4 * ND + 6 + KEPT * ND + 2.0

        def w_pos(k):
            if k < NL:
                return w_free(k)
            return P16 + W16 * (k - NL)

        def raw_read(eng, k):
            if k < NL:
                eng.wait_ge(*weights_split(k))
            else:
                eng.wait_ge(s_w16, k - NL + 1)

        seq = sorted(range(NL + E), key=w_pos)
        assert [k for k in seq if k < NL] == list(range(NL))
        turn = {k: n for n, k in enumerate(seq)}

        def load_w(k):
            n = turn[k]

            def fn(sp):
                if n >= 2:
                    raw_read(sp, seq[n - 2])
                if k < NL:
                    src = t["w_0"][:, LOADS[k], :]
                else:
                    src = t["w_1"][:, ORDER16[k - NL], :]
                sp.dma_start(wraw[:, n % 2, :], src).then_inc(s_raw[n % 2], 16)
            return fn

        def round_w(k):
            def fn(pool):
                if k >= NW:
                    pool.wait_ge(s_m2, 4 * last_use[BEFORE[k]] + 4)
                if k == 0:
                    pool.wait_ge(ld["x3"], 16)
                pool.dma_start(wh[:, SLOT[k], :], t["w_0"][:, LOADS[k], :]).then_inc(s_wd[SLOT[k]], 16)
            return fn

        def split_w(k):
            n = turn[k]

            def fn(eng):
                eng.wait_ge(s_raw[n % 2], 16 * (n // 2 + 1))
                eng.wait_ge(s_wd[SLOT[k]], 16 * (1 + SLOT[:k].count(SLOT[k])))
                if k >= NW:
                    eng.wait_ge(s_m2, 4 * last_use[BEFORE[k]] + 4)
                for p in range(2):
                    sl = slice(p * 512, p * 512 + 512)
                    last = eng.tensor_tensor(wl[:, SLOT[k], sl], wraw[:, n % 2, sl],
                                             wh[:, SLOT[k], sl].bitcast(F32), ALU.subtract)
                last.then_inc(weights_split(k)[0], 1)
            return fn

        last_kept = max(where[("y", s)] for s in range(ND))

        def w16_high(k):
            n, e = turn[k], ORDER16[k - NL]

            def fn(act):
                act.wait_ge(s_raw[n % 2], 16 * (n // 2 + 1))
                act.wait_ge(*in_tmp(last_kept))
                act.activation(w16[:, e * 2048:e * 2048 + 1024], wraw[:, n % 2, :], ACT.Copy, scale=WS).then_inc(s_w16h, 1)
            return fn

        def w16_low(k):
            n, e = turn[k], ORDER16[k - NL]

            def fn(dve):
                dve.wait_ge(s_w16h, k - NL + 1)
                dve.scalar_tensor_tensor(w16[:, e * 2048 + 1024:e * 2048 + 2048], wraw[:, n % 2, :], WS,
                                         w16[:, e * 2048:e * 2048 + 1024], ALU.mult, ALU.subtract).then_inc(s_w16, 1)
            return fn

        for k in range(NL + E):
            if k < NL:
                at("pool", w_free(k), round_w(k))
                if k < NWP:
                    at("pool", w_free(k) + (AT["split"] if k >= NW else 0.1), split_w(k))
                else:
                    at("dve", w_free(k) + AT["splitd"], split_w(k))
            else:
                at("act", w_pos(k) + AT["w16h"], w16_high(k))
                at("dve", w_pos(k) + AT["w16l"], w16_low(k))
            n = turn[k]
            at("sp", -60.0 + n if n < 2 else w_pos(seq[n - 2]) + AT["raw"], load_w(k))

        def sp_loads(sp):
            for g in range(NG):
                if g == 0:
                    s0 = load_sem("c0")
                    sp.dma_start(w1c[:, :], t["w1c"]).then_inc(s0, 16)
                    sp.dma_start(b1c[:, :], t["b1c"]).then_inc(s0, 16)
                    sp.dma_start(vc[:, :], t["vc"]).then_inc(s0, 16)
                sp.dma_start(acc[:, g * 512:g * 512 + 512], t["xT"][:, g * 512:g * 512 + 512]).then_inc(load_sem(f"x{g}"), 16)
            s0 = load_sem("ids")
            sp.dma_start(tyr[:, :], t["itype"].rearrange("(a n) -> a n", a=1)).then_inc(s0, 16)
            sp.dma_start(lid[:, :], t["ilang"].rearrange("(a n) -> a n", a=1)).then_inc(s0, 16)
            sp.wait_ge(s0, 32)
            for b in range(B):
                r = sp.value_load(tyr[0:1, b:b + 1], min_val=0, max_val=2)
                sp.dma_start(maskt[:, b, :], t["maskt"][bass.ds(r, 1), :, :].rearrange("a p c -> p (a c)"))\
                    .then_inc(load_sem(f"mask{b}"), 16)

        def sp_loads2(sp):
            sp.dma_start(xtm[:, :, 0:D], t["xtm"]).then_inc(load_sem("xtm"), 16)
            sp.dma_start(gw0[:, :], t["gw0"]).then_inc(load_sem("gw0"), 16)
            sp.dma_start(b1f[0][:, :], t["b1_0"]).then_inc(load_sem("b1f0"), 16)
            sp.dma_start(bitc[:, :], t["bitc"]).then_inc(load_sem("bitc"), 16)

        for name in ("ident", "ty", "sel", "identb"):
            load_sem(name)

        def act_loads(act):
            act.dma_start(ident[:, :], t["ident"]).then_inc(ld["ident"], 16)
            act.dma_start(ty[:, :], t["itype"].rearrange("(n a) -> n a", a=1)).then_inc(ld["ty"], 16)
            act.dma_start(sel[:, :], t["sel"]).then_inc(ld["sel"], 16)
            act.dma_start(identb[:, :], t["identb"]).then_inc(ld["identb"], 16)

        at("sp", -100, sp_loads)
        at("sp", -59.5, sp_loads2)
        at("act", -101, act_loads)

        def sp_later(sp):
            sp.dma_start(b2f[0][:, :], t["b2_0"]).then_inc(load_sem("b2f0"), 16)
            sp.dma_start(b2f[1][:, :], t["b2_1"]).then_inc(load_sem("b2f1"), 16)
            sp.dma_start(b1f[1][:, :], t["b1_1"]).then_inc(load_sem("b1f1"), 16)
            sp.dma_start(gw1[:, :], t["gw1"]).then_inc(load_sem("gw1"), 16)
            sp.dma_start(fgb[:, :], t["fgb"]).then_inc(load_sem("fgb"), 16)
            sp.dma_start(iota8[:, :, :], t["iota8"]).then_inc(load_sem("iota8"), 16)
            s0 = load_sem("sort")
            sp.dma_start(triu[:, :], t["triu"]).then_inc(s0, 16)
            sp.dma_start(it256[:, :], t["it256"]).then_inc(s0, 16)
            sp.dma_start(region[:, :], t["region"]).then_inc(s0, 16)
            sp.wait_ge(t_zm, 1)
            zr = scx.rearrange("(n p c) d -> n p (c d)", p=128, c=ZC)
            for i in range(NZ):
                sp.dma_start(zr[i, :, :], zer[:, :]).then_inc(t_z, 16)
            s0 = load_sem("lang")
            sp.wait_ge(p_no, B)
            for b in range(B):
                r = sp.value_load(lid[0:1, b:b + 1], min_val=0, max_val=LANGS - 1)
                sp.dma_start(cw1[:, b, :], t["cw1"][bass.ds(r, 1), :, :].rearrange("a p c -> p (a c)")).then_inc(s0, 16)
                sp.dma_start(cb1[:, b:b + 1], t["cb1"][bass.ds(r, 1), :].rearrange("a p -> p a")).then_inc(s0, 16)
                sp.dma_start(cw2[:, b, :], t["cw2"][bass.ds(r, 1), :, :].rearrange("a p c -> p (a c)")).then_inc(s0, 16)
                sp.dma_start(gbc[:, b, :], t["gbc"][bass.ds(r, 1), :].to_broadcast([128, 2 * D])).then_inc(s0, 16)

        at("sp", 14, sp_later)

        EB = [0, 1, 2, 3, 4, 5, 4, 5]

        def warm(pe, n):
            for _ in range(n):
                pe.matmul(bank[7][:, 0:128], onesb[:, :], onesb[:, :], start=True, stop=True)

        def pe_prologue(pe):
            pe.wait_ge(p_one, 1)
            warm(pe, WARM[0])
            pe.wait_ge(ld["c0"], 48)
            for g in range(NG):
                pe.wait_ge(ld[f"x{g}"], 16)
                pe.matmul(bank[g][0:A, :], w1c[:, :], acc[:, g * 512:g * 512 + 512], start=True, stop=True).then_inc(p_at, 1)
            pe.wait_ge(p_v, 1)
            for b in range(B):
                pe.wait_ge(p_th, b // 2 + 1)
                last = pe.matmul(bank[4][0:B, 0:S], vz[:, B - 1 - b:2 * B - 1 - b], attn[:, b * S:b * S + S],
                                 start=(b == 0), stop=(b == B - 1))
            last.then_inc(p_sc, 1)
            pe.wait_ge(ld["ident"], 16)
            pe.wait_ge(p_row, 1)
            for l in range(2):
                last = pe.transpose(bank[5][:, l * B:l * B + B], rows[:, l * 128:l * 128 + 128], ident[0:B, 0:B])
            last.then_inc(p_sc, 1)

        def exponent(b):
            def fn(pe):
                if b == 0:
                    warm(pe, WARM[1])
                    pe.wait_ge(p_m, 1)
                    pe.wait_ge(ld["identb"], 16)
                pe.wait_ge(ld[f"mask{b}"], 16)
                if b == 5:
                    pe.wait_ge(p_col, 1)
                if b >= 6:
                    pe.wait_ge(p_ex, 2 * (b - 1))
                o = bank[EB[b]][:, :]
                sl = selr[:, b * 128:b * 128 + 128]
                pe.matmul(o, sl, mh[:, :, :].rearrange("b c s -> b (c s)"), start=True, stop=False)
                pe.matmul(o, sl, ml[:, :, :].rearrange("b c s -> b (c s)"), start=False, stop=False)
                pe.matmul(o, identb[:, :], maskt[:, b, 0:512], start=False, stop=True).then_inc(p_pm, 1)
            return fn

        def pooled(b):
            def fn(pe):
                o = misc_bank(pe, ("po", b))
                if b == 0:
                    pe.wait_ge(ld["xtm"], 16)
                    pe.wait_ge(p_one, 2)
                pe.wait_ge(p_ex, 2 * b + 2)
                for j in range(2):
                    for l in range(2):
                        last = pe.matmul(o[:, j * 256:j * 256 + D + 1], ET(b)[:, l * S + j * 128:l * S + j * 128 + 128],
                                         xtm[:, 2 * b + l, :], start=(l == 0), stop=(l == 1))
                last.then_inc(p_po, 1)
            return fn

        def trans(b):
            def fn(pe):
                o = misc_bank(pe, ("pt", b))
                pe.wait_ge(p_no, b + 1)
                for j in range(2):
                    last = pe.transpose(o[:, j * 128:j * 128 + 128], ptm[:, b % 2, j * 128:j * 128 + 128], ident[:, :])
                last.then_inc(p_tr, 1)
            return fn

        def logit(b):
            def fn(pe):
                o = misc_bank(pe, ("pl", b))
                if b == 0:
                    pe.wait_ge(ld["gw0"], 16)
                pe.wait_ge(p_ev, b + 1)
                for j in range(2):
                    last = pe.matmul(o[:, j * E:j * E + E], pT[:, b % 2, j * 128:j * 128 + 128], gw0[:, :],
                                     start=True, stop=True)
                last.then_inc(p_lg, 1)
            return fn

        def evac(b):
            def fn(act):
                act.wait_ge(p_tr, b + 1)
                if b >= 2:
                    act.wait_ge(p_lg, b - 1)
                    act.wait_ge(p_x, b - 1)
                act.activation(pT[:, b % 2, :], bank[mb[("pt", b)][0]][:, 0:256], ACT.Copy).then_inc(p_ev, 1)
            return fn

        def norm(b):
            def fn(dve):
                def ln(ins):
                    link(dve, "dve", ins)
                pb = bank[mb[("po", b)][0]]
                dve.wait_ge(p_po, b + 1)
                if b >= 2:
                    dve.wait_ge(p_tr, b - 1)
                ln(dve.tensor_tensor(rr[:, b % 2, 0, :], pb[:, D:512:256], maskt[:, b, 512:514], ALU.mult))
                ln(dve.reciprocal(rr[:, b % 2, 1, :], rr[:, b % 2, 0, :]))
                for j in range(2):
                    last = dve.tensor_scalar(ptm[:, b % 2, j * 128:j * 128 + 128], pb[:, j * 256:j * 256 + D],
                                             rr[:, b % 2, 1, j:j + 1], None, ALU.mult)
                last.then_inc(p_no, 1)
            return fn

        def xsplit(b):
            def fn(dve):
                dve.wait_ge(p_ev, b + 1)
                o_h = xh[:, b // 4, (b % 4) * S:(b % 4) * S + S]
                o_l = xl[:, b // 4, (b % 4) * S:(b % 4) * S + S]
                link(dve, "dve", dve.tensor_copy(o_h, pT[:, b % 2, :]))
                dve.tensor_tensor(o_l, pT[:, b % 2, :], o_h.bitcast(F32), ALU.subtract).then_inc(p_x, 1)
            return fn

        def logcopy(b):
            def fn(dve):
                dve.wait_ge(p_lg, b + 1)
                dve.tensor_copy(L32[:, 2 * b * E:2 * b * E + 2 * E], bank[mb[("pl", b)][0]][:, 0:2 * E]).then_inc(p_lc, 1)
            return fn

        at("pe", -100, pe_prologue)
        for b in range(B):
            p = PB[b]
            at("pe", mpos[("po", b)], pooled(b))
            at("dve", p + PD[0], norm(b))
            at("pe", mpos[("pt", b)], trans(b))
            at("act", p + (PD[2] if b > 1 else 2.1), evac(b))
            at("dve", p + (PD[3] if b > 1 else 2.2), xsplit(b))
            at("pe", mpos[("pl", b)], logit(b))
            at("dve", p + (PD[5] if b > 1 else 4.1), logcopy(b))

        def act_prologue(act):
            act.wait_ge(p_one, 1)
            act.activation(junk[0:1, 0, 0:1], onesb[0:1, 0:1], ACT.Tanh)
            act.wait_ge(ld["c0"], 48)
            for g in range(NG):
                act.wait_ge(p_at, g + 1)
                act.activation(attn[:, g * 512:g * 512 + 512], bank[g][0:A, :], ACT.Tanh, bias=b1c[:, :]).then_inc(p_th, 1)
            act.wait_ge(p_col, 1)

        def act_exponent(i):
            def fn(act):
                act.wait_ge(p_pm, i + 1)
                for l in range(2):
                    act.activation(ET(i)[:, l * S:l * S + S], bank[EB[i]][:, l * S:l * S + S], ACT.Exp,
                                   bias=scol[:, l * B + i:l * B + i + 1], scale=-1.0).then_inc(p_ex, 1)
                if i == B - 1:
                    act.wait_ge(ld["b1f0"], 16)
            return fn

        for b in range(B):
            at("pe", -40.0 + b, exponent(b))
            at("act", -40.0 + b + 0.45, act_exponent(b))

        at("act", -100, act_prologue)

        def dve_prologue(dve):
            def ln(ins):
                link(dve, "dve", ins)
            dve.memset(onesb[:, :], 1.0).then_inc(p_one, 1)
            ln(dve.memset(vz[:, :], 0.0))
            dve.memset(xtm[:, :, D:D + 1], 1.0).then_inc(p_one, 1)
            dve.wait_ge(ld["c0"], 48)
            dve.tensor_copy(vz[:, B - 1:B], vc[:, :]).then_inc(p_v, 1)
            dve.memset(pre[:, 0:1], -BIG)
            dve.memset(suf[:, S + 1:S + 2], -BIG)
            dve.wait_ge(ld["ty"], 16)
            dve.tensor_scalar(is_t[:, 0:1], ty[:, :], 0.0, None, ALU.is_equal)
            ln(dve.tensor_scalar(is_t[:, 1:2], ty[:, :], 1.0, None, ALU.is_equal))
            ln(dve.tensor_tensor(is_t[:, 3:4], is_t[:, 0:1], is_t[:, 1:2], ALU.add))
            ln(dve.tensor_scalar(is_t[:, 2:3], is_t[:, 3:4], -1.0, 1.0, ALU.mult, ALU.add))
            dve.wait_ge(ld["sel"], 16)
            dve.tensor_copy(selr[:, :], sel)
            dve.wait_ge(p_sc, 1)
            dve.tensor_copy(rows, bank[4][0:B, 0:S]).then_inc(p_row, 1)
            dve.wait_ge(p_row, 1)
            ln(dve.tensor_tensor_scan(pre[:, 1:S + 1], rows[:, :], rows[:, :], -BIG, ALU.max, ALU.max))
            ln(dve.tensor_tensor_scan(suf[:, S:0:-1], rows[:, ::-1], rows[:, ::-1], -BIG, ALU.max, ALU.max))
            dve.wait_ge(p_sc, 2)
            dve.tensor_copy(scol[:, :], bank[5][:, 0:NT]).then_inc(p_col, 1)
            ln(dve.tensor_tensor(cl[:, :], pre[:, 0:S], suf[:, 2:S + 2], ALU.max))
            ln(dve.tensor_scalar(cl[:, :], cl[:, :], is_t[:, 2:3], None, ALU.mult))
            ln(dve.scalar_tensor_tensor(cl[:, :], pre[:, 1:S + 1], is_t[:, 0:1], cl[:, :], ALU.mult, ALU.add))
            ln(dve.scalar_tensor_tensor(mrow, suf[:, 1:S + 1], is_t[:, 1:2], cl[:, :], ALU.mult, ALU.add))
            mr2 = mrow.unsqueeze(1).to_broadcast([B, 2, S])
            ln(dve.tensor_copy(mh[:, :, :], mr2))
            dve.tensor_tensor(ml[:, :, :], mr2, mh[:, :, :].bitcast(F32), ALU.subtract).then_inc(p_m, 1)

        at("dve", -100, dve_prologue)

        NALL = N * E
        T_POS = NALL - KTH + 1

        def bis_count(r):
            def fn(dve):
                def ln(ins):
                    link(dve, "dve", ins)
                if r == 0:
                    dve.wait_ge(ld["bitc"], 16)
                    dve.wait_ge(p_lc, B)
                    dve.tensor_scalar(junk[:, 0, :], L32[:, :], 0.0, None, ALU.is_ge, ALU.add, accum_out=cnt3[:, 0, 0:1])\
                        .then_inc(b_cnt, 1)
                    return
                dve.wait_ge(b_upd, r)
                for i in range(3 if r > 1 else 1):
                    last = dve.tensor_scalar(junk[:, i, :], L2[:, :], cand[:, i:i + 1].bitcast(F32), None, ALU.is_ge,
                                             ALU.add, accum_out=cnt3[:, r % 2, i:i + 1])
                last.then_inc(b_cnt, 1)
            return fn

        def bis_sum(r):
            def fn(pe):
                o = misc_bank(pe, ("bis", r))
                if r == 0:
                    pe.wait_ge(p_one, 1)
                pe.wait_ge(b_cnt, r + 1)
                n = 3 if r > 1 else 1
                pe.matmul(o[:, 0:n], onesb[:, :], cnt3[:, r % 2, 0:n], start=True, stop=True).then_inc(b_sum, 1)
            return fn

        def bis_update(r):
            def fn(dve):
                def ln(ins):
                    link(dve, "dve", ins)
                o = bank[mb[("bis", r)][0]]
                dve.wait_ge(b_sum, r + 1)
                if r == 0:
                    ln(dve.tensor_scalar(bis[:, 0:1], o[:, 0:1], float(T_POS), None, ALU.is_lt))
                    ln(dve.tensor_scalar(bis[:, 1:2], bis[:, 0:1], -2.0, 1.0, ALU.mult, ALU.add))
                    ln(dve.tensor_scalar(bis[:, 2:3], bis[:, 0:1], float(KTH - T_POS), float(T_POS), ALU.mult, ALU.add))
                    ln(dve.tensor_scalar(L2[:, :], L32[:, :], bis[:, 1:2], None, ALU.mult))
                    ln(dve.memset(cur_i[:, :], 0))
                    dve.tensor_copy(cand[:, 0:3], bitc[:, 0:3]).then_inc(b_upd, 1)
                    return
                n = 3 if r > 1 else 1
                shift = 30 if r == 1 else 30 - 2 * (r - 1)
                ln(dve.tensor_scalar(bisj[:, 0:n], o[:, 0:n], bis[:, 2:3], None, ALU.is_ge, ALU.add,
                                     accum_out=bis[:, 3:4]))
                ln(dve.tensor_scalar(inc_i[:, :], bis[:, 3:4], float(2 ** shift), None, ALU.mult))
                ln(dve.tensor_tensor(cur_i[:, r % 2:r % 2 + 1], cur_i[:, (r + 1) % 2:(r + 1) % 2 + 1], inc_i[:, :],
                                     ALU.bitwise_or))
                if r < 16:
                    dve.tensor_tensor(cand[:, 0:3], bitc[:, 3 * r:3 * r + 3],
                                      cur_i[:, r % 2:r % 2 + 1].to_broadcast([128, 3]), ALU.bitwise_or)\
                        .then_inc(b_upd, 1)
                else:
                    ln(dve.tensor_scalar(bis[:, 4:5], cur_i[:, 0:1].bitcast(F32), bis[:, 1:2], None, ALU.mult))
                    dve.scalar_tensor_tensor(G0[:, :], L32[:, :], bis[:, 4:5], L32[:, :], ALU.is_ge, ALU.mult)\
                        .then_inc(b_upd, 1)
            return fn

        for r in range(17):
            at("dve", B0 + 2 * r, bis_count(r))
            at("pe", mpos[("bis", r)], bis_sum(r))
            at("dve", B0 + 2 * r + AT["upd"], bis_update(r))

        def gates0_T(pe):
            o = misc_bank(pe, ("gT0", 0))
            pe.wait_ge(b_upd, 17)
            pe.transpose(o[:, 0:128], G0[:, :], ident[:, :]).then_inc(b_gt, 1)

        def gates0_ev(act):
            act.wait_ge(b_gt, 1)
            act.activation(gT0[:, :], bank[mb[("gT0", 0)][0]][:, 0:128], ACT.Copy).then_inc(b_ev, 1)

        def gates0_out(sp):
            sp.wait_ge(b_ev, 1)
            sp.dma_start(scr[0].rearrange("t e p -> (t e) p"), gT0[:, :]).then_inc(s_scr, 16)
            sp.wait_ge(s_scr, 16)
            sp.dma_start(gTb[:, :].rearrange("e (t p) -> e t p", p=128), scr[0].rearrange("t e p -> e t p"))\
                .then_inc(s_gtb[0], 16)

        at("pe", PG, gates0_T)
        at("act", PG, gates0_ev)
        at("sp", PG + 1, gates0_out)

        b2_order = [v for _, k, v in terms if k == "b2"]

        def b2_mm(v):
            layer, g = v

            def fn(pe):
                o = misc_bank(pe, ("b2", v))
                pe.wait_ge(ld[f"b2f{layer}"], 16)
                pe.wait_ge(s_gtb[0] if layer == 0 else s_gtb[1 + g], 16)
                pe.matmul(o[:, :], b2f[layer][:, :], gTb[:, g * 512:g * 512 + 512], start=True, stop=True)\
                    .then_inc(b_b2, 1)
            return fn

        for v in b2_order:
            at("pe", mpos[("b2", v)], b2_mm(v))

        def mid(g):
            m = M0[g]

            def pe_h(pe):
                o = misc_bank(pe, ("h", g))
                if g == 0:
                    pe.wait_ge(ld["lang"], 16 * 4 * B)
                pe.wait_ge(s_acc, done0[g])
                for i in range(2):
                    b = 2 * g + i
                    last = pe.matmul(o[0:A, i * S:i * S + S], cw1[:, b, :], acc[:, b * S:b * S + S], start=True, stop=True)
                last.then_inc(m_h, 1)

            def act_h(act):
                o = bank[mb[("h", g)][0]]
                act.wait_ge(m_h, g + 1)
                if g == 0:
                    act.wait_ge(ld["lang"], 16 * 4 * B)
                else:
                    act.wait_ge(m_xa, g)
                for i in range(2):
                    b = 2 * g + i
                    act.activation(hTs[0:A, i * S:i * S + S], o[0:A, i * S:i * S + S], ACT.Relu,
                                   bias=cb1[:, b:b + 1]).then_inc(m_hs, 1)

            def pe_xa(pe):
                o = misc_bank(pe, ("xa", g))
                pe.wait_ge(m_one, 1)
                pe.wait_ge(m_hs, 2 * g + 2)
                for i in range(4):
                    c = g * 512 + i * 128
                    pe.matmul(o[:, i * 128:i * 128 + 128], acc[:, c:c + 128], ident[:, :], start=True, stop=False)
                    last = pe.matmul(o[:, i * 128:i * 128 + 128], hTs[:, i * 128:i * 128 + 128],
                                     cw2[:, 2 * g + i // 2, :], start=False, stop=True)
                last.then_inc(m_xa, 1)

            def stats(src, k, done, ready):
                def each(dve):
                    ready(dve)
                    for i in range(4):
                        last = dve.bn_stats(st[:, i, :], src[:, i * 128:i * 128 + 128])
                    return last

                def join(dve):
                    for i in range(4):
                        last = dve.bn_aggr(mv[:, k, i, :], st[:, i, :])
                    last.then_inc(done, 1)
                return [each, join]

            def ready1(dve):
                dve.wait_ge(m_xa, g + 1)
                if g:
                    dve.wait_ge(m_mv2, g)
                    dve.wait_ge(m_n1, g)

            def rstd(k, ready, done):
                def fn(pool):
                    pool.wait_ge(ready, g + 1)
                    link(pool, "pool", pool.tensor_scalar(rs[:, k, :], mv[:, k, :, 1], EPS, None, ALU.add))
                    pool.tensor_tensor(rs[:, k, :], rs[:, k, :], mhalf[:, :], ALU.pow).then_inc(done, 1)
                return fn

            def dve_n1(dve):
                o = bank[mb[("xa", g)][0]]
                dve.wait_ge(m_rs, g + 1)
                if g:
                    dve.wait_ge(m_x2, g)
                for i in range(4):
                    last = dve.tensor_scalar(n1[:, i * 128:i * 128 + 128], o[:, i * 128:i * 128 + 128],
                                             mv[:, 0, i, 0:1], rs[:, 0, i:i + 1], ALU.subtract, ALU.mult)
                last.then_inc(m_n1, 1)

            def scale(eng):
                eng.wait_ge(m_n1, g + 1)
                if g == 0:
                    eng.wait_ge(ld["lang"], 16 * 4 * B)
                else:
                    eng.wait_ge(m_x2T, g)
                    eng.wait_ge(m_n2, g)
                for i in range(2):
                    b = 2 * g + i
                    v3 = n1[:, i * S:i * S + S].rearrange("p (t d) -> p t d", t=2)
                    last = eng.tensor_tensor(v3, v3, gbc[:, b:b + 1, 0:D].to_broadcast([128, 2, D]), ALU.mult)
                return last

            def shift(eng):
                for i in range(2):
                    b = 2 * g + i
                    v3 = n1[:, i * S:i * S + S].rearrange("p (t d) -> p t d", t=2)
                    o3 = x2[:, i * S:i * S + S].rearrange("p (t d) -> p t d", t=2)
                    last = eng.tensor_tensor(o3, v3, gbc[:, b:b + 1, D:2 * D].to_broadcast([128, 2, D]), ALU.add)
                last.then_inc(m_x2, 1)

            def ready2(dve):
                dve.wait_ge(m_x2, g + 1)
                dve.wait_ge(m_mv, g + 1)
                if g:
                    dve.wait_ge(m_n2, g)

            n2 = n2A[:, 4 * (g % GA):4 * (g % GA) + 4, :].rearrange("p t d -> p (t d)")

            def dve_n2(dve):
                dve.wait_ge(m_rs2, g + 1)
                if g == GA:
                    dve.wait_ge(t_sc, 16 * 2 * TA)
                for i in range(4):
                    last = dve.tensor_scalar(n2[:, i * 128:i * 128 + 128], x2[:, i * 128:i * 128 + 128],
                                             mv[:, 1, i, 0:1], rs[:, 1, i:i + 1], ALU.subtract, ALU.mult)
                last.then_inc(m_n2, 1)

            def pe_x2T(pe):
                o = misc_bank(pe, ("x2T", g))
                pe.wait_ge(m_x2, g + 1)
                for i in range(4):
                    last = pe.transpose(o[:, i * 128:i * 128 + 128], x2[:, i * 128:i * 128 + 128], ident[:, :])
                last.then_inc(m_x2T, 1)

            def pe_nT(pe):
                o = misc_bank(pe, ("nT", g))
                pe.wait_ge(m_n2, g + 1)
                for i in range(4):
                    last = pe.transpose(o[:, i * 128:i * 128 + 128], n2[:, i * 128:i * 128 + 128], ident[:, :])
                last.then_inc(m_nT, 1)

            def act_xn(act):
                o = bank[mb[("nT", g)][0]]
                if g == 0:
                    act.wait_ge(ld["fgb"], 16)
                else:
                    act.wait_ge(m_lg, g)
                act.wait_ge(m_nT, g + 1)
                act.activation(xn32[:, :], o[:, :], ACT.Identity, bias=fgb[:, 1:2], scale=fgb[:, 0:1]).then_inc(m_xn, 1)

            def dve_split(dve):
                dve.wait_ge(m_xn, g + 1)
                link(dve, "dve", dve.tensor_scalar(xbh[:, :], xn32[:, :], XS, None, ALU.mult))
                dve.scalar_tensor_tensor(xbl[:, :], xn32[:, :], XS, xbh[:, :], ALU.mult, ALU.subtract).then_inc(m_sp, 1)

            def pe_lg(pe):
                o = misc_bank(pe, ("lg", g))
                if g == 0:
                    pe.wait_ge(ld["gw1"], 16)
                pe.wait_ge(m_xn, g + 1)
                for i in range(4):
                    last = pe.matmul(o[:, i * E:i * E + E], xn32[:, i * 128:i * 128 + 128], gw1[:, :], start=True, stop=True)
                last.then_inc(m_lg, 1)

            def dve_d(dve):
                o = bank[mb[("lg", g)][0]][:, 0:32].rearrange("p (t e) -> p t e", t=4)
                dve.wait_ge(m_lg, g + 1)
                link(dve, "dve", dve.tensor_reduce(c4[:, :, 0], o, AX.X, ALU.max))
                dve.tensor_tensor(lg[:, :, :], o, c4[:, :, 0:1].to_broadcast([128, 4, E]), ALU.subtract).then_inc(m_d, 1)

            def act_exp(act):
                act.wait_ge(m_d, g + 1)
                act.activation(ex[:, :, :], lg[:, :, :], ACT.Exp).then_inc(m_e, 1)

            def top():
                sl = slice(4 * g, 4 * g + 4)
                parts = []

                def part(fn):
                    parts.append(fn)

                @part
                def _(dve):
                    dve.wait_ge(m_e, g + 1)
                    if g == 0:
                        dve.wait_ge(ld["iota8"], 16)
                    else:
                        dve.wait_ge(m_cT, g)
                    return dve.tensor_reduce(c4[:, :, 1], ex[:, :, :], AX.X, ALU.add)

                @part
                def _(dve):
                    return dve.reciprocal(c4[:, :, 2], c4[:, :, 1])

                @part
                def _(dve):
                    return dve.tensor_tensor(pr[:, :, :], ex[:, :, :], c4[:, :, 2:3].to_broadcast([128, 4, E]), ALU.mult)

                @part
                def _(dve):
                    for i in range(4):
                        last = dve.max(mx8[:, i, :], pr[:, i, :])
                    return last

                @part
                def _(dve):
                    for i in range(4):
                        dve.max_index(ix8[:, i, :], mx8[:, i, :], pr[:, i, :])
                    return dve.tensor_tensor(c4[:, :, 3], mx8[:, :, 0], mx8[:, :, 1], ALU.add)

                @part
                def _(dve):
                    dve.tensor_copy(ixf[:, :, :], ix8[:, :, :])
                    return dve.reciprocal(c4[:, :, 4], c4[:, :, 3])

                @part
                def _(dve):
                    for k in range(2):
                        dve.tensor_tensor(oh[:, k, :, :], iota8[:, :, :], ixf[:, :, k:k + 1].to_broadcast([128, 4, E]),
                                          ALU.is_equal)
                    return dve.tensor_tensor(wk[:, :, :], mx8[:, :, 0:2], c4[:, :, 4:5].to_broadcast([128, 4, 2]), ALU.mult)

                if g < GA:
                    @part
                    def _(dve):
                        dve.tensor_copy(OH[:, :, sl, :].rearrange("p k t e -> p k (t e)"),
                                        oh[:, :, :, :].rearrange("p k t e -> p k (t e)"))
                        dve.tensor_copy(wA[:, sl, :], wk[:, :, :])
                        if g == 0:
                            dve.memset(cumb[:, 0, :], 0.0)
                        return dve.tensor_tensor(OB[:, sl, :], oh[:, 0, :, :], oh[:, 1, :, :], ALU.add)

                    for i in range(4 * g, 4 * g + 4):
                        @part
                        def _(dve, i=i):
                            return dve.tensor_tensor(cumb[:, i + 1, :], cumb[:, i, :], OB[:, i, :], ALU.add)

                @part
                def _(dve):
                    for k in range(2):
                        last = dve.tensor_tensor(oh[:, k, :, :], oh[:, k, :, :], wk[:, :, k:k + 1].to_broadcast([128, 4, E]),
                                                 ALU.mult)
                    return last

                @part
                def _(dve):
                    dve.tensor_tensor(cw[:, :, :], oh[:, 0, :, :], oh[:, 1, :, :], ALU.add).then_inc(m_cw, 1)
                return parts

            def pe_cT(pe):
                o = misc_bank(pe, ("cT", g))
                pe.wait_ge(m_cw, g + 1)
                pe.transpose(o[0:32, 0:128], cw[:, :, :].rearrange("p t e -> p (t e)"), ident[:, :]).then_inc(m_cT, 1)

            def act_cE(act):
                act.wait_ge(m_cT, g + 1)
                if g:
                    act.wait_ge(s_scr1[g - 1], 16)
                act.activation(cwT[:, :], bank[mb[("cT", g)][0]][0:32, 0:128], ACT.Copy).then_inc(m_cE, 1)

            def sp_gates(sp):
                sp.wait_ge(m_cE, g + 1)
                sp.dma_start(scr[1][4 * g:4 * g + 4, :, :].rearrange("t e p -> (t e) p"), cwT[:, :]).then_inc(s_scr1[g], 16)

            def sp_gtb(sp):
                sp.wait_ge(s_scr1[g], 16)
                sp.wait_ge(b_b2, b2_order.index((0, g)) + 1)
                sp.dma_start(gTb[:, g * 512:g * 512 + 512].rearrange("e (t p) -> e t p", p=128),
                             scr[1][4 * g:4 * g + 4, :, :].rearrange("t e p -> e t p")).then_inc(s_gtb[1 + g], 16)

            at("pe", mpos[("h", g)], pe_h)
            at("act", m + after("act_h", g), act_h)
            at("pe", mpos[("xa", g)], pe_xa)
            spread("dve", "dve", m + after("stats", g), 0.15, stats(bank[mb[("xa", g)][0]], 0, m_mv, ready1))
            at("pool", m + after("rstd", g), rstd(0, m_mv, m_rs))
            at("dve", m + after("n1", g), dve_n1)
            if g == GA - 1:
                spread("dve", "dve", m + after("n1", g) + AT["x2d"], 0.15, [scale, shift])
            else:
                spread("pool", "pool", m + AT["x2"], 0.01, [scale, shift])
            spread("dve", "dve", m + after("stats2", g), 0.15, stats(x2, 1, m_mv2, ready2))
            at("pool", m + after("rstd2", g), rstd(1, m_mv2, m_rs2))
            at("dve", m + after("n2", g), dve_n2)
            at("pe", mpos[("x2T", g)], pe_x2T)
            at("pe", mpos[("nT", g)], pe_nT)
            at("act", m + after("xn", g), act_xn)
            if g == GA:
                at("dve", m + 16.5, dve_split)
            at("pe", mpos[("lg", g)], pe_lg)
            at("dve", m + after("d", g), dve_d)
            at("act", m + after("exp", g), act_exp)
            spread("dve", "dve", m + after("top", g), 0.15, top())
            at("pe", mpos[("cT", g)], pe_cT)
            at("act", m + after("cT", g) + 0.1, act_cE)
            at("sp", m + after("cT", g) + 0.5, sp_gates)
            at("sp", m + after("cT", g) + 3.0, sp_gtb)

        for g in range(NG):
            mid(g)

        def pe_rank(g):
            def fn(pe):
                o = misc_bank(pe, ("rk", g))
                pe.wait_ge(m_cw, g + 1)
                pe.wait_ge(ld["sort"], 48)
                sl = slice(4 * g, 4 * g + 4)
                pe.matmul(o[:, 0:4 * E], triu[:, :], OB[:, sl, :].rearrange("p t e -> p (t e)"), start=True, stop=False)
                last = pe.matmul(o[:, 0:4 * E], onesb[:, :], cumb[:, sl, :].rearrange("p t e -> p (t e)"),
                                 start=False, stop=True)
                if g == GA - 1:
                    last = pe.matmul(o[:, 4 * E:5 * E], onesb[:, :], cumb[:, TA, :], start=True, stop=True)
                last.then_inc(t_rk, 1)
            return fn

        def rank(g):
            sl = slice(4 * g, 4 * g + 4)

            def add_region(dve):
                dve.wait_ge(t_rk, g + 1)
                if g == 0:
                    dve.wait_ge(ld["sort"], 48)
                o = bank[mb[("rk", g)][0]]
                return dve.tensor_tensor(rk4[:, :, :], o[:, 0:4 * E].rearrange("p (t e) -> p t e", e=E),
                                         region[:, :].unsqueeze(1).to_broadcast([128, 4, E]), ALU.add)

            def chosen(dve):
                for k in range(2):
                    last = dve.tensor_tensor(oh2[:, k, :, :], OH[:, k, sl, :], rk4[:, :, :], ALU.mult)
                return last

            def total(dve):
                return dve.tensor_reduce(pk[:, :, sl], oh2[:, :, :, :], AX.X, ALU.add)

            def whole(dve):
                dve.tensor_copy(idx[:, :, sl], pk[:, :, sl]).then_inc(t_ix, 1)
            return [add_region, chosen, total, whole]

        tile_parts = []

        def tiles(fn):
            tile_parts.append(fn)

        @tiles
        def _(dve):
            dve.wait_ge(t_zm, 1)
            dve.wait_ge(t_rk, GA)
            return dve.tensor_scalar(ci[:, :], bank[mb[("rk", GA - 1)][0]][:, 4 * E:5 * E], float(TS - 1), None, ALU.add)

        @tiles
        def _(dve):
            return dve.tensor_scalar(ci[:, :], ci[:, :], -TS, None, ALU.bitwise_and)

        @tiles
        def _(dve):
            return dve.tensor_copy(e8[:, 0, :], ci[:, :])

        @tiles
        def _(dve):
            dve.tensor_scalar(e8[:, 2, :], e8[:, 0, :], -1.0, float(CAP), ALU.mult, ALU.add)
            return dve.tensor_tensor_scan(e8[:, 1, :], e8[:, 0, :], zer[:, 0:E], 0.0, ALU.add, ALU.add)

        @tiles
        def _(dve):
            return dve.tensor_tensor(cmp_[:, :, :], e8[:, 1:2, :].to_broadcast([128, NTL, E]),
                                     it256[:, :].unsqueeze(2).to_broadcast([128, NTL, E]), ALU.is_le)

        @tiles
        def _(dve):
            dve.tensor_reduce(tef[:, 0, :], cmp_[:, :, :], AX.X, ALU.add)
            return dve.tensor_tensor(cmp2[:, :, :], cmp_[:, :, :], e8[:, 2:3, :].to_broadcast([128, NTL, E]), ALU.mult)

        @tiles
        def _(dve):
            return dve.tensor_reduce(tef[:, 1, :], cmp2[:, :, :], AX.X, ALU.add)

        @tiles
        def _(dve):
            dve.tensor_scalar(tei[:, 0, :], tef[:, 0, :], float(E - 1), 2048.0, ALU.min, ALU.mult)
            dve.tensor_scalar(tei[:, 1, :], tef[:, 0, :], float(E - 1), 4.0, ALU.min, ALU.mult)
            return dve.tensor_tensor(tef[:, 1, :], tef[:, 1, :], it256[:, :], ALU.add)

        @tiles
        def _(dve):
            dve.tensor_scalar(tei[:, 2, :], tef[:, 1, :], float(E * CAP), None, ALU.min).then_inc(t_te, 1)

        place_parts = []

        def places(fn):
            place_parts.append(fn)

        @places
        def _(dve):
            dve.wait_ge(t_te, 1)
            return dve.tensor_tensor(e8[:, 3, :], e8[:, 1, :], e8[:, 0, :], ALU.subtract)

        @places
        def _(dve):
            return dve.tensor_tensor(e8[:, 3, :], e8[:, 3, :], region[:, :], ALU.subtract)

        @places
        def _(dve):
            for k in range(2):
                last = dve.tensor_tensor(OH[:, k, :, :], OH[:, k, :, :], e8[:, 3:4, :].to_broadcast([128, TA, E]), ALU.mult)
            return last

        @places
        def _(dve):
            return dve.tensor_reduce(pk2[:, :, :], OH[:, :, :, :], AX.X, ALU.add)

        @places
        def _(dve):
            return dve.tensor_tensor(pk2[:, :, :], pk2[:, :, :], pk[:, :, :], ALU.add)

        @places
        def _(dve):
            dve.tensor_copy(idx2[:, :, :], pk2[:, :, :]).then_inc(t_pl, 1)

        def scatter(g, i, k):
            def fn(pool):
                if i == 4 * g and k == 0:
                    pool.wait_ge(t_ix, g + 1)
                    pool.wait_ge(m_n2, g + 1)
                    if g == 0:
                        pool.wait_ge(t_z, 16 * NZ)
                pool.indirect_dma_start(scx, bass.IndirectOffsetOnAxis(idx[:, k, i:i + 1], 0), n2A[:, i, :], None)\
                    .then_inc(t_sc, 16)
            return fn

        for g in range(GA):
            at("pe", mpos[("rk", g)], pe_rank(g))
            spread("dve", "dve", RK[g] + AT["rankd"], 0.15, rank(g))
            for n in range(8):
                at("pool", RK[g] + after("scatter", g) + (0.9 * n if g < GA - 1 else 0.01 * n), scatter(g, 4 * g + n // 2, n % 2))
        spread("dve", "dve", RK[GA - 1] + 1.75, 0.15, tile_parts)
        spread("dve", "dve", US + 12.3, 0.4, place_parts)

        def dve_fgs(dve):
            dve.wait_ge(ld["fgb"], 16)
            dve.tensor_scalar(fgs[:, :], fgb[:, :], XS, None, ALU.mult).then_inc(t_fg, 1)

        at("dve", 60.2, dve_fgs)

        def tile(i):
            p = tpos(i)

            def sp_in(sp):
                if i == 0:
                    sp.wait_ge(t_sc, 16 * 2 * TA)
                    sp.wait_ge(t_te, 1)
                    sp.wait_ge(s_w, NWP)
                    sp.wait_ge(*weights_split(NL - 1))
                    sp.wait_ge(s_w16, E)
                if i >= NX:
                    sp.wait_ge(t_tr, i - NX + 1)
                r = sp.value_load(tei[0:1, 2, i:i + 1], min_val=0, max_val=E * CAP)
                sp.dma_start(xr[:, i % NX, :, :], scx[bass.ds(r, TS), :].rearrange("(z p) d -> p z d", p=128))\
                    .then_inc(t_xr[i % NX], 16)

            def pe_t(pe):
                o = misc_bank(pe, ("t", i))
                pe.wait_ge(t_xr[i % NX], 16 * (i // NX + 1))
                for z in range(2):
                    last = pe.transpose(o[:, z * 128:z * 128 + 128], xr[:, i % NX, z, :], ident[:, :])
                last.then_inc(t_tr, 1)

            def act_x(act):
                if i == 0:
                    act.wait_ge(t_fg, 1)
                if i >= 2:
                    act.wait_ge(t_xl, i - 1)
                act.wait_ge(t_tr, i + 1)
                act.activation(xt32[:, i % 2, :], bank[mb[("t", i)][0]][:, 0:TS], ACT.Identity,
                               bias=fgs[:, 1:2], scale=fgs[:, 0:1]).then_inc(t_x32, 1)

            def dve_x(dve):
                dve.wait_ge(t_x32, i + 1)
                if i >= NX:
                    dve.wait_ge(s_m1, US + 2 * (i - NX) + 2)
                dve.tensor_copy(xth[:, i % NX, :], xt32[:, i % 2, :]).then_inc(t_xh, 1)

            def pool_x(pool):
                pool.wait_ge(t_xh, i + 1)
                pool.tensor_tensor(xtl[:, i % NX, :], xt32[:, i % 2, :], xth[:, i % NX, :], ALU.subtract).then_inc(t_xl, 1)

            def dve_y(dve):
                if i >= 2:
                    dve.wait_ge(t_ys[i % 2], 16 * (i // 2))
                dve.wait_ge(s_m2, US + 2 * i + 2)
                dve.tensor_scalar(yo[:, i % 2, :], bank[4 + res_of[("tile", i)] % 2][:, 0:2 * D], 1.0 / (WS * HS), None,
                                  ALU.mult).then_inc(t_yo, 1)

            def sp_out(sp):
                sp.wait_ge(t_yo, i + 1)
                sp.dma_start(scy[i * TS:i * TS + TS, :].rearrange("(z p) d -> p z d", p=128),
                             yo[:, i % 2, :].rearrange("p (z d) -> p z d", z=2)).then_inc(t_ys[i % 2], 16)

            at("sp", p - 1 if i < NX else tpos(i - NX) + 0.5, sp_in)
            at("pe", mpos[("t", i)], pe_t)
            at("act", p + 0.1, act_x)
            at("dve", p + AT["tdve"], dve_x)
            at("pool", p + 0.3, pool_x)
            at("dve", US + 2 * i + 1 + LAG + AT["yo"], dve_y)
            at("sp", US + 2 * i + 1 + LAG + 1.7, sp_out)

        for i in range(NTL):
            tile(i)

        def gather(i, k):
            n = 2 * i + k

            def fn(pool):
                if n == 0:
                    for z in range(2):
                        pool.wait_ge(t_ys[z], 16 * ((NTL + 1 - z) // 2))
                    pool.wait_ge(t_pl, 1)
                    pool.wait_ge(s_m2, US)
                pool.indirect_dma_start(yg[:, n, :], None, scy, bass.IndirectOffsetOnAxis(idx2[:, k, i:i + 1], 0))\
                    .then_inc(t_yg[i], 16)
            return fn

        def weigh(i):
            def fn(dve):
                n = 2 * i
                if i >= 2:
                    dve.wait_ge(t_moe, i - 1)
                dve.wait_ge(t_yg[i], 32)
                dve.tensor_scalar(mo1[:, i % 2, :], yg[:, n, :], wA[:, i, 0:1], None, ALU.mult).then_inc(t_mo1, 1)
                dve.wait_ge(t_mo1, i + 1)
                n += 1
                dve.scalar_tensor_tensor(mo[:, i % 2, :], yg[:, n, :], wA[:, i, 1:2], mo1[:, i % 2, :],
                                         ALU.mult, ALU.add).then_inc(t_mo, 1)
            return fn

        def moe(i):
            g = i // 4

            def fn(pe):
                if i % 4 == 0:
                    o = misc_bank(pe, ("moe", g))
                    pe.wait_ge(s_gtb[1 + g], 16)
                    pe.wait_ge(ld["b2f1"], 16)
                else:
                    o = bank[mb[("moe", g)][0]]
                if i % 4 == 0:
                    pe.matmul(o[:, :], b2f[1][:, :], gTb[:, g * 512:g * 512 + 512], start=True, stop=False,
                              skip_group_check=True)
                o = o[:, (i % 4) * 128:(i % 4) * 128 + 128]
                pe.wait_ge(t_mo, i + 1)
                pe.matmul(o, mo[:, i % 2, :], ident[:, :], start=False, stop=(i % 4 == 3), skip_group_check=True).then_inc(t_moe, 1)
            return fn

        for i in range(TA):
            at("pool", MO + 1.6 * i, gather(i, 0))
            at("pool", MO + 1.6 * i + 0.8, gather(i, 1))
            at("dve", WP[i], weigh(i))
            at("pe", WP[i] + AT["moe"], moe(i))

        def pool_consts(pool):
            pool.memset(zer[:, :], 0.0).then_inc(t_zm, 1)
            pool.wait_ge(t_zm, 1)
            pool.memset(hTs[A:A + 1, :], 1.0).then_inc(m_one, 1)
            pool.wait_ge(m_one, 1)
            link(pool, "pool", pool.memset(mhalf[:, :], -0.5))

        at("pool", -99, pool_consts)

        def act_b1(act):
            act.wait_ge(ld["b1f1"], 16)

        at("act", 100, act_b1)

        def store(g):
            def fn(sp):
                sp.wait_ge(s_acc, done1[g])
                sp.dma_start(out[:, g * 512:g * 512 + 512], acc[:, g * 512:g * 512 + 512]).then_inc(s_out, 16)
            return fn

        for g in range(NG):
            at("sp", 1000 + g, store(g))

        def finish(sp):
            sp.wait_ge(s_out, 16 * NG)

        at("sp", 2000, finish)

        for q in Q.values():
            q.sort(key=lambda x: (x[0], x[1]))

        block = ctx.enter_context(nc.Block())

        @block.sync
        def _(eng):
            for _, _, fn in Q["sp"]:
                fn(eng)

        @block.tensor
        def _(eng):
            for _, _, fn in Q["pe"]:
                fn(eng)

        @block.scalar
        def _(eng):
            for _, _, fn in Q["act"]:
                fn(eng)

        @block.vector
        def _(eng):
            for _, _, fn in Q["dve"]:
                fn(eng)

        @block.gpsimd
        def _(eng):
            for _, _, fn in Q["pool"]:
                fn(eng)


def constants():
    def bf(v):
        return (np.ascontiguousarray(v, np.float32).view(np.uint32) >> 16).astype(np.uint16)

    l = np.arange(S)[:, None]
    j = np.arange(S)[None, :]
    allowed = np.stack([l <= j, l >= j, l != j])
    mask = np.where(allowed, 0.0, BIG).astype(np.float32)
    cnt = allowed.sum(axis=1).astype(np.float32)
    maskt = np.zeros((3, 128, 514), np.float32)
    for c in range(2):
        maskt[:, :, c * S:c * S + S] = mask[:, c * 128:c * 128 + 128, :]
        maskt[:, :, 2 * S + c] = cnt[:, c * 128:c * 128 + 128]
    sel = np.zeros((B, B, 128), np.float32)
    for b in range(B):
        sel[b, b, :] = 1.0
    bits = np.zeros((16, 3), np.int64)
    bits[0] = [1 << 30, 0, 0]
    for r in range(1, 16):
        bits[r] = [k << (30 - 2 * r) for k in (1, 2, 3)]
    return {
        "maskt": bf(maskt),
        "sel": sel.reshape(B, B * 128),
        "ident": np.eye(128, dtype=np.float32),
        "identb": bf(np.eye(128)),
        "bitc": np.broadcast_to(bits.reshape(1, 48).astype(np.int32), (128, 48)).copy(),
        "iota8": np.broadcast_to(np.arange(E, dtype=np.float32), (128, 4, E)).copy(),
        "triu": bf(np.triu(np.ones((128, 128)), 1)),
        "region": np.broadcast_to(CAP * np.arange(E, dtype=np.float32), (128, E)).copy(),
        "it256": np.broadcast_to(TS * np.arange(NTL, dtype=np.float32), (128, NTL)).copy(),
    }


def kernel(**inputs):
    import concourse.bacc as bacc
    from concourse.bass_utils import run_bass_kernel_spmd

    i = {k: np.asarray(v) for k, v in inputs.items()}
    c = np.ascontiguousarray
    x = i["x"].reshape(N, D)
    a = {
        "xT": c(x.T),
        "xtm": c(x.reshape(NT, 128, D).transpose(1, 0, 2)),
        "itype": i["itok_B_0_2"],
        "ilang": i["itok_B_0_8"],
        "w1c": i["L0_cond_W1"],
        "b1c": i["L0_cond_b1"].reshape(A, 1),
        "vc": i["L0_cond_v"].reshape(A, 1),
        "gw0": c(i["L0_ffn_gate_weight"].T),
        "b1_0": c(i["L0_ffn_b1"].reshape(E, 4, 128).transpose(2, 0, 1).reshape(128, 4 * E)),
        "w_0": c(np.concatenate([i["L0_ffn_w1"].transpose(2, 0, 1),
                                 i["L0_ffn_w2"].transpose(2, 0, 1).reshape(4, 128, E, D).transpose(1, 2, 0, 3)
                                 .reshape(128, E, 4 * D)], axis=2)),
        "b2_0": i["L0_ffn_b2"],
        "cw1": i["L1_cond_W1"],
        "cb1": i["L1_cond_b1"],
        "cw2": c(np.concatenate([i["L1_cond_W2"], i["L1_cond_b2"][:, None, :]], axis=1)),
        "gbc": c(np.concatenate([i["L1_cond_gamma"], i["L1_cond_beta"]], axis=1)),
        "gw1": i["L1_ffn_gate_w"],
        "b1_1": c(i["L1_ffn_b1"].reshape(E, 4, 128).transpose(2, 0, 1).reshape(128, 4 * E)),
        "w_1": c(np.concatenate([i["L1_ffn_w1"].transpose(1, 0, 2),
                                 i["L1_ffn_w2"].reshape(E, 4, 128, D).transpose(2, 0, 1, 3)
                                 .reshape(128, E, 4 * D)], axis=2)),
        "b2_1": i["L1_ffn_b2"],
        "fgb": c(np.stack([i["L1_ffn_gamma"], i["L1_ffn_beta"]], axis=1)),
    }
    a.update(constants())
    nc = bacc.Bacc("TRN2", target_bir_lowering=False, num_devices=1)
    arrays, t = {}, {}
    for name, v in a.items():
        v = c(v)
        arrays["in_" + name] = v
        t[name] = nc.dram_tensor("in_" + name, v.shape, mybir.dt.from_np(v.dtype), kind="ExternalInput").ap()
    for name in ("maskt", "identb", "triu"):
        t[name] = t[name].bitcast(BF16)
    out = nc.dram_tensor("out_T", [D, N], F32, kind="ExternalOutput").ap()
    build_adaln_ffn(nc, t, out)
    r = run_bass_kernel_spmd(nc, [arrays], core_ids=[0])
    return c(np.asarray(r.results[0]["out_T"]).T).reshape(B, S, D)
```
